# Optimizing a Trainium2 kernel written in Bass

```python
import numpy as np
import jax
import jax.numpy as jnp

def _softmax(x, axis=-1):
    return jax.nn.softmax(x, axis=axis)

def _gelu(x):
    return jax.nn.gelu(x, approximate=True)

def _silu(x):
    return jax.nn.silu(x)

def _sigmoid(x):
    return jax.nn.sigmoid(x)

def _layernorm(x, axis=-1, eps=1e-05):
    m = jnp.mean(x, axis=axis, keepdims=True)
    v = jnp.var(x, axis=axis, keepdims=True)
    return (x - m) / jnp.sqrt(v + eps)

def _scatter_add(tgt, idx, src, axis=0):
    return tgt.at[idx].add(src)

def _segment_sum(src, seg, n):
    return jax.ops.segment_sum(src, seg, n)
kernel_name = 'mk_decoder_postln_d2_seqx_r8_9982dd'

def setup_inputs(seed: int=0):
    np.random.seed(seed)
    _w = jnp.asarray

    def _rec_inputs():
        import jax
        import jax.numpy as jnp
        _rk = jax.random.key(seed)
        x = -0.0002928 + 1 * jax.random.normal(jax.random.fold_in(_rk, 1), (64, 128, 128), jnp.float32)
        _lenS = 128 - jax.random.randint(jax.random.fold_in(_rk, 7), (64,), 0, max(1, 128 // 4) + 1, jnp.int32)
        _lenS2 = 77 - jax.random.randint(jax.random.fold_in(_rk, 8), (64,), 0, max(1, 77 // 4) + 1, jnp.int32)
        _ctx_1024P = jax.random.normal(jax.random.fold_in(_rk, 11), (64, 16, 128), jnp.float32)
        _ctx_1024c = jax.random.dirichlet(jax.random.fold_in(_rk, 511), 0.3 * jnp.ones((16,), jnp.float32), (64, 77))
        _ctx_1024t = jnp.einsum('bsk,bkd->bsd', _ctx_1024c, _ctx_1024P)
        _ctx_1024t = _ctx_1024t * jax.lax.rsqrt(jnp.mean(jnp.square(_ctx_1024t)) + 1e-12) * 0.953939
        ctx_1024 = 4.13588e-05 + 0.999923 * (_ctx_1024t + 0.3 * jax.random.normal(jax.random.fold_in(_rk, 611), (64, 77, 128), jnp.float32))
        fside_Bx16xSxS2_0 = -6.00028e-06 + 0.100001 * jax.random.normal(jax.random.fold_in(_rk, 12), (64, 16, 128, 77), jnp.float32)
        return (x, ctx_1024, fside_Bx16xSxS2_0)
    x, ctx_1024, fside_Bx16xSxS2_0 = _rec_inputs()

    def _L0_attn_setup():
        import jax, jax.numpy as jnp
        import numpy as np
        BATCH, SEQ, D_IN = (4, 512, 128)
        HID = 2 * D_IN

        def log_g(x):
            return jnp.where(x >= 0, jnp.log(jax.nn.relu(x) + 0.5), -jax.nn.softplus(-x))
        key = jax.random.key(seed)
        k_x, k_wf, k_wo = jax.random.split(key, 3)
        x = jax.random.normal(k_x, (BATCH, SEQ, D_IN), dtype=jnp.float32)
        W_fwd = jax.random.normal(k_wf, (3 * HID, D_IN), dtype=jnp.float32) * (1.0 / np.sqrt(D_IN))
        W_out = jax.random.normal(k_wo, (D_IN, HID), dtype=jnp.float32) * (1.0 / np.sqrt(HID))
        return {'x': x, 'W_fwd': W_fwd, 'W_out': W_out}
    _L0_attn_all = _L0_attn_setup()
    _L0_attn_in = {k: v for k, v in _L0_attn_all.items() if k in ('W_fwd', 'W_out')}
    del _L0_attn_all

    def _L0_xattn_setup():
        import jax, jax.numpy as jnp
        import numpy as np
        HIDDEN = 128
        NUM_HEADS = 16
        HEAD_DIM = HIDDEN // NUM_HEADS
        key = jax.random.key(seed)
        k1, k2, k3, k4, k5, k6 = jax.random.split(key, 6)
        B, SQ, SKV = (4, 128, 256)
        s = HIDDEN ** (-0.5)
        return {'xq': jax.random.normal(k1, (B, SQ, HIDDEN), jnp.float32), 'xkv': jax.random.normal(k2, (B, SKV, HIDDEN), jnp.float32), 'Wq': jax.random.normal(k3, (HIDDEN, HIDDEN), jnp.float32) * s, 'Wkv': jax.random.normal(k4, (2 * HIDDEN, HIDDEN), jnp.float32) * s, 'Wout': jax.random.normal(k5, (HIDDEN, HIDDEN), jnp.float32) * s, 'bout': jax.random.normal(k6, (HIDDEN,), jnp.float32) * 0.01}
    _L0_xattn_all = _L0_xattn_setup()
    _L0_xattn_in = {k: v for k, v in _L0_xattn_all.items() if k in ('Wq', 'Wkv', 'Wout', 'bout')}
    del _L0_xattn_all

    def _L0_ffn_setup():
        import jax, jax.numpy as jnp
        import numpy as np
        B, S, D, F, E, NS, K = (2, 128, 128, 512, 8, 8, 2)
        FS = F // NS
        key = jax.random.key(seed)
        ks = jax.random.split(key, 8)
        scale = 0.02
        return {'hidden_states': jax.random.normal(ks[0], (B, S, D), jnp.float32), 'gate_W': jax.random.normal(ks[1], (E, D), jnp.float32) * scale, 'w1_e': jax.random.normal(ks[2], (E, D, F), jnp.float32) * scale, 'w3_e': jax.random.normal(ks[3], (E, D, F), jnp.float32) * scale, 'w2_e': jax.random.normal(ks[4], (E, F, D), jnp.float32) * scale, 'w1_s': jax.random.normal(ks[5], (NS, D, FS), jnp.float32) * scale, 'w3_s': jax.random.normal(ks[6], (NS, D, FS), jnp.float32) * scale, 'w2_s': jax.random.normal(ks[7], (NS, FS, D), jnp.float32) * scale}
    _L0_ffn_all = _L0_ffn_setup()
    _L0_ffn_in = {k: v for k, v in _L0_ffn_all.items() if k in ('gate_W', 'w1_e', 'w3_e', 'w2_e', 'w1_s', 'w3_s', 'w2_s')}
    del _L0_ffn_all

    def _L1_attn_setup():
        import jax, jax.numpy as jnp
        import numpy as np
        B, S, H = (8, 256, 128)
        key = jax.random.key(seed)
        k1, k2, k3 = jax.random.split(key, 3)
        x = jax.random.normal(k1, (B, S, H), dtype=jnp.float32)
        W_qkv = jax.random.normal(k2, (3 * H, H), dtype=jnp.float32) / np.sqrt(H)
        W_out = jax.random.normal(k3, (H, H), dtype=jnp.float32) / np.sqrt(H)
        return {'x': x, 'W_qkv': W_qkv, 'W_out': W_out}
    _L1_attn_all = _L1_attn_setup()
    _L1_attn_in = {k: v for k, v in _L1_attn_all.items() if k in ('W_qkv', 'W_out')}
    del _L1_attn_all

    def _L1_xattn_setup():
        import jax, jax.numpy as jnp
        import numpy as np
        import math
        H = 16
        D = 128
        FF = 512
        DK = D // H
        EPS = 1e-05

        def layer_norm(x, g, b):
            mu = jnp.mean(x, axis=-1, keepdims=True)
            var = jnp.var(x, axis=-1, keepdims=True)
            return (x - mu) * jax.lax.rsqrt(var + EPS) * g + b
        key = jax.random.key(seed)
        ks = jax.random.split(key, 16)
        B, S = (2, 256)
        s = 1.0 / math.sqrt(D)
        return {'x_q': jax.random.normal(ks[0], (B, S, D), jnp.float32), 'x_kv': jax.random.normal(ks[1], (B, S, D), jnp.float32), 'bias': jax.random.normal(ks[2], (B, H, S, S), jnp.float32) * 0.1, 'Wq': jax.random.normal(ks[3], (D, D), jnp.float32) * s, 'Wk': jax.random.normal(ks[4], (D, D), jnp.float32) * s, 'Wv': jax.random.normal(ks[5], (D, D), jnp.float32) * s, 'Wo': jax.random.normal(ks[6], (D, D), jnp.float32) * s, 'W1': jax.random.normal(ks[7], (FF, D), jnp.float32) * s, 'b1': jnp.zeros((FF,), jnp.float32), 'W2': jax.random.normal(ks[8], (D, FF), jnp.float32) * (1.0 / math.sqrt(FF)), 'b2': jnp.zeros((D,), jnp.float32), 'g1': jnp.ones((D,), jnp.float32), 'be1': jnp.zeros((D,), jnp.float32), 'g2': jnp.ones((D,), jnp.float32), 'be2': jnp.zeros((D,), jnp.float32)}
    _L1_xattn_all = _L1_xattn_setup()
    _L1_xattn_in = {k: v for k, v in _L1_xattn_all.items() if k in ('Wq', 'Wk', 'Wv', 'Wo', 'W1', 'b1', 'W2', 'b2', 'g1', 'be1', 'g2', 'be2')}
    del _L1_xattn_all

    def _L1_ffn_setup():
        import jax, jax.numpy as jnp
        import numpy as np
        DIM = 128
        DEPTH = 2
        HEADS = 8
        DIM_HEAD = 64
        WINDOW = 64
        INNER = HEADS * DIM_HEAD
        HID = int(DIM * 4 * 2 / 3)
        B, N = (2, 1024)
        QK_SCALE = 8.0

        def shift_token(t):
            t1, t2 = jnp.split(t, 2, axis=-1)
            t2 = jnp.pad(t2, ((0, 0), (1, 0), (0, 0)))[:, :-1]
            return jnp.concatenate([t1, t2], axis=-1)

        def l2norm(t):
            return t / jnp.clip(jnp.linalg.norm(t, axis=-1, keepdims=True), 1e-12)

        def rotate_half(x):
            x1, x2 = jnp.split(x, 2, axis=-1)
            return jnp.concatenate([-x2, x1], axis=-1)

        def rotary_xpos(q, k):
            n = q.shape[-2]
            half_idx = jnp.arange(0, DIM_HEAD, 2, dtype=jnp.float32)
            inv_freq = 1.0 / 10000.0 ** (half_idx / DIM_HEAD)
            t = jnp.arange(n, dtype=jnp.float32)
            freqs = t[:, None] * inv_freq[None, :]
            freqs = jnp.concatenate([freqs, freqs], axis=-1)
            base = (half_idx + 0.4 * DIM_HEAD) / (1.4 * DIM_HEAD)
            power = (t - n // 2) / float(WINDOW // 2)
            scale = base[None, :] ** power[:, None]
            scale = jnp.concatenate([scale, scale], axis=-1)
            cos, sin = (jnp.cos(freqs), jnp.sin(freqs))
            q = q * cos * scale + rotate_half(q) * sin * scale
            k = k * cos / scale + rotate_half(k) * sin / scale
            return (q, k)

        def local_attention(q, k, v):
            b, h, n, d = q.shape
            w = n // WINDOW
            bq = q.reshape(b, h, w, WINDOW, d) * QK_SCALE
            bk = k.reshape(b, h, w, WINDOW, d)
            bv = v.reshape(b, h, w, WINDOW, d)

            def look_around(t):
                p = jnp.pad(t, ((0, 0), (0, 0), (1, 0), (0, 0), (0, 0)))
                return jnp.concatenate([p[:, :, :w], p[:, :, 1:]], axis=3)
            bk, bv = (look_around(bk), look_around(bv))
            bt = jnp.arange(n).reshape(w, WINDOW)
            btp = jnp.pad(bt, ((1, 0), (0, 0)), constant_values=-1)
            btk = jnp.concatenate([btp[:w], btp[1:]], axis=1)
            sim = jnp.einsum('bhwid,bhwjd->bhwij', bq, bk)
            i = bt[:, :, None]
            j = btk[:, None, :]
            mask = (i < j) | (i > j + WINDOW) | (j == -1)
            sim = jnp.where(mask, -jnp.finfo(sim.dtype).max, sim)
            attn = jax.nn.softmax(sim, axis=-1)
            out = jnp.einsum('bhwij,bhwjd->bhwid', attn, bv)
            return out.reshape(b, h, n, d)

        def _layer(x, wqkv, qs, ksc, wo, lg, lb, w1, b1, w2, b2):
            b, n, _ = x.shape
            h = shift_token(x)
            qkv = h @ wqkv
            q, k, v = jnp.split(qkv, 3, axis=-1)
            to_heads = lambda t: t.reshape(b, n, HEADS, DIM_HEAD).transpose(0, 2, 1, 3)
            q, k, v = (to_heads(q), to_heads(k), to_heads(v))
            q = l2norm(q) * qs
            k = l2norm(k) * ksc
            q, k = rotary_xpos(q, k)
            o = local_attention(q, k, v)
            o = o.transpose(0, 2, 1, 3).reshape(b, n, INNER)
            x = x + o @ wo
            h = shift_token(x)
            mu = h.mean(-1, keepdims=True)
            var = h.var(-1, keepdims=True)
            h = (h - mu) / jnp.sqrt(var + 1e-05) * lg + lb
            h = h @ w1 + b1
            a, g = jnp.split(h, 2, axis=-1)
            h = a * jax.nn.gelu(g, approximate=False)
            x = x + h @ w2 + b2
            return x
        key = jax.random.key(seed)
        ks = jax.random.split(key, 6)
        return {'x': jax.random.normal(ks[0], (B, N, DIM), jnp.float32), 'wqkv': jax.random.normal(ks[1], (DEPTH, DIM, 3 * INNER), jnp.float32) * 0.02, 'q_scale': jnp.ones((DEPTH, DIM_HEAD), jnp.float32), 'k_scale': jnp.ones((DEPTH, DIM_HEAD), jnp.float32), 'wo': jax.random.normal(ks[2], (DEPTH, INNER, DIM), jnp.float32) * 0.02, 'ln_g': jnp.ones((DEPTH, DIM), jnp.float32), 'ln_b': jnp.zeros((DEPTH, DIM), jnp.float32), 'w1': jax.random.normal(ks[3], (DEPTH, DIM, 2 * HID), jnp.float32) * 0.02, 'b1': jnp.zeros((DEPTH, 2 * HID), jnp.float32), 'w2': jax.random.normal(ks[4], (DEPTH, HID, DIM), jnp.float32) * 0.02, 'b2': jnp.zeros((DEPTH, DIM), jnp.float32)}
    _L1_ffn_all = _L1_ffn_setup()
    _L1_ffn_in = {k: v for k, v in _L1_ffn_all.items() if k in ('wqkv', 'q_scale', 'k_scale', 'wo', 'ln_g', 'ln_b', 'w1', 'b1', 'w2', 'b2')}
    del _L1_ffn_all
    return {'x': x, 'ctx_1024': ctx_1024, 'fside_Bx16xSxS2_0': fside_Bx16xSxS2_0, 'L0_attn_W_fwd': _L0_attn_in['W_fwd'], 'L0_attn_W_out': _L0_attn_in['W_out'], 'L0_xattn_Wq': _L0_xattn_in['Wq'], 'L0_xattn_Wkv': _L0_xattn_in['Wkv'], 'L0_xattn_Wout': _L0_xattn_in['Wout'], 'L0_xattn_bout': _L0_xattn_in['bout'], 'L0_ffn_gate_W': _L0_ffn_in['gate_W'], 'L0_ffn_w1_e': _L0_ffn_in['w1_e'], 'L0_ffn_w3_e': _L0_ffn_in['w3_e'], 'L0_ffn_w2_e': _L0_ffn_in['w2_e'], 'L0_ffn_w1_s': _L0_ffn_in['w1_s'], 'L0_ffn_w3_s': _L0_ffn_in['w3_s'], 'L0_ffn_w2_s': _L0_ffn_in['w2_s'], 'L1_attn_W_qkv': _L1_attn_in['W_qkv'], 'L1_attn_W_out': _L1_attn_in['W_out'], 'L1_xattn_Wq': _L1_xattn_in['Wq'], 'L1_xattn_Wk': _L1_xattn_in['Wk'], 'L1_xattn_Wv': _L1_xattn_in['Wv'], 'L1_xattn_Wo': _L1_xattn_in['Wo'], 'L1_xattn_W1': _L1_xattn_in['W1'], 'L1_xattn_b1': _L1_xattn_in['b1'], 'L1_xattn_W2': _L1_xattn_in['W2'], 'L1_xattn_b2': _L1_xattn_in['b2'], 'L1_xattn_g1': _L1_xattn_in['g1'], 'L1_xattn_be1': _L1_xattn_in['be1'], 'L1_xattn_g2': _L1_xattn_in['g2'], 'L1_xattn_be2': _L1_xattn_in['be2'], 'L1_ffn_wqkv': _L1_ffn_in['wqkv'], 'L1_ffn_q_scale': _L1_ffn_in['q_scale'], 'L1_ffn_k_scale': _L1_ffn_in['k_scale'], 'L1_ffn_wo': _L1_ffn_in['wo'], 'L1_ffn_ln_g': _L1_ffn_in['ln_g'], 'L1_ffn_ln_b': _L1_ffn_in['ln_b'], 'L1_ffn_w1': _L1_ffn_in['w1'], 'L1_ffn_b1': _L1_ffn_in['b1'], 'L1_ffn_w2': _L1_ffn_in['w2'], 'L1_ffn_b2': _L1_ffn_in['b2']}

def reference(x, ctx_1024, fside_Bx16xSxS2_0, L0_attn_W_fwd, L0_attn_W_out, L0_xattn_Wq, L0_xattn_Wkv, L0_xattn_Wout, L0_xattn_bout, L0_ffn_gate_W, L0_ffn_w1_e, L0_ffn_w3_e, L0_ffn_w2_e, L0_ffn_w1_s, L0_ffn_w3_s, L0_ffn_w2_s, L1_attn_W_qkv, L1_attn_W_out, L1_xattn_Wq, L1_xattn_Wk, L1_xattn_Wv, L1_xattn_Wo, L1_xattn_W1, L1_xattn_b1, L1_xattn_W2, L1_xattn_b2, L1_xattn_g1, L1_xattn_be1, L1_xattn_g2, L1_xattn_be2, L1_ffn_wqkv, L1_ffn_q_scale, L1_ffn_k_scale, L1_ffn_wo, L1_ffn_ln_g, L1_ffn_ln_b, L1_ffn_w1, L1_ffn_b1, L1_ffn_w2, L1_ffn_b2):
    import jax
    import jax.numpy as jnp

    def _L0_attn_ref(x, W_fwd, W_out):
        import jax, jax.numpy as jnp
        import numpy as np
        BATCH, SEQ, D_IN = (4, 512, 128)
        HID = 2 * D_IN

        def log_g(x):
            return jnp.where(x >= 0, jnp.log(jax.nn.relu(x) + 0.5), -jax.nn.softplus(-x))
        gates = jnp.einsum('bsd,hd->bsh', x, W_fwd)
        f_gate, i_gate, hidden = jnp.split(gates, 3, axis=-1)
        diff = jax.nn.softplus(-f_gate) - jax.nn.softplus(-i_gate)
        log_f = -jax.nn.softplus(diff)
        log_i = -jax.nn.softplus(-diff)
        log_values = log_i + log_g(hidden)
        a_star = jnp.cumsum(log_f, axis=1)
        log_h = a_star + jax.lax.cumlogsumexp(log_values - a_star, axis=1)
        h = jnp.exp(log_h)
        return jnp.einsum('bsh,dh->bsd', h, W_out)

    def _L0_xattn_ref(xq, xkv, Wq, Wkv, Wout, bout):
        import jax, jax.numpy as jnp
        import numpy as np
        HIDDEN = 128
        NUM_HEADS = 16
        HEAD_DIM = HIDDEN // NUM_HEADS
        B, SQ, H = xq.shape
        SKV = xkv.shape[1]
        scale = HEAD_DIM ** (-0.5)
        q = (xq @ Wq.T).reshape(B, SQ, NUM_HEADS, HEAD_DIM)
        kv = (xkv @ Wkv.T).reshape(B, SKV, 2, NUM_HEADS, HEAD_DIM)
        k, v = (kv[:, :, 0], kv[:, :, 1])
        att = jax.nn.softmax(jnp.einsum('bxhd,byhd->bhxy', q, k) * scale, axis=-1)
        x = jnp.einsum('bhxy,byhd->bxhd', att, v).reshape(B, SQ, H)
        return x @ Wout.T + bout

    def _L0_ffn_ref(hidden_states, gate_W, w1_e, w3_e, w2_e, w1_s, w3_s, w2_s):
        import jax, jax.numpy as jnp
        import numpy as np
        B, S, D, F, E, NS, K = (2, 128, 128, 512, 8, 8, 2)
        FS = F // NS
        b, s, d = hidden_states.shape
        e = gate_W.shape[0]
        flat = hidden_states.reshape(-1, d)
        T = flat.shape[0]
        logits = (flat @ gate_W.T).astype(jnp.float32)
        probs = jax.nn.softmax(logits, axis=-1)
        top_v, top_i = jax.lax.top_k(probs, K)
        gates = jnp.zeros((T, e), probs.dtype).at[jnp.arange(T)[:, None], top_i].set(top_v)
        g = jax.nn.silu(jnp.einsum('td,edf->etf', flat, w1_e))
        u = jnp.einsum('td,edf->etf', flat, w3_e)
        out_e = jnp.einsum('etf,efd->etd', g * u, w2_e)
        routed = jnp.einsum('te,etd->td', gates, out_e).reshape(b, s, d)
        gs = jax.nn.silu(jnp.einsum('bsd,ndf->nbsf', hidden_states, w1_s))
        us = jnp.einsum('bsd,ndf->nbsf', hidden_states, w3_s)
        shared = jnp.einsum('nbsf,nfd->bsd', gs * us, w2_s) / w1_s.shape[0]
        alpha = 0.5
        return alpha * shared + (1.0 - alpha) * routed

    def _L1_attn_ref(x, W_qkv, W_out):
        import jax, jax.numpy as jnp
        import numpy as np
        B, S, H = (8, 256, 128)
        h = x.shape[-1]
        scale = 1.0 / np.sqrt(h).astype(np.float32)
        y = jnp.einsum('bsh,oh->bso', x, W_qkv).reshape(*x.shape, 3)
        q, k, v = (y[..., 0], y[..., 1], y[..., 2])
        scores = jnp.einsum('bqh,bkh->bqk', q, k) * scale
        attn = jax.nn.softmax(scores, axis=-1)
        ctx = jnp.einsum('bqk,bkh->bqh', attn, v)
        out = jnp.einsum('bsh,oh->bso', ctx, W_out)
        return out

    def _L1_xattn_ref(x_q, x_kv, bias, Wq, Wk, Wv, Wo, W1, b1, W2, b2, g1, be1, g2, be2):
        import jax, jax.numpy as jnp
        import numpy as np
        import math
        H = 16
        D = 128
        FF = 512
        DK = D // H
        EPS = 1e-05

        def layer_norm(x, g, b):
            mu = jnp.mean(x, axis=-1, keepdims=True)
            var = jnp.var(x, axis=-1, keepdims=True)
            return (x - mu) * jax.lax.rsqrt(var + EPS) * g + b
        B, S, _ = x_q.shape

        def split(x):
            return x.reshape(B, -1, H, DK).transpose(0, 2, 1, 3)
        q = split(x_q @ Wq.T)
        k = split(x_kv @ Wk.T)
        v = split(x_kv @ Wv.T)
        scores = jnp.einsum('bhqd,bhkd->bhqk', q, k) / math.sqrt(DK) + bias
        p = jax.nn.softmax(scores, axis=-1)
        o = jnp.einsum('bhqk,bhkd->bhqd', p, v)
        o = o.transpose(0, 2, 1, 3).reshape(B, S, D)
        x = x_q + o @ Wo.T
        h = jax.nn.gelu(layer_norm(x, g1, be1) @ W1.T + b1, approximate=False)
        x = x + h @ W2.T + b2
        return layer_norm(x, g2, be2)

    def _L1_ffn_ref(x, wqkv, q_scale, k_scale, wo, ln_g, ln_b, w1, b1, w2, b2):
        import jax, jax.numpy as jnp
        import numpy as np
        DIM = 128
        DEPTH = 2
        HEADS = 8
        DIM_HEAD = 64
        WINDOW = 64
        INNER = HEADS * DIM_HEAD
        HID = int(DIM * 4 * 2 / 3)
        B, N = (2, 1024)
        QK_SCALE = 8.0

        def shift_token(t):
            t1, t2 = jnp.split(t, 2, axis=-1)
            t2 = jnp.pad(t2, ((0, 0), (1, 0), (0, 0)))[:, :-1]
            return jnp.concatenate([t1, t2], axis=-1)

        def l2norm(t):
            return t / jnp.clip(jnp.linalg.norm(t, axis=-1, keepdims=True), 1e-12)

        def rotate_half(x):
            x1, x2 = jnp.split(x, 2, axis=-1)
            return jnp.concatenate([-x2, x1], axis=-1)

        def rotary_xpos(q, k):
            n = q.shape[-2]
            half_idx = jnp.arange(0, DIM_HEAD, 2, dtype=jnp.float32)
            inv_freq = 1.0 / 10000.0 ** (half_idx / DIM_HEAD)
            t = jnp.arange(n, dtype=jnp.float32)
            freqs = t[:, None] * inv_freq[None, :]
            freqs = jnp.concatenate([freqs, freqs], axis=-1)
            base = (half_idx + 0.4 * DIM_HEAD) / (1.4 * DIM_HEAD)
            power = (t - n // 2) / float(WINDOW // 2)
            scale = base[None, :] ** power[:, None]
            scale = jnp.concatenate([scale, scale], axis=-1)
            cos, sin = (jnp.cos(freqs), jnp.sin(freqs))
            q = q * cos * scale + rotate_half(q) * sin * scale
            k = k * cos / scale + rotate_half(k) * sin / scale
            return (q, k)

        def local_attention(q, k, v):
            b, h, n, d = q.shape
            w = n // WINDOW
            bq = q.reshape(b, h, w, WINDOW, d) * QK_SCALE
            bk = k.reshape(b, h, w, WINDOW, d)
            bv = v.reshape(b, h, w, WINDOW, d)

            def look_around(t):
                p = jnp.pad(t, ((0, 0), (0, 0), (1, 0), (0, 0), (0, 0)))
                return jnp.concatenate([p[:, :, :w], p[:, :, 1:]], axis=3)
            bk, bv = (look_around(bk), look_around(bv))
            bt = jnp.arange(n).reshape(w, WINDOW)
            btp = jnp.pad(bt, ((1, 0), (0, 0)), constant_values=-1)
            btk = jnp.concatenate([btp[:w], btp[1:]], axis=1)
            sim = jnp.einsum('bhwid,bhwjd->bhwij', bq, bk)
            i = bt[:, :, None]
            j = btk[:, None, :]
            mask = (i < j) | (i > j + WINDOW) | (j == -1)
            sim = jnp.where(mask, -jnp.finfo(sim.dtype).max, sim)
            attn = jax.nn.softmax(sim, axis=-1)
            out = jnp.einsum('bhwij,bhwjd->bhwid', attn, bv)
            return out.reshape(b, h, n, d)

        def _layer(x, wqkv, qs, ksc, wo, lg, lb, w1, b1, w2, b2):
            b, n, _ = x.shape
            h = shift_token(x)
            qkv = h @ wqkv
            q, k, v = jnp.split(qkv, 3, axis=-1)
            to_heads = lambda t: t.reshape(b, n, HEADS, DIM_HEAD).transpose(0, 2, 1, 3)
            q, k, v = (to_heads(q), to_heads(k), to_heads(v))
            q = l2norm(q) * qs
            k = l2norm(k) * ksc
            q, k = rotary_xpos(q, k)
            o = local_attention(q, k, v)
            o = o.transpose(0, 2, 1, 3).reshape(b, n, INNER)
            x = x + o @ wo
            h = shift_token(x)
            mu = h.mean(-1, keepdims=True)
            var = h.var(-1, keepdims=True)
            h = (h - mu) / jnp.sqrt(var + 1e-05) * lg + lb
            h = h @ w1 + b1
            a, g = jnp.split(h, 2, axis=-1)
            h = a * jax.nn.gelu(g, approximate=False)
            x = x + h @ w2 + b2
            return x
        for l in range(DEPTH):
            x = _layer(x, wqkv[l], q_scale[l], k_scale[l], wo[l], ln_g[l], ln_b[l], w1[l], b1[l], w2[l], b2[l])
        return x
    x = _layernorm(x + _L0_attn_ref(x, L0_attn_W_fwd, L0_attn_W_out), axis=-1)
    x = _layernorm(x + _L0_xattn_ref(x, ctx_1024, L0_xattn_Wq, L0_xattn_Wkv, L0_xattn_Wout, L0_xattn_bout), axis=-1)
    x = _layernorm(x + _L0_ffn_ref(x, L0_ffn_gate_W, L0_ffn_w1_e, L0_ffn_w3_e, L0_ffn_w2_e, L0_ffn_w1_s, L0_ffn_w3_s, L0_ffn_w2_s), axis=-1)
    x = _layernorm(x + _L1_attn_ref(x, L1_attn_W_qkv, L1_attn_W_out), axis=-1)
    x = _layernorm(x + _L1_xattn_ref(x, ctx_1024, fside_Bx16xSxS2_0, L1_xattn_Wq, L1_xattn_Wk, L1_xattn_Wv, L1_xattn_Wo, L1_xattn_W1, L1_xattn_b1, L1_xattn_W2, L1_xattn_b2, L1_xattn_g1, L1_xattn_be1, L1_xattn_g2, L1_xattn_be2), axis=-1)
    x = _layernorm(x + _L1_ffn_ref(x, L1_ffn_wqkv, L1_ffn_q_scale, L1_ffn_k_scale, L1_ffn_wo, L1_ffn_ln_g, L1_ffn_ln_b, L1_ffn_w1, L1_ffn_b1, L1_ffn_w2, L1_ffn_b2), axis=-1)
    return x

_drawn_inputs = setup_inputs


def setup_inputs(seed=0):
    import zlib

    import numpy as np

    out = dict(_drawn_inputs(seed))
    spreads = {'L1_xattn_b1': (0.0, 0.31),
     'L1_xattn_b2': (0.0, 0.1),
     'L1_xattn_g1': (1.0, 0.2),
     'L1_xattn_be1': (0.0, 0.271),
     'L1_xattn_g2': (1.0, 0.2),
     'L1_xattn_be2': (0.0, 0.1),
     'L1_ffn_q_scale': (1.0, 0.6),
     'L1_ffn_k_scale': (1.0, 0.6),
     'L1_ffn_ln_g': (1.0, 0.6),
     'L1_ffn_ln_b': (0.0, 0.8),
     'L1_ffn_b1': (0.0, 0.8),
     'L1_ffn_b2': (0.0, 0.606)}
    factors = {'fside_Bx16xSxS2_0': 8.0,
     'L0_xattn_bout': 5.28,
     'L0_ffn_gate_W': 8.0,
     'L0_ffn_w1_e': 8.0,
     'L0_ffn_w3_e': 8.0,
     'L0_ffn_w2_e': 8.0,
     'L0_ffn_w1_s': 8.0,
     'L0_ffn_w3_s': 8.0,
     'L0_ffn_w2_s': 8.0,
     'L1_ffn_w1': 6.677,
     'L1_ffn_w2': 6.501}
    for name, (base, spread) in spreads.items():
        noise = np.random.default_rng([zlib.crc32(name.encode()), seed]).standard_normal(out[name].shape)
        drawn = base * np.exp(spread * noise) if base else spread * noise
        out[name] = jnp.asarray(drawn.astype(out[name].dtype))
    for name, factor in factors.items():
        out[name] = (out[name] * factor).astype(out[name].dtype)
    return out
```

```python
import math
import numpy as np
from contextlib import ExitStack

import concourse.bass as bass
from concourse import mybir

B, S, D = 64, 128, 128
GB = 4
NG = B // GB
GT = GB * S
S2 = 77
HEADS16 = 16
EPS = 1e-5
LN_EXP = "natural_log_exp_and_others"

F32 = mybir.dt.float32
BF16 = mybir.dt.bfloat16
ALU = mybir.AluOpType
ACT = mybir.ActivationFunctionType
AX = mybir.AxisListType


def groups(eng, peeled=4):
    for g in range(peeled):
        yield g, g % 2
    with eng.Fori(peeled // 2, NG // 2) as pair:
        yield pair * 2, 0
        yield pair * 2 + 1, 1


def there(n):
    return not isinstance(n, int) or n >= 0


def has(g):
    return not isinstance(g, int) or g < NG


def steps(eng, peeled=4):
    yield from groups(eng, peeled)
    yield NG, 0
    yield NG + 1, 1


def had(g, depth):
    return not isinstance(g, int) or g >= depth


class Phase:

    def __init__(self, nc, name):
        self.nc, self.name, self.stack, self.sems = nc, name, ExitStack(), []

    def __enter__(self):
        self.stack.__enter__()
        self.stored = [self.sem(f"stored{u}") for u in range(2)]
        self.pool_loaded = [self.sem(f"pool_loaded{u}") for u in range(2)]
        return self

    def __exit__(self, *e):
        self.stack.__exit__(*e)
        self.nc.clear_and_free_semaphores(self.sems)
        self.nc.all_engine_barrier()

    def sb(self, name, shape, dt=F32):
        return self.stack.enter_context(self.nc.sbuf_tensor(f"{self.name}_{name}", shape, dt))

    def ps(self, name, shape):
        return self.stack.enter_context(self.nc.psum_tensor(f"{self.name}_{name}", shape, F32))

    def sem(self, name):
        self.sems.append(self.nc.alloc_semaphore(f"{self.name}_{name}"))
        return self.sems[-1]

    def block(self):
        return self.stack.enter_context(self.nc.Block())


class Norm:

    def __init__(self, ph, name, eps, count=GB):
        self.count, self.eps = count, eps
        self.stats = ph.sb(f"{name}_stats", [S, count, 6])
        self.mv = ph.sb(f"{name}_mv", [S, count, 2])
        self.rstd = ph.sb(f"{name}_rstd", [S, count])
        self.summed = ph.sem(f"{name}_summed")
        self.stats_done = ph.sem(f"{name}_stats_done")
        self.mv_done = ph.sem(f"{name}_mv_done")
        self.ln_done = ph.sem(f"{name}_ln_done")
        self.rstd_done = ph.sem(f"{name}_rstd_done")
        self.normed = ph.sem(f"{name}_normed")

    def dve_stats(self, nc, dve, g, x):
        n = self.count
        for b in range(n):
            nc.vector.bn_stats(self.stats[:, b, :], x[:, b, :]).then_inc(self.stats_done, 1)
        dve.wait_ge(self.stats_done, (g + 1) * n)
        dve.nop(nofuse=True)
        for b in range(n):
            nc.vector.bn_aggr(self.mv[:, b, :], self.stats[:, b, :]).then_inc(self.mv_done, 1)

    def act_rstd(self, nc, act, g):
        act.wait_ge(self.mv_done, (g + 1) * self.count)
        nc.scalar.activation(self.rstd[:, :], self.mv[:, :, 1], ACT.Ln, bias=self.eps).then_inc(self.ln_done, 1)
        act.wait_ge(self.ln_done, g + 1)
        nc.scalar.activation(self.rstd[:, :], self.rstd[:, :], ACT.Exp, scale=-0.5).then_inc(self.rstd_done, 1)

    def dve_scale(self, nc, dve, g, out, x):
        dve.wait_ge(self.rstd_done, g + 1)
        for b in range(self.count):
            nc.vector.tensor_scalar(out[:, b, :], x[:, b, :], self.mv[:, b, 0:1], self.rstd[:, b:b + 1],
                                    ALU.subtract, ALU.mult).then_inc(self.normed, 1)


def load_constants(ph, eng, pairs):
    for to, of in pairs:
        eng.dma_start(to, of).then_inc(ph.consts_in, 16)
    return 16 * len(pairs)


def phase_recurrence(nc, x_in, x_out, w_gates, w_out, ident_in, eps_in):
    HID = 256
    NC = HID // 128
    with Phase(nc, "rec") as ph:
        sb, ps, sem = ph.sb, ph.ps, ph.sem
        w1 = sb("w1", [D, 3 * HID])
        w2 = sb("w2", [128, NC, D])
        ident = sb("ident", [128, 128])
        eps = sb("eps", [128, 2])
        x = [sb(f"x{u}", [S, GB, D]) for u in range(2)]
        xr = [sb(f"xr{u}", [S, GB, D]) for u in range(2)]
        xT = [sb(f"xT{u}", [D, GT]) for u in range(2)]
        E = [sb(f"E{c}", [128, 3, GT]) for c in range(NC)]
        LI = [sb(f"LI{c}", [128, GT]) for c in range(NC)]
        LH = [sb(f"LH{c}", [128, GT]) for c in range(NC)]
        T = [sb(f"T{c}", [128, GT]) for c in range(NC)]
        Dd = [sb(f"D{c}", [128, GT]) for c in range(NC)]
        Fg = [sb(f"F{c}", [128, GT]) for c in range(NC)]
        G = [sb(f"G{c}", [128, GT]) for c in range(NC)]
        hs = [[sb(f"hs{u}{c}", [128, GT]) for c in range(NC)] for u in range(2)]
        R = sb("R", [S, GB, D])
        xo = [sb(f"xo{u}", [S, GB, D]) for u in range(2)]
        pT = ps("pT", [128, GT])
        pg = [[ps(f"pg{c}{j}", [128, GT]) for j in range(3)] for c in range(NC)]
        pO = ps("pO", [S, GB, D])
        ph.consts_in = sem("consts_in")
        x_in_sem = [sem(f"x_loaded{u}") for u in range(2)]
        r_loaded = [sem(f"r_loaded{u}") for u in range(2)]
        xT_ready, xT_copied, gate_ready, exp_done = sem("xT_ready"), sem("xT_copied"), sem("gate_ready"), sem("exp_done")
        clamped, lnI_done, lnH_done, t_done, lnT_done, sig_done = (
            sem("clamped"), sem("lnI_done"), sem("lnH_done"), sem("t_done"), sem("lnT_done"), sem("sig_done"))
        d_done, f_done, g_done, v_done, scanned, out_ready = (
            sem("d_done"), sem("f_done"), sem("g_done"), sem("v_done"), sem("scanned"), sem("out_ready"))
        stored = ph.stored
        norm = Norm(ph, "norm", eps[:, 0:1])
        block = ph.block()
        NCONST = 4

        @block.sync
        def _(sp):
            load_constants(ph, sp, [(w1[:, :], w_gates), (w2[:, :, :], w_out), (ident[:, :], ident_in), (eps[:, :], eps_in)])
            for g, u in groups(sp):
                if had(g, 2):
                    sp.wait_ge(xT_ready, g - 1)
                sp.dma_start(x[u][:, :, :], x_in[g, :, :, :]).then_inc(x_in_sem[u], 16)
                if had(g, 2):
                    sp.wait_ge(norm.summed, g - 1)
                sp.dma_start(xr[u][:, :, :], x_in[g, :, :, :]).then_inc(r_loaded[u], 16)

        @block.gpsimd
        def _(pool):
            for g, u in groups(pool):
                pool.wait_ge(norm.normed, g * GB + GB)
                pool.dma_start(x_out[g, :, :, :], xo[u][:, :, :]).then_inc(stored[u], 16)
            for u in range(2):
                pool.wait_ge(stored[u], 16 * (NG // 2))

        @block.tensor
        def _(pe):
            pe.wait_ge(ph.consts_in, 16 * NCONST)

            def gates(g, u):
                pe.wait_ge(x_in_sem[u], (g - u) * 8 + 16)
                if had(g, 1):
                    pe.wait_ge(xT_copied, g)
                for b in range(GB):
                    last = nc.tensor.transpose(pT[:, b * S:(b + 1) * S], x[u][:, b, :], ident[:, :])
                last.then_inc(xT_ready, 1)
                pe.wait_ge(xT_copied, g + 1)
                for c in range(NC):
                    for j in range(3):
                        if had(g, 1):
                            pe.wait_ge(exp_done, (g - 1) * (3 * NC) + 3 * c + j + 1)
                            if j == 2:
                                pe.wait_ge(g_done, (g - 1) * NC + c + 1)
                        nc.tensor.matmul(pg[c][j][:, :], w1[:, j * HID + c * 128:j * HID + (c + 1) * 128],
                                         xT[u][:, :], start=True, stop=True).then_inc(gate_ready, 1)

            def project(g, u):
                if had(g, 1):
                    pe.wait_ge(norm.summed, g)
                pe.wait_ge(scanned, (g + 1) * (NC * GB))
                for b in range(GB):
                    for c in range(NC):
                        last = nc.tensor.matmul(pO[:, b, :], hs[u][c][:, b * S:(b + 1) * S], w2[:, c, :],
                                                start=(c == 0), stop=(c == NC - 1))
                last.then_inc(out_ready, 1)

            for g, u in steps(pe):
                if has(g):
                    gates(g, u)
                if there(g - 1) and has(g - 1):
                    project(g - 1, 1 - u)

        @block.scalar
        def _(act):
            nc.scalar.preload_act_table_set(LN_EXP)
            act.wait_ge(ph.consts_in, 16 * NCONST)

            def copy_xT(g, u):
                act.wait_ge(xT_ready, g + 1)
                if had(g, 2):
                    act.wait_ge(gate_ready, (g - 1) * (3 * NC))
                nc.scalar.activation(xT[u][:, :], pT[:, :], ACT.Copy).then_inc(xT_copied, 1)

            def exponentials(g):
                for c in range(NC):
                    if had(g, 1):
                        act.wait_ge(t_done, (g - 1) * NC + c + 1)
                        act.wait_ge(lnH_done, (g - 1) * NC + c + 1)
                    for j in range(3):
                        act.wait_ge(gate_ready, g * (3 * NC) + 3 * c + j + 1)
                        nc.scalar.activation(E[c][:, j, :], pg[c][j][:, :], ACT.Exp, scale=-1.0).then_inc(exp_done, 1)

            def sigmoids(g):
                for c in range(NC):
                    act.wait_ge(clamped, g * NC + c + 1)
                    if had(g, 1):
                        act.wait_ge(d_done, (g - 1) * NC + c + 1)
                        act.wait_ge(g_done, (g - 1) * NC + c + 1)
                    nc.scalar.activation(LH[c][:, :], E[c][:, 2, :], ACT.Ln, bias=1.0).then_inc(lnH_done, 1)
                    nc.scalar.activation(LI[c][:, :], E[c][:, 1, :], ACT.Ln, bias=1.0).then_inc(lnI_done, 1)
                    act.wait_ge(lnH_done, g * NC + c + 1)
                    nc.scalar.activation(LH[c][:, :], LH[c][:, :], ACT.Exp, scale=-1.0).then_inc(sig_done, 1)

            def ln_total(g):
                for c in range(NC):
                    act.wait_ge(t_done, g * NC + c + 1)
                    nc.scalar.activation(T[c][:, :], T[c][:, :], ACT.Ln, bias=eps[:, 1:2]).then_inc(lnT_done, 1)

            def forget(g):
                for c in range(NC):
                    act.wait_ge(d_done, g * NC + c + 1)
                    if had(g, 1):
                        act.wait_ge(scanned, (g - 1) * (NC * GB) + GB * (c + 1))
                    nc.scalar.activation(Fg[c][:, :], Dd[c][:, :], ACT.Exp).then_inc(f_done, 1)

            for g, u in steps(act):
                if has(g):
                    copy_xT(g, u)
                if there(g - 1) and has(g - 1):
                    ln_total(g - 1)
                    forget(g - 1)
                if has(g):
                    exponentials(g)
                if has(g):
                    sigmoids(g)
                if there(g - 2):
                    norm.act_rstd(nc, act, g - 2)

        @block.vector
        def _(dve):
            def clamp_and_total(g):
                for c in range(NC):
                    dve.wait_ge(exp_done, g * (3 * NC) + 3 * (c + 1))
                    nc.vector.tensor_scalar(E[c][:, :, :], E[c][:, :, :], 2.0 ** 62, None, ALU.min).then_inc(clamped, 1)
                for c in range(NC):
                    dve.wait_ge(clamped, g * NC + c + 1)
                    if had(g, 1):
                        dve.wait_ge(d_done, (g - 1) * NC + c + 1)
                    nc.vector.tensor_tensor(T[c][:, :], E[c][:, 0, :], E[c][:, 1, :], ALU.add).then_inc(t_done, 1)

            def g_of_hidden(g):
                for c in range(NC):
                    dve.wait_ge(sig_done, g * NC + c + 1)
                    if had(g, 1):
                        dve.wait_ge(scanned, (g - 1) * (NC * GB) + GB * (c + 1))
                    nc.vector.scalar_tensor_tensor(out=G[c][:, :], in0=pg[c][2][:, :], scalar=0.5, in1=LH[c][:, :],
                                                   op0=ALU.add, op1=ALU.max).then_inc(g_done, 1)

            def log_forget(g):
                for c in range(NC):
                    dve.wait_ge(lnT_done, g * NC + c + 1)
                    dve.wait_ge(lnI_done, g * NC + c + 1)
                    if had(g, 1):
                        dve.wait_ge(f_done, (g - 1) * NC + c + 1)
                    nc.vector.tensor_tensor(Dd[c][:, :], LI[c][:, :], T[c][:, :], ALU.subtract).then_inc(d_done, 1)

            def scan(g, u):
                for c in range(NC):
                    dve.wait_ge(f_done, g * NC + c + 1)
                    dve.wait_ge(g_done, g * NC + c + 1)
                    nc.vector.scalar_tensor_tensor(out=G[c][:, :], in0=Fg[c][:, :], scalar=1.0, in1=G[c][:, :],
                                                   op0=ALU.subtract, op1=ALU.mult).then_inc(v_done, 1)
                for c in range(NC):
                    dve.wait_ge(v_done, g * NC + c + 1)
                    if had(g, 2):
                        dve.wait_ge(out_ready, g - 1)
                    for b in range(GB):
                        t = slice(b * S, (b + 1) * S)
                        nc.vector.tensor_tensor_scan(hs[u][c][:, t], Fg[c][:, t], G[c][:, t], 0.0,
                                                     ALU.mult, ALU.subtract).then_inc(scanned, 1)

            def residual(g, u):
                dve.wait_ge(out_ready, g + 1)
                if had(g, 1):
                    dve.wait_ge(norm.normed, g * GB)
                dve.wait_ge(r_loaded[u], (g - u) * 8 + 16)
                nc.vector.tensor_tensor(R[:, :, :], pO[:, :, :], xr[u][:, :, :], ALU.add).then_inc(norm.summed, 1)
                dve.wait_ge(norm.summed, g + 1)
                norm.dve_stats(nc, dve, g, R)

            def normalise(g, u):
                if had(g, 2):
                    dve.wait_ge(stored[u], (g - u) * 8)
                norm.dve_scale(nc, dve, g, xo[u], R)

            for g, u in steps(dve):
                if there(g - 1) and has(g - 1):
                    log_forget(g - 1)
                    scan(g - 1, 1 - u)
                if has(g):
                    clamp_and_total(g)
                if has(g):
                    g_of_hidden(g)
                if there(g - 2):
                    normalise(g - 2, u)
                if there(g - 1) and has(g - 1):
                    residual(g - 1, 1 - u)


QG = 4
QH = 4
DH = 8
K4 = GB * S2
SCALE8 = DH ** -0.5


def phase_cross(nc, name, x_in, x_out, ctx_in, w_q, w_k, w_v, w_out, ident_in, mask_in, consts_in, bout_in=None, bias_in=None):
    biased = bias_in is not None
    with Phase(nc, name) as ph:
        sb, ps, sem = ph.sb, ph.ps, ph.sem
        wq, wk, wv, wo = (sb(n, [D, D]) for n in ("wq", "wk", "wv", "wo"))
        ident = sb("ident", [128, 128])
        identb = sb("identb", [128, 128], BF16)
        mask = sb("mask", [128, HEADS16])
        consts = sb("consts", [128, 2])
        x = [sb(f"x{u}", [S, GB, D]) for u in range(2)]
        xr = [sb(f"xr{u}", [S, GB, D]) for u in range(2)]
        ctxT = [sb(f"ctxT{u}", [D, K4]) for u in range(2)]
        xT = sb("xT", [D, GT])
        qT = [sb(f"qT{u}", [D, GT]) for u in range(2)]
        kT = [sb(f"kT{u}", [D, K4]) for u in range(2)]
        Km = [sb(f"Km{u}", [D, HEADS16, K4]) for u in range(2)]
        V = [sb(f"V{u}", [S2, GB * HEADS16, DH + 1]) for u in range(2)]
        neg_max = [sb(f"neg_max{i}", [S, QH], BF16) for i in range(2)]
        PT = [sb(f"PT{i}", [S2, QH * S]) for i in range(2)]
        rec = sb("rec", [S, HEADS16])
        on = sb("on", [S, HEADS16, DH])
        oT = sb("oT", [D, S])
        R = [sb(f"R{u}", [S, GB, D]) for u in range(2)]
        if biased:
            bias = [sb(f"bias{i}", [S, HEADS16, S2]) for i in range(2)]
            biased_s = [sb(f"biased_s{i}", [S, QH, S2]) for i in range(2)]
        else:
            Qm = [sb(f"Qm{u}", [D, HEADS16, GT]) for u in range(2)]
            bout = sb("bout", [S, D])
            xo = [sb(f"xo{u}", [S, GB, D]) for u in range(2)]
        pS = [ps(f"pS{i}", [S, QH, S2]) for i in range(2)]
        pT = [ps(f"pT{i}", [S2, QH, S]) for i in range(2)]
        pO = ps("pO", [S, HEADS16, DH + 1])
        pPrep = ps("pPrep", [128, 512])
        pOT = ps("pOT", [D, S])
        pF = ps("pF", [S, D])

        ph.consts_in = sem("consts_in")
        loaded, r_loaded = [sem(f"loaded{u}") for u in range(2)], ph.pool_loaded
        bias_loaded = [sem(f"bias_loaded{i}") for i in range(2)]
        ident_done, ones_done, xr_done = sem("ident_done"), sem("ones_done"), sem("xr_done")
        prep_ready = sem("prep_ready")
        prep_copied = sem("prep_copied")
        qm_done, km_done = sem("qm_done"), sem("km_done")
        s_ready, added, max_done, st_ready, exp_done = (
            sem("s_ready"), sem("added"), sem("max_done"), sem("st_ready"), sem("exp_done"))
        pv_done, rec_done, on_done, ot_ready, ot_copied, f_ready = (
            sem("pv_done"), sem("rec_done"), sem("on_done"), sem("ot_ready"), sem("ot_copied"), sem("f_ready"))
        stored = ph.stored
        norm = Norm(ph, "norm", consts[:, 0:1])
        block = ph.block()
        const_pairs = [(wq[:, :], w_q), (wk[:, :], w_k), (wv[:, :], w_v), (wo[:, :], w_out),
                       (ident[:, :], ident_in), (mask[:, :], mask_in), (consts[:, :], consts_in)]
        if not biased:
            const_pairs.append((bout[:, :], bout_in.partition_broadcast(S)))
        all_consts = 16 * len(const_pairs)

        def there(n):
            return not isinstance(n, int) or n >= 0

        def has(g):
            return not isinstance(g, int) or g < NG

        def steps(eng):
            yield from groups(eng)
            yield NG, 0
            yield NG + 1, 1

        @block.sync
        def _(sp):
            load_constants(ph, sp, const_pairs)

            def load_bias(g):
                for b in range(GB):
                    n = g * GB + b
                    if there(n - 2):
                        sp.wait_ge(added, (n - 1) * QG)
                    sp.dma_start(bias[b % 2][:, :, :], bias_in[g, b, :, :, :]).then_inc(bias_loaded[b % 2], 16)

            for g, u in groups(sp):
                if had(g, 2):
                    sp.wait_ge(prep_ready, (g - 1) * 4)
                sp.dma_start(x[u][:, :, :], x_in[g, :, :, :]).then_inc(loaded[u], 16)
                sp.dma_start(ctxT[u][:, :], ctx_in[g, :, :]).then_inc(loaded[u], 16)
                if biased and there(g - 1):
                    load_bias(g - 1)
            if biased:
                load_bias(NG - 1)

        @block.gpsimd
        def _(pool):
            for u in range(2):
                nc.gpsimd.memset(V[u][:, :, DH:DH + 1], 1.0).then_inc(ones_done, 1)
            pool.wait_ge(ph.consts_in, all_consts)
            nc.gpsimd.tensor_copy(identb[:, :], ident[:, :]).then_inc(ident_done, 1)

            def store(g, u):
                if biased:
                    pool.wait_ge(norm.summed, g * GB + GB)
                    pool.dma_start(x_out[g, :, :, :], R[u][:, :, :]).then_inc(stored[u], 16)
                else:
                    pool.wait_ge(norm.normed, g * GB + GB)
                    pool.dma_start(x_out[g, :, :, :], xo[u][:, :, :]).then_inc(stored[u], 16)

            for g, u in steps(pool):
                if there(g - 2):
                    store(g - 2, u)
                if has(g):
                    pool.dma_start(xr[u][:, :, :], x_in[g, :, :, :]).then_inc(r_loaded[u], 16)
                if has(g) and not biased:
                    pool.wait_ge(r_loaded[u], (g - u) * 8 + 16)
                    for b in range(GB):
                        nc.gpsimd.tensor_tensor(xr[u][:, b, :], xr[u][:, b, :], bout[:, :], ALU.add).then_inc(xr_done, 1)
            for u in range(2):
                pool.wait_ge(stored[u], 16 * (NG // 2))

        @block.tensor
        def _(pe):
            pe.wait_ge(ph.consts_in, all_consts)
            pe.wait_ge(ident_done, 1)
            pe.wait_ge(ones_done, 2)

            def prepare(g, u, b):
                if b == 0:
                    pe.wait_ge(loaded[u], (g - u) * 16 + 32)
                if b or there(g - 1):
                    pe.wait_ge(prep_copied, g * 4 + b)
                if b == 0:
                    for i in range(GB):
                        last = nc.tensor.transpose(pPrep[:, i * S:(i + 1) * S], x[u][:, i, :], ident[:, :])
                elif b == 1:
                    last = nc.tensor.matmul(pPrep[:, :], wq[:, :], xT[:, :], start=True, stop=True)
                elif b == 2:
                    last = nc.tensor.matmul(pPrep[:, 0:K4], wk[:, :], ctxT[u][:, :], start=True, stop=True)
                else:
                    for i in range(GB):
                        last = nc.tensor.matmul(pPrep[0:S2, i * D:(i + 1) * D], ctxT[u][:, i * S2:(i + 1) * S2],
                                                wv[:, :], start=True, stop=True)
                last.then_inc(prep_ready, 1)

            def scores(G, u, b, q):
                n = (G * GB + b) * QG + q
                if b == 0 and q == 0:
                    pe.wait_ge(prep_copied, G * 4 + 4)
                if b == 0:
                    pe.wait_ge(km_done, G * HEADS16 + QH * (q + 1))
                    if not biased:
                        pe.wait_ge(qm_done, (G + 1) * HEADS16)
                if there(n - 2):
                    pe.wait_ge(added if biased else max_done, n - 1)
                heads = slice(QH * q, QH * q + QH)
                nc.tensor.matmul(pS[q % 2][:, :, :], qT[u][:, b * S:(b + 1) * S],
                                 Km[u][:, heads, b * S2:(b + 1) * S2], start=True, stop=True).then_inc(s_ready, 1)

            def scores_t(G, u, b, q):
                n = (G * GB + b) * QG + q
                if there(n - 2):
                    pe.wait_ge(exp_done, n - 1)
                out = pT[q % 2]
                heads = slice(QH * q, QH * q + QH)
                if biased:
                    pe.wait_ge(added, n + 1)
                    for h in range(QH):
                        nc.tensor.matmul(out[:, h, :], biased_s[q % 2][:, h, :], ident[:, :],
                                         start=(h == 0), stop=False, skip_group_check=True)
                else:
                    nc.tensor.matmul(out[:, :, :], kT[u][:, b * S2:(b + 1) * S2],
                                     Qm[u][:, heads, b * S:(b + 1) * S], start=True, stop=False, skip_group_check=True)
                pe.wait_ge(max_done, n + 1)
                for h in range(QH):
                    last = nc.tensor.matmul(out[:, h, :], neg_max[q % 2][:, h:h + 1].to_broadcast([S, S2]), identb[:, :],
                                            start=False, stop=(h == QH - 1), skip_group_check=True)
                last.then_inc(st_ready, 1)

            def values(G, u, b, q):
                n = (G * GB + b) * QG + q
                pe.wait_ge(exp_done, n + 1)
                if q == 0 and there(n - 1):
                    pe.wait_ge(on_done, G * GB + b)
                for h in range(QH):
                    last = nc.tensor.matmul(pO[:, QH * q + h, :], PT[q % 2][:, h * S:(h + 1) * S],
                                            V[u][:, b * HEADS16 + QH * q + h, :], start=True, stop=True)
                last.then_inc(pv_done, 1)

            def turn(n):
                pe.wait_ge(on_done, n + 1)
                if there(n - 1):
                    pe.wait_ge(ot_copied, n)
                nc.tensor.transpose(pOT[:, :], on[:, :, :].rearrange("p h d -> p (h d)"), ident[:, :]).then_inc(ot_ready, 1)

            def project(n):
                pe.wait_ge(ot_copied, n + 1)
                if there(n - 1):
                    pe.wait_ge(norm.summed, n)
                nc.tensor.matmul(pF[:, :], oT[:, :], wo[:, :], start=True, stop=True).then_inc(f_ready, 1)

            for g, u in steps(pe):
                G, w = g - 1, 1 - u
                for b in range(GB):
                    n = G * GB + b
                    if has(g):
                        prepare(g, u, b)
                        if isinstance(g, int) and g == 0 and b == GB - 1:
                            scores(0, 0, 0, 0)
                    if there(G) and has(G):
                        for q in range(QG):
                            if q < QG - 1:
                                scores(G, w, b, q + 1)
                            elif b < GB - 1:
                                scores(G, w, b + 1, 0)
                            elif has(g):
                                scores(g, u, 0, 0)
                            scores_t(G, w, b, q)
                            if q:
                                values(G, w, b, q - 1)
                            elif b:
                                values(G, w, b - 1, QG - 1)
                            elif there(G - 1):
                                values(G - 1, u, GB - 1, QG - 1)
                            if q == 1 and there(n - 1):
                                turn(n - 1)
                            if q == 3 and there(n - 1):
                                project(n - 1)
                    elif isinstance(g, int) and g == NG + 1 and b == 0:
                        values(NG - 1, u, GB - 1, QG - 1)
                        turn(NG * GB - 1)
                        project(NG * GB - 1)

        @block.scalar
        def _(act):
            nc.scalar.preload_act_table_set(LN_EXP)
            act.wait_ge(ph.consts_in, all_consts)

            def copy_prep(g, u, b):
                act.wait_ge(prep_ready, g * 4 + b + 1)
                if b == 0 and there(g - 1):
                    act.wait_ge(prep_ready, g * 4)
                if b == 1 and there(g - 2):
                    act.wait_ge(st_ready, (g - 1) * GB * QG)
                if b == 3 and there(g - 2):
                    act.wait_ge(pv_done, (g - 1) * GB * QG)
                if b == 0:
                    ins = nc.scalar.activation(xT[:, :], pPrep[:, :], ACT.Copy)
                elif b == 1:
                    ins = nc.scalar.activation(qT[u][:, :], pPrep[:, :], ACT.Copy, scale=SCALE8 if biased else 1.0)
                elif b == 2:
                    ins = nc.scalar.activation(kT[u][:, :], pPrep[:, 0:K4], ACT.Copy)
                else:
                    ins = nc.scalar.activation(V[u][:, :, 0:DH], pPrep[0:S2, :].rearrange("p (h d) -> p h d", d=DH), ACT.Copy)
                ins.then_inc(prep_copied, 1)

            def exp(n, q):
                act.wait_ge(st_ready, n + 1)
                if there(n - 2):
                    act.wait_ge(pv_done, n - 1)
                nc.scalar.activation(PT[q % 2][:, :], pT[q % 2][:, :, :].rearrange("p h s -> p (h s)"), ACT.Exp,
                                     scale=1.0 if biased else SCALE8).then_inc(exp_done, 1)

            def copy_ot(n):
                act.wait_ge(ot_ready, n + 1)
                if there(n - 1):
                    act.wait_ge(f_ready, n)
                nc.scalar.activation(oT[:, :], pOT[:, :], ACT.Copy).then_inc(ot_copied, 1)

            for g, u in steps(act):
                G = g - 1
                for b in range(GB):
                    n = G * GB + b
                    if has(g):
                        copy_prep(g, u, b)
                    if there(G) and has(G):
                        for q in range(QG):
                            exp(n * QG + q, q)
                            if q == 1 and there(n - 1):
                                copy_ot(n - 1)
                    elif isinstance(g, int) and g == NG + 1 and b == 0:
                        copy_ot(NG * GB - 1)
                    if b == 1 and there(G - 1) and not biased:
                        norm.act_rstd(nc, act, G - 1)

        @block.vector
        def _(dve):
            dve.wait_ge(ph.consts_in, all_consts)

            def masked(g, u, b, q):
                if b < 2 or b == 2 and biased:
                    return
                if q == 0:
                    dve.wait_ge(prep_copied, g * 4 + b)
                    if there(g - 2):
                        dve.wait_ge(st_ready, (g - 1) * GB * QG)
                to, of, done = (Qm, qT, qm_done) if b == 2 else (Km, kT, km_done)
                for h in range(QH * q, QH * q + QH):
                    nc.vector.tensor_scalar(to[u][:, h, :], of[u][:, :], mask[:, h:h + 1], None, ALU.mult).then_inc(done, 1)

            def maximum(seq, b, q):
                n = seq * QG + q
                dve.wait_ge(s_ready, n + 1)
                if there(n - 2):
                    dve.wait_ge(st_ready, n - 1)
                of = pS[q % 2]
                if biased:
                    if q == 0:
                        dve.wait_ge(bias_loaded[b % 2], (seq - b % 2) * 8 + 16)
                    nc.vector.tensor_tensor(biased_s[q % 2][:, :, :], of[:, :, :], bias[b % 2][:, QH * q:QH * q + QH, :],
                                            ALU.add).then_inc(added, 1)
                    dve.wait_ge(added, n + 1)
                    of = biased_s[q % 2]
                nc.vector.tensor_reduce(neg_max[q % 2][:, :], of[:, :, :], AX.X, ALU.max, negate=True).then_inc(max_done, 1)

            def divide(n):
                dve.wait_ge(pv_done, (n + 1) * QG)
                if there(n - 1):
                    dve.wait_ge(on_done, n)
                nc.vector.reciprocal(rec[:, :], pO[:, :, DH]).then_inc(rec_done, 1)
                dve.wait_ge(rec_done, n + 1)
                if there(n - 1):
                    dve.wait_ge(ot_ready, n)
                nc.vector.tensor_tensor(on[:, :, :], pO[:, :, 0:DH], rec[:, :].unsqueeze(2).to_broadcast([S, HEADS16, DH]),
                                        ALU.mult).then_inc(on_done, 1)

            def residual(G, u, b):
                n = G * GB + b
                dve.wait_ge(f_ready, n + 1)
                if b == 0:
                    if biased:
                        dve.wait_ge(r_loaded[u], (G - u) * 8 + 16)
                        if there(G - 2):
                            dve.wait_ge(stored[u], (G - u) * 8)
                    else:
                        dve.wait_ge(xr_done, (G + 1) * GB)
                        if there(G - 2):
                            dve.wait_ge(norm.normed, (G - 1) * GB)
                nc.vector.tensor_tensor(R[u][:, b, :], pF[:, :], xr[u][:, b, :], ALU.add).then_inc(norm.summed, 1)

            for g, u in steps(dve):
                G, w = g - 1, 1 - u
                for b in range(GB):
                    n = G * GB + b
                    for q in range(QG):
                        if there(G) and has(G):
                            if b == 0 and q == 0 and isinstance(G, int) and G == 0:
                                maximum(n, b, q)
                            if q < QG - 1:
                                maximum(n, b, q + 1)
                            elif b < GB - 1 or has(g):
                                maximum(n + 1, (b + 1) % GB, 0)
                        if has(g):
                            masked(g, u, b, q)
                        last = isinstance(g, int) and g == NG + 1
                        if q == 0 and there(n - 2) and (has(G) or last and b == 0):
                            residual(*((G, w, b - 2) if b >= 2 else (G - 1, u, b + 2)))
                        if q == 0 and there(n - 1) and (has(G) or last and b == 0):
                            divide(n - 1)
                        if last and b == 0 and q == 1:
                            residual(NG - 1, u, GB - 1)
                    if b == 1 and there(G - 1) and not biased:
                        dve.wait_ge(norm.summed, G * GB)
                        norm.dve_stats(nc, dve, G - 1, R[u])
                    if b == 2 and there(G - 1) and not biased:
                        if there(G - 3):
                            dve.wait_ge(stored[u], (G - 1 - u) * 8)
                        norm.dve_scale(nc, dve, G - 1, xo[u], R[u])


E_R = 8
NE = E_R + 1
FC = 4
TOP = 2
ALPHA = 0.5
F16 = mybir.dt.float16
W_SCALE = 64.0


def phase_experts(nc, x_in, x_out, gate_in, w1_in, w3_in, w2_in, ident_in, iota_in, consts_in):
    with Phase(nc, "moe") as ph:
        sb, ps, sem = ph.sb, ph.ps, ph.sem
        w1, w3 = sb("w1", [D, NE, FC * 128]), sb("w3", [D, NE, FC * 128])
        w2 = sb("w2", [128, NE, FC, D])
        w1s, w3s = ([sb(f"{n}{half}", [D, NE, FC * 128], F16) for half in ("high", "low")] for n in ("w1", "w3"))
        wg = sb("wg", [D, E_R])
        ident, iota, consts = sb("ident", [128, 128]), sb("iota", [S, E_R]), sb("consts", [128, 2])
        x = [sb(f"x{u}", [S, GB, D]) for u in range(2)]
        xT = [sb(f"xT{u}", [D, GT]) for u in range(2)]
        xs = [[sb(f"x{half}{u}", [D, GT], F16) for half in ("high", "low")] for u in range(2)]
        logits, top = sb("logits", [S, GB, E_R]), sb("top", [S, GB, 8])
        where = sb("where", [S, GB, 8], mybir.dt.uint32)
        wheref, shifted, probs = sb("wheref", [S, GB, TOP]), sb("shifted", [S, GB, E_R]), sb("probs", [S, GB, E_R])
        chosen = [sb(f"chosen{k}", [S, GB, E_R]) for k in range(TOP)]
        total, scale = sb("total", [S, GB]), sb("scale", [S, GB])
        gate = [sb(f"gate{u}", [S, GB, E_R]) for u in range(2)]
        act_g = [sb(f"act_g{i}", [128, GT]) for i in range(2)]
        H = [[sb(f"H{i}{c}", [128, GT]) for c in range(FC)] for i in range(2)]
        acc = [sb(f"acc{u}", [S, GB, D]) for u in range(2)]
        xo = [sb(f"xo{u}", [S, GB, D]) for u in range(2)]
        pG = [ps(f"pG{i}", [128, GT]) for i in range(2)]
        pU = [ps(f"pU{i}", [128, GT]) for i in range(2)]
        pO = [ps(f"pO{i}", [S, GB, D]) for i in range(2)]
        pX, pL = ps("pX", [128, GT]), ps("pL", [S, GB, E_R])
        ph.consts_in = sem("consts_in")
        loaded = [sem(f"loaded{u}") for u in range(2)]
        xt_ready, xt_copied, logits_ready, probs_exp = sem("xt_ready"), sem("xt_copied"), sem("logits_ready"), sem("probs_exp")
        w_high, w_low, x_high, x_low = sem("w_high"), sem("w_low"), sem("x_high"), sem("x_low")
        small = sem("small")
        g_ready, u_ready, silu_done, h_done, o_ready, acc_done = (
            sem("g_ready"), sem("u_ready"), sem("silu_done"), sem("h_done"), sem("o_ready"), sem("acc_done"))
        stored = ph.stored
        norm = Norm(ph, "norm", consts[:, 0:1])
        block = ph.block()
        pairs = [(ident[:, :], ident_in), (wg[:, :], gate_in), (iota[:, :], iota_in), (consts[:, :], consts_in),
                 (w1[:, :, :], w1_in), (w3[:, :, :], w3_in), (w2[:, :, :, :], w2_in)]
        all_consts = 16 * len(pairs)
        SMALL = 2 * GB + 10

        def there(n):
            return not isinstance(n, int) or n >= 0

        def has(g):
            return not isinstance(g, int) or g < NG

        def steps(eng):
            yield from groups(eng)
            yield NG, 0
            yield NG + 1, 1

        @block.sync
        def _(sp):
            load_constants(ph, sp, pairs)
            for g, u in groups(sp):
                if there(g - 2):
                    sp.wait_ge(acc_done, (g - 2) * (NE * GB) + GB)
                sp.dma_start(x[u][:, :, :], x_in[g, :, :, :]).then_inc(loaded[u], 16)

        @block.gpsimd
        def _(pool):
            for g, u in steps(pool):
                if has(g):
                    pool.wait_ge(xt_copied, g + 1)
                    if there(g - 2):
                        pool.wait_ge(u_ready, (g - 1) * (NE * FC))
                    nc.gpsimd.tensor_tensor(xs[u][1][:, :], xT[u][:, :], xs[u][0][:, :], ALU.subtract).then_inc(x_low, 1)
                if there(g - 2):
                    pool.wait_ge(norm.normed, (g - 1) * GB)
                    pool.dma_start(x_out[g - 2, :, :, :], xo[u][:, :, :]).then_inc(stored[u], 16)
            for u in range(2):
                pool.wait_ge(stored[u], 16 * (NG // 2))

        @block.tensor
        def _(pe):
            pe.wait_ge(ph.consts_in, all_consts)

            def turn_x(g, u):
                pe.wait_ge(loaded[u], (g - u) * 8 + 16)
                if there(g - 1):
                    pe.wait_ge(xt_copied, g)
                for b in range(GB):
                    last = nc.tensor.transpose(pX[:, b * S:(b + 1) * S], x[u][:, b, :], ident[:, :])
                last.then_inc(xt_ready, 1)

            def gate_logits(g, u):
                pe.wait_ge(xt_copied, g + 1)
                if there(g - 1):
                    pe.wait_ge(small, (g - 1) * SMALL + 1)
                for b in range(GB):
                    last = nc.tensor.matmul(pL[:, b, :], xT[u][:, b * S:(b + 1) * S], wg[:, :], start=True, stop=True)
                last.then_inc(logits_ready, 1)

            def three_products(out, halves, e, w, c):
                (high, low), (x_h, x_l), cols = halves, xs[w], slice(c * 128, (c + 1) * 128)
                nc.tensor.matmul(out[:, :], high[:, e, cols], x_h[:, :], start=True, stop=False)
                nc.tensor.matmul(out[:, :], high[:, e, cols], x_l[:, :], start=False, stop=False)
                return nc.tensor.matmul(out[:, :], low[:, e, cols], x_h[:, :], start=False, stop=True)

            def up(m, e, w, c):
                k = m * FC + c
                if c == 0 and isinstance(m, int) and m < NE:
                    pe.wait_ge(w_low, 2 * (e + 1))
                if c == 0 and e == 0:
                    pe.wait_ge(x_low, m // NE + 1)
                if there(k - 2):
                    pe.wait_ge(silu_done, k - 1)
                three_products(pG[c % 2], w1s, e, w, c).then_inc(g_ready, 1)
                if there(k - 2):
                    pe.wait_ge(h_done, k - 1)
                three_products(pU[c % 2], w3s, e, w, c).then_inc(u_ready, 1)

            def down(m, e, i):
                pe.wait_ge(h_done, m * FC + FC)
                if there(m - 2):
                    pe.wait_ge(acc_done, (m - 1) * GB)
                for b in range(GB):
                    for c in range(FC):
                        last = nc.tensor.matmul(pO[i][:, b, :], H[i][c][:, b * S:(b + 1) * S], w2[:, e, c, :],
                                                start=(c == 0), stop=(c == FC - 1))
                last.then_inc(o_ready, 1)

            for g, u in steps(pe):
                G, w = g - 1, 1 - u
                if has(g):
                    turn_x(g, u)
                if there(G) and has(G):
                    for e in range(NE):
                        m, i = G * NE + e, (w * NE + e) % 2
                        for c in range(FC):
                            up(m, e, w, c)
                            if c == 0 and there(m - 1):
                                down(m - 1, (e - 1) % NE, 1 - i)
                        if e == 0 and has(g):
                            gate_logits(g, u)
                elif has(g):
                    gate_logits(g, u)
                else:
                    down(NG * NE - 1, NE - 1, (NG * NE - 1) % 2)

        @block.scalar
        def _(act):
            act.wait_ge(ph.consts_in, all_consts)
            for e in range(NE):
                for w_of, halves in ((w1, w1s), (w3, w3s)):
                    nc.scalar.activation(halves[0][:, e, :], w_of[:, e, :], ACT.Copy, scale=W_SCALE).then_inc(w_high, 1)

            def copy_xt(g, u):
                act.wait_ge(xt_ready, g + 1)
                if there(g - 2):
                    act.wait_ge(u_ready, (g - 1) * (NE * FC))
                nc.scalar.activation(xs[u][0][:, :], pX[:, :], ACT.Copy).then_inc(x_high, 1)
                nc.scalar.activation(xT[u][:, :], pX[:, :], ACT.Copy).then_inc(xt_copied, 1)

            def exp_logits(g):
                act.wait_ge(small, g * SMALL + 2 * GB + 2)
                nc.scalar.activation(probs[:, :, :], shifted[:, :, :], ACT.Exp).then_inc(probs_exp, 1)

            for g, u in steps(act):
                G, w = g - 1, 1 - u
                if has(g):
                    copy_xt(g, u)
                if there(G) and has(G):
                    for e in range(NE):
                        m, i = G * NE + e, (w * NE + e) % 2
                        for c in range(FC):
                            k = m * FC + c
                            act.wait_ge(g_ready, k + 1)
                            if there(k - 2):
                                act.wait_ge(h_done, k - 1)
                            nc.scalar.activation(act_g[c % 2][:, :], pG[c % 2][:, :], ACT.Silu,
                                                 scale=1.0 / W_SCALE).then_inc(silu_done, 1)
                        if e == 1:
                            nc.scalar.preload_act_table_set(LN_EXP)
                            if there(G - 1):
                                norm.act_rstd(nc, act, G - 1)
                            if has(g):
                                exp_logits(g)
                else:
                    nc.scalar.preload_act_table_set(LN_EXP)
                    if has(g):
                        exp_logits(g)
                    else:
                        norm.act_rstd(nc, act, NG - 1)

        @block.vector
        def _(dve):
            dve.wait_ge(ph.consts_in, all_consts)
            for e in range(NE):
                for j, (w_of, halves) in enumerate(((w1, w1s), (w3, w3s))):
                    dve.wait_ge(w_high, 2 * e + j + 1)
                    nc.vector.scalar_tensor_tensor(out=halves[1][:, e, :], in0=w_of[:, e, :], scalar=W_SCALE,
                                                   in1=halves[0][:, e, :], op0=ALU.mult, op1=ALU.subtract).then_inc(w_low, 1)

            def bc(a):
                return a.unsqueeze(2).to_broadcast([S, GB, E_R])

            def gates_before_exp(g):
                at = g * SMALL
                dve.wait_ge(logits_ready, g + 1)
                nc.vector.tensor_copy(logits[:, :, :], pL[:, :, :]).then_inc(small, 1)
                dve.wait_ge(small, at + 1)
                dve.nop(nofuse=True)
                for b in range(GB):
                    nc.vector.max(top[:, b, :], logits[:, b, :]).then_inc(small, 1)
                dve.wait_ge(small, at + 1 + GB)
                dve.nop(nofuse=True)
                for b in range(GB):
                    nc.vector.max_index(where[:, b, :], top[:, b, :], logits[:, b, :]).then_inc(small, 1)
                if there(g - 1):
                    dve.wait_ge(probs_exp, g)
                nc.vector.tensor_tensor(shifted[:, :, :], logits[:, :, :], bc(top[:, :, 0]), ALU.subtract).then_inc(small, 1)

            def gates_after_exp(g, u):
                at = g * SMALL + 2 * GB + 2
                dve.wait_ge(small, at - 1)
                nc.vector.tensor_copy(wheref[:, :, :], where[:, :, 0:TOP]).then_inc(small, 1)
                dve.wait_ge(probs_exp, g + 1)
                nc.vector.reduce_sum(total[:, :], probs[:, :, :], AX.X).then_inc(small, 1)
                dve.wait_ge(small, at + 1)
                iota_b = iota[:, :].unsqueeze(1).to_broadcast([S, GB, E_R])
                for k in range(TOP):
                    nc.vector.tensor_tensor(chosen[k][:, :, :], iota_b, bc(wheref[:, :, k]), ALU.is_equal).then_inc(small, 1)
                dve.wait_ge(small, at + 2)
                nc.vector.reciprocal(scale[:, :], total[:, :]).then_inc(small, 1)
                dve.wait_ge(small, at + 4)
                nc.vector.tensor_tensor(chosen[0][:, :, :], chosen[0][:, :, :], chosen[1][:, :, :], ALU.add).then_inc(small, 1)
                dve.wait_ge(small, at + 5)
                nc.vector.scalar_tensor_tensor(out=shifted[:, :, :], in0=probs[:, :, :], scalar=1.0 - ALPHA,
                                               in1=bc(scale[:, :]), op0=ALU.mult, op1=ALU.mult).then_inc(small, 1)
                dve.wait_ge(small, at + 7)
                if there(g - 2):
                    dve.wait_ge(acc_done, (g - 1) * (NE * GB) - GB)
                nc.vector.tensor_tensor(gate[u][:, :, :], shifted[:, :, :], chosen[0][:, :, :], ALU.mult).then_inc(small, 1)

            def add_expert(G, w, m, e, i):
                dve.wait_ge(o_ready, m + 1)
                for b in range(GB):
                    if e == 0:
                        if b == 0:
                            dve.wait_ge(small, (G + 1) * SMALL)
                            if there(G - 2):
                                dve.wait_ge(norm.normed, (G - 1) * GB)
                    else:
                        dve.wait_ge(acc_done, m * GB - GB + b + 1)
                    by = ALPHA / E_R if e == NE - 1 else gate[w][:, b, e:e + 1]
                    nc.vector.scalar_tensor_tensor(out=acc[w][:, b, :], in0=pO[i][:, b, :], scalar=by,
                                                   in1=(x if e == 0 else acc)[w][:, b, :],
                                                   op0=ALU.mult, op1=ALU.add).then_inc(acc_done, 1)

            for g, u in steps(dve):
                G, w = g - 1, 1 - u
                if there(G) and has(G):
                    for e in range(NE):
                        m, i = G * NE + e, (w * NE + e) % 2
                        for c in range(FC):
                            k = m * FC + c
                            dve.wait_ge(u_ready, k + 1)
                            dve.wait_ge(silu_done, k + 1)
                            if c == 0 and there(m - 2):
                                dve.wait_ge(o_ready, m - 1)
                            nc.vector.scalar_tensor_tensor(out=H[i][c][:, :], in0=pU[c % 2][:, :], scalar=1.0 / W_SCALE,
                                                           in1=act_g[c % 2][:, :], op0=ALU.mult, op1=ALU.mult).then_inc(h_done, 1)
                            if c == 0 and there(m - 1):
                                if e:
                                    add_expert(G, w, m - 1, e - 1, 1 - i)
                                else:
                                    add_expert(G - 1, u, m - 1, NE - 1, 1 - i)
                        if e == 0 and there(G - 1):
                            dve.wait_ge(acc_done, m * GB)
                            norm.dve_stats(nc, dve, G - 1, acc[u])
                        if e == 1 and has(g):
                            gates_before_exp(g)
                        if e == 2 and there(G - 1):
                            if there(G - 3):
                                dve.wait_ge(stored[u], (G - 1 - u) * 8)
                            norm.dve_scale(nc, dve, G - 1, xo[u], acc[u])
                        if e == 2 and has(g):
                            gates_after_exp(g, u)
                elif has(g):
                    gates_before_exp(g)
                    gates_after_exp(g, u)
                else:
                    m = NG * NE - 1
                    add_expert(NG - 1, u, m, NE - 1, m % 2)
                    dve.wait_ge(acc_done, NG * NE * GB)
                    norm.dve_stats(nc, dve, NG - 1, acc[u])
                    dve.wait_ge(stored[u], (NG - 1 - u) * 8)
                    norm.dve_scale(nc, dve, NG - 1, xo[u], acc[u])


def phase_attention(nc, x_in, x_out, w_q, w_k, w_v, w_out, ident_in, consts_in):
    with Phase(nc, "att") as ph:
        sb, ps, sem = ph.sb, ph.ps, ph.sem
        wq, wk, wv, wo = (sb(n, [D, D]) for n in ("wq", "wk", "wv", "wo"))
        ident, consts = sb("ident", [128, 128]), sb("consts", [128, 2])
        x = [sb(f"x{u}", [S, GB, D]) for u in range(2)]
        xr = [sb(f"xr{u}", [S, GB, D]) for u in range(2)]
        xT = sb("xT", [D, GT])
        qT = [sb(f"qT{u}", [D, GT]) for u in range(2)]
        kT = [sb(f"kT{u}", [D, GT]) for u in range(2)]
        V = [sb(f"V{u}", [S, GB, D]) for u in range(2)]
        neg_max, P, PT, cT = sb("neg_max", [S, GB]), sb("P", [S, GB, S]), sb("PT", [S, GT]), sb("cT", [D, GT])
        total, rec = [sb(f"total{u}", [S, GB]) for u in range(2)], sb("rec", [S, GB])
        R, xo = sb("R", [S, GB, D]), [sb(f"xo{u}", [S, GB, D]) for u in range(2)]
        pX, pQ, pK, pP, pC = (ps(n, [128, GT]) for n in ("pX", "pQ", "pK", "pP", "pC"))
        pV, pS, pO = (ps(n, [S, GB, D]) for n in ("pV", "pS", "pO"))
        ph.consts_in = sem("consts_in")
        loaded, r_loaded = [sem(f"loaded{u}") for u in range(2)], ph.pool_loaded
        stored = ph.stored
        x_ready, x_copied, q_ready, q_copied, k_ready, k_copied, v_ready, v_copied = (
            sem(n) for n in ("x_ready", "x_copied", "q_ready", "q_copied", "k_ready", "k_copied", "v_ready", "v_copied"))
        s_ready, max_done, exp_done, p_ready, p_copied, c_ready, c_copied, o_ready, rec_done = (
            sem(n) for n in ("s_ready", "max_done", "exp_done", "p_ready", "p_copied", "c_ready", "c_copied", "o_ready",
                             "rec_done"))
        norm = Norm(ph, "norm", consts[:, 0:1])
        block = ph.block()
        pairs = [(wq[:, :], w_q), (wk[:, :], w_k), (wv[:, :], w_v), (wo[:, :], w_out), (ident[:, :], ident_in),
                 (consts[:, :], consts_in)]
        all_consts = 16 * len(pairs)

        @block.sync
        def _(sp):
            load_constants(ph, sp, pairs)
            for g, u in groups(sp):
                if there(g - 2):
                    sp.wait_ge(x_ready, g - 1)
                sp.dma_start(x[u][:, :, :], x_in[g, :, :, :]).then_inc(loaded[u], 16)

        @block.gpsimd
        def _(pool):
            for g, u in steps(pool):
                if there(g - 2):
                    pool.wait_ge(norm.normed, (g - 1) * GB)
                    pool.dma_start(x_out[g - 2, :, :, :], xo[u][:, :, :]).then_inc(stored[u], 16)
                if has(g):
                    pool.dma_start(xr[u][:, :, :], x_in[g, :, :, :]).then_inc(r_loaded[u], 16)
            for u in range(2):
                pool.wait_ge(stored[u], 16 * (NG // 2))

        @block.tensor
        def _(pe):
            pe.wait_ge(ph.consts_in, all_consts)
            for g, u in steps(pe):
                w = 1 - u
                if has(g):
                    pe.wait_ge(loaded[u], (g - u) * 8 + 16)
                    if there(g - 1):
                        pe.wait_ge(x_copied, g)
                    for b in range(GB):
                        last = nc.tensor.transpose(pX[:, b * S:(b + 1) * S], x[u][:, b, :], ident[:, :])
                    last.then_inc(x_ready, 1)
                if there(g - 1) and has(g - 1):
                    pe.wait_ge(q_copied, g)
                    pe.wait_ge(k_copied, g)
                    if there(g - 2):
                        pe.wait_ge(exp_done, (g - 1) * GB)
                    for b in range(GB):
                        t = slice(b * S, (b + 1) * S)
                        last = nc.tensor.matmul(pS[:, b, :], qT[w][:, t], kT[w][:, t], start=True, stop=True)
                    last.then_inc(s_ready, 1)
                if has(g):
                    pe.wait_ge(x_copied, g + 1)
                    if there(g - 1):
                        pe.wait_ge(q_copied, g)
                    nc.tensor.matmul(pQ[:, :], wq[:, :], xT[:, :], start=True, stop=True).then_inc(q_ready, 1)
                    if there(g - 1):
                        pe.wait_ge(k_copied, g)
                    nc.tensor.matmul(pK[:, :], wk[:, :], xT[:, :], start=True, stop=True).then_inc(k_ready, 1)
                    if there(g - 1):
                        pe.wait_ge(v_copied, g)
                    for b in range(GB):
                        last = nc.tensor.matmul(pV[:, b, :], xT[:, b * S:(b + 1) * S], wv[:, :], start=True, stop=True)
                    last.then_inc(v_ready, 1)
                if there(g - 1) and has(g - 1):
                    if there(g - 2):
                        pe.wait_ge(p_copied, g - 1)
                    for b in range(GB):
                        pe.wait_ge(exp_done, (g - 1) * GB + b + 1)
                        last = nc.tensor.transpose(pP[:, b * S:(b + 1) * S], P[:, b, :], ident[:, :])
                    last.then_inc(p_ready, 1)
                if there(g - 2):
                    pe.wait_ge(c_copied, g - 1)
                    if there(g - 3):
                        pe.wait_ge(norm.summed, (g - 2) * GB)
                    for b in range(GB):
                        last = nc.tensor.matmul(pO[:, b, :], cT[:, b * S:(b + 1) * S], wo[:, :], start=True, stop=True)
                    last.then_inc(o_ready, 1)
                if there(g - 1) and has(g - 1):
                    pe.wait_ge(p_copied, g)
                    pe.wait_ge(v_copied, g)
                    if there(g - 2):
                        pe.wait_ge(c_copied, g - 1)
                    for b in range(GB):
                        t = slice(b * S, (b + 1) * S)
                        last = nc.tensor.matmul(pC[:, t], V[w][:, b, :], PT[:, t], start=True, stop=True)
                    last.then_inc(c_ready, 1)

        @block.scalar
        def _(act):
            nc.scalar.preload_act_table_set(LN_EXP)
            act.wait_ge(ph.consts_in, all_consts)
            for g, u in steps(act):
                if has(g):
                    act.wait_ge(x_ready, g + 1)
                    if there(g - 1):
                        act.wait_ge(v_ready, g)
                    nc.scalar.activation(xT[:, :], pX[:, :], ACT.Copy).then_inc(x_copied, 1)
                if there(g - 1) and has(g - 1):
                    if there(g - 2):
                        act.wait_ge(p_ready, g - 1)
                    if there(g - 3):
                        act.wait_ge(rec_done, g - 2)
                    act.wait_ge(max_done, g)
                    for b in range(GB):
                        nc.scalar.activation(P[:, b, :], pS[:, b, :], ACT.Exp, bias=neg_max[:, b:b + 1],
                                             accum_out=total[1 - u][:, b:b + 1]).then_inc(exp_done, 1)
                if has(g):
                    act.wait_ge(q_ready, g + 1)
                    if there(g - 2):
                        act.wait_ge(s_ready, g - 1)
                    nc.scalar.activation(qT[u][:, :], pQ[:, :], ACT.Copy, scale=float(D) ** -0.5).then_inc(q_copied, 1)
                    act.wait_ge(k_ready, g + 1)
                    nc.scalar.activation(kT[u][:, :], pK[:, :], ACT.Copy).then_inc(k_copied, 1)
                if there(g - 1) and has(g - 1):
                    act.wait_ge(p_ready, g)
                    if there(g - 2):
                        act.wait_ge(c_ready, g - 1)
                    nc.scalar.activation(PT[:, :], pP[:, :], ACT.Copy).then_inc(p_copied, 1)
                if there(g - 2):
                    norm.act_rstd(nc, act, g - 2)

        @block.vector
        def _(dve):
            dve.wait_ge(ph.consts_in, all_consts)
            for g, u in steps(dve):
                if there(g - 1) and has(g - 1):
                    dve.wait_ge(s_ready, g)
                    if there(g - 2):
                        dve.wait_ge(exp_done, (g - 1) * GB)
                    nc.vector.tensor_reduce(neg_max[:, :], pS[:, :, :], AX.X, ALU.max, negate=True).then_inc(max_done, 1)
                if there(g - 2):
                    nc.vector.reciprocal(rec[:, :], total[u][:, :]).then_inc(rec_done, 1)
                if has(g):
                    dve.wait_ge(v_ready, g + 1)
                    if there(g - 2):
                        dve.wait_ge(c_ready, g - 1)
                    nc.vector.tensor_copy(V[u][:, :, :], pV[:, :, :]).then_inc(v_copied, 1)
                if there(g - 2):
                    dve.wait_ge(o_ready, g - 1)
                    dve.wait_ge(rec_done, g - 1)
                    dve.wait_ge(r_loaded[u], (g - 2 - u) * 8 + 16)
                    for b in range(GB):
                        nc.vector.scalar_tensor_tensor(out=R[:, b, :], in0=pO[:, b, :], scalar=rec[:, b:b + 1],
                                                       in1=xr[u][:, b, :], op0=ALU.mult, op1=ALU.add).then_inc(norm.summed, 1)
                    dve.wait_ge(norm.summed, (g - 1) * GB)
                    norm.dve_stats(nc, dve, g - 2, R)
                if there(g - 1) and has(g - 1):
                    dve.wait_ge(c_ready, g)
                    if there(g - 2):
                        dve.wait_ge(o_ready, g - 1)
                    nc.vector.tensor_copy(cT[:, :], pC[:, :]).then_inc(c_copied, 1)
                if there(g - 2):
                    if there(g - 4):
                        dve.wait_ge(stored[u], (g - 2 - u) * 8)
                    norm.dve_scale(nc, dve, g - 2, xo[u], R)


def phase_feedforward(nc, x_in, x1_in, x_out, w1_in, b1_in, w2_in, b2_in, g1_in, be1_in, g2_in, be2_in, ident_in, consts_in):
    FC1 = 4
    with Phase(nc, "ffn") as ph:
        sb, ps, sem = ph.sb, ph.ps, ph.sem
        w1, w2 = sb("w1", [D, FC1 * 128]), sb("w2", [128, FC1, D])
        ident, consts = sb("ident", [128, 128]), sb("consts", [128, 2])
        b1, g1, be1 = sb("b1", [128, FC1]), sb("g1", [D, 1]), sb("be1", [D, 1])
        b2, g2, be2 = sb("b2", [S, D]), sb("g2", [S, D]), sb("be2", [S, D])
        x1 = [sb(f"x1{u}", [S, GB, D]) for u in range(2)]
        x1b = [sb(f"x1b{u}", [S, GB, D]) for u in range(2)]
        x0 = [sb(f"x0{u}", [S, GB, D]) for u in range(2)]
        x2, y, xo = ([sb(f"{n}{u}", [S, GB, D]) for u in range(2)] for n in ("x2", "y", "xo"))
        n1, nT = sb("n1", [S, GB, D]), [sb(f"nT{u}", [D, GT]) for u in range(2)]
        H = [sb(f"H{c}", [128, GT]) for c in range(FC1)]
        pX, pH, pO = ps("pX", [D, GT]), [ps(f"pH{c}", [128, GT]) for c in range(FC1)], ps("pO", [S, GB, D])
        ph.consts_in = sem("consts_in")
        loaded, r_loaded = [sem(f"loaded{u}") for u in range(2)], [sem(f"r_loaded{u}") for u in range(2)]
        stored = ph.stored
        x1b_done, x0b_done, t_ready, t_copied, h_ready, gelu_done, o_ready, x2_done, scaled, y_done = (
            sem(n) for n in ("x1b_done", "x0b_done", "t_ready", "t_copied", "h_ready", "gelu_done", "o_ready", "x2_done",
                             "scaled", "y_done"))
        norm1, norm2, norm3 = (Norm(ph, f"norm{i}", consts[:, 0:1]) for i in (1, 2, 3))
        block = ph.block()
        pairs = [(w1[:, :], w1_in), (w2[:, :, :], w2_in), (ident[:, :], ident_in), (consts[:, :], consts_in),
                 (b1[:, :], b1_in), (g1[:, :], g1_in), (be1[:, :], be1_in), (b2[:, :], b2_in.partition_broadcast(S)),
                 (g2[:, :], g2_in.partition_broadcast(S)), (be2[:, :], be2_in.partition_broadcast(S))]
        all_consts = 16 * len(pairs)

        def steps3(eng):
            yield from steps(eng, 6)
            yield NG + 2, 0

        @block.sync
        def _(sp):
            load_constants(ph, sp, pairs)
            for g, u in groups(sp):
                if there(g - 2):
                    sp.wait_ge(norm1.normed, (g - 1) * GB)
                    sp.wait_ge(x1b_done, (g - 1) * GB)
                sp.dma_start(x1[u][:, :, :], x1_in[g, :, :, :]).then_inc(loaded[u], 16)
                if there(g - 2):
                    sp.wait_ge(y_done, g - 1)
                sp.dma_start(x0[u][:, :, :], x_in[g, :, :, :]).then_inc(r_loaded[u], 16)

        @block.gpsimd
        def _(pool):
            pool.wait_ge(ph.consts_in, all_consts)
            for g, u in steps3(pool):
                if has(g):
                    pool.wait_ge(loaded[u], (g - u) * 8 + 16)
                    if there(g - 2):
                        pool.wait_ge(x2_done, g - 1)
                    for b in range(GB):
                        nc.gpsimd.tensor_tensor(x1b[u][:, b, :], x1[u][:, b, :], b2[:, :], ALU.add).then_inc(x1b_done, 1)
                    pool.wait_ge(r_loaded[u], (g - u) * 8 + 16)
                    for b in range(GB):
                        nc.gpsimd.tensor_tensor(x0[u][:, b, :], x0[u][:, b, :], be2[:, :], ALU.add).then_inc(x0b_done, 1)
                if there(g - 3):
                    pool.wait_ge(norm3.normed, (g - 2) * GB)
                    pool.dma_start(x_out[g - 3, :, :, :], xo[1 - u][:, :, :]).then_inc(stored[1 - u], 16)
            for u in range(2):
                pool.wait_ge(stored[u], 16 * (NG // 2))

        @block.tensor
        def _(pe):
            pe.wait_ge(ph.consts_in, all_consts)
            for g, u in steps(pe):
                if there(g - 1) and has(g - 1):
                    pe.wait_ge(t_copied, g)
                    for c in range(FC1):
                        if there(g - 2):
                            pe.wait_ge(gelu_done, (g - 2) * FC1 + c + 1)
                        nc.tensor.matmul(pH[c][:, :], w1[:, c * 128:(c + 1) * 128], nT[1 - u][:, :],
                                         start=True, stop=True).then_inc(h_ready, 1)
                if there(g - 1) and has(g - 1):
                    pe.wait_ge(gelu_done, g * FC1)
                    if there(g - 2):
                        pe.wait_ge(x2_done, g - 1)
                    for b in range(GB):
                        for c in range(FC1):
                            last = nc.tensor.matmul(pO[:, b, :], H[c][:, b * S:(b + 1) * S], w2[:, c, :],
                                                    start=(c == 0), stop=(c == FC1 - 1))
                    last.then_inc(o_ready, 1)
                if has(g):
                    if there(g - 1):
                        pe.wait_ge(t_copied, g)
                    for b in range(GB):
                        pe.wait_ge(norm1.normed, g * GB + b + 1)
                        last = nc.tensor.transpose(pX[:, b * S:(b + 1) * S], n1[:, b, :], ident[:, :])
                    last.then_inc(t_ready, 1)

        @block.scalar
        def _(act):
            act.wait_ge(ph.consts_in, all_consts)
            for g, u in steps3(act):
                if there(g - 1) and has(g - 1):
                    for c in range(FC1):
                        act.wait_ge(h_ready, (g - 1) * FC1 + c + 1)
                        if c == 0 and there(g - 2):
                            act.wait_ge(o_ready, g - 1)
                        nc.scalar.activation(H[c][:, :], pH[c][:, :], ACT.Gelu, bias=b1[:, c:c + 1]).then_inc(gelu_done, 1)
                nc.scalar.preload_act_table_set(LN_EXP)
                if has(g):
                    norm1.act_rstd(nc, act, g)
                if there(g - 2) and has(g - 2):
                    norm2.act_rstd(nc, act, g - 2)
                if there(g - 3):
                    norm3.act_rstd(nc, act, g - 3)
                if has(g):
                    act.wait_ge(t_ready, g + 1)
                    if there(g - 2):
                        act.wait_ge(h_ready, (g - 1) * FC1)
                    nc.scalar.activation(nT[u][:, :], pX[:, :], ACT.Identity, scale=g1[:, 0:1],
                                         bias=be1[:, 0:1]).then_inc(t_copied, 1)

        @block.vector
        def _(dve):
            dve.wait_ge(ph.consts_in, all_consts)
            for g, u in steps3(dve):
                if has(g):
                    dve.wait_ge(loaded[u], (g - u) * 8 + 16)
                    norm1.dve_stats(nc, dve, g, x1[u])
                if there(g - 2) and has(g - 2):
                    norm2.dve_stats(nc, dve, g - 2, x2[u])
                if there(g - 3):
                    norm3.dve_stats(nc, dve, g - 3, y[1 - u])
                if has(g):
                    if there(g - 1):
                        dve.wait_ge(t_ready, g)
                    norm1.dve_scale(nc, dve, g, n1, x1[u])
                if there(g - 2) and has(g - 2):
                    norm2.dve_scale(nc, dve, g - 2, x2[u], x2[u])
                if there(g - 3):
                    if there(g - 5):
                        dve.wait_ge(stored[1 - u], (g - 4 + u) * 8)
                    norm3.dve_scale(nc, dve, g - 3, xo[1 - u], y[1 - u])
                if there(g - 2) and has(g - 2):
                    dve.wait_ge(norm2.normed, (g - 1) * GB)
                    nc.vector.tensor_tensor(x2[u][:, :, :], x2[u][:, :, :], g2[:, :].unsqueeze(1).to_broadcast([S, GB, D]),
                                            ALU.mult).then_inc(scaled, 1)
                if there(g - 1) and has(g - 1):
                    dve.wait_ge(o_ready, g)
                    dve.wait_ge(x1b_done, g * GB)
                    if there(g - 3):
                        dve.wait_ge(y_done, g - 2)
                    nc.vector.tensor_tensor(x2[1 - u][:, :, :], pO[:, :, :], x1b[1 - u][:, :, :], ALU.add).then_inc(x2_done, 1)
                if there(g - 2) and has(g - 2):
                    dve.wait_ge(scaled, g - 1)
                    dve.wait_ge(x0b_done, (g - 1) * GB)
                    if there(g - 4):
                        dve.wait_ge(norm3.normed, (g - 3) * GB)
                    nc.vector.tensor_tensor(y[u][:, :, :], x2[u][:, :, :], x0[u][:, :, :], ALU.add).then_inc(y_done, 1)
                if there(g - 1) and has(g - 1):
                    dve.wait_ge(x2_done, g)
                if there(g - 2) and has(g - 2):
                    dve.wait_ge(y_done, g - 1)


WH, WD = 8, 64
INNER = WH * WD
HALF = WD // 2
PAIRS = WH // 2
NSEQ = NG * GB
DRAIN = 7
LN2_16 = 16 * 0.6931471805599453


def phase_window(nc, name, x_in, x_out, wqkv_in, wo_in, tables_in, q_scale_in, k_scale_in, ident_in, mask_in, consts_in):
    with Phase(nc, name) as ph:
        sb, ps, sem = ph.sb, ph.ps, ph.sem
        wqkv, wo = sb("wqkv", [D, 3 * INNER]), sb("wo", [128, PAIRS, D])
        ident, identb, maskb = sb("ident", [128, 128]), sb("identb", [128, 128], BF16), sb("maskb", [S, S], BF16)
        maskf, consts = sb("maskf", [S, S]), sb("consts", [128, 4])
        tables = sb("tables", [S, 4, WD])
        scales = sb("scales", [S, 4, WD])
        x, xr, R = ([sb(f"{n}{u}", [S, GB, D]) for u in range(2)] for n in ("x", "xr", "R"))
        xs = sb("xs", [D, S])
        sq = [sb(f"sq{i}", [S, WH, WD]) for i in range(2)]
        ss = sb("ss", [S, 2 * WH])
        rn = [sb(f"rn{i}", [S, 2 * WH]) for i in range(2)]
        A = [sb(f"A{i}", [S, WH, WD]) for i in range(2)]
        Bm = [sb(f"B{i}", [S, WH, WD]) for i in range(2)]
        rot = [[sb(f"rot{j}{i}", [S, WH, WD]) for i in range(2)] for j in range(2)]
        V = [sb(f"V{b}", [S, INNER]) for b in range(GB)]
        qT, kTm = sb("qT", [128, PAIRS, S]), sb("kTm", [128, PAIRS, 2, S])
        neg_max, bias = sb("neg_max", [S, WH]), sb("bias", [S, WH])
        P, PT = [sb(f"P{i}", [S, WH, S]) for i in range(2)], sb("PT", [S, WH, S])
        total, rec, oT = sb("total", [S, WH]), sb("rec", [S, WH]), sb("oT", [128, PAIRS, S])
        pQ, pK, pV = (ps(n, [S, 512]) for n in ("pQ", "pK", "pV"))
        pT = [ps(f"pT{i}", [128, 4, S]) for i in range(2)]
        pS = [ps(f"pS{i}", [S, 4, S]) for i in range(2)]
        pO = ps("pO", [128, PAIRS, S])
        ph.consts_in = sem("consts_in")
        stored = ph.stored
        loaded, r_loaded = ([sem(f"{n}{u}") for u in range(2)] for n in ("loaded", "r_loaded"))
        set_up, tabled = sem("set_up"), sem("tabled")
        (xt_ready, xs_copied, v_ready, k_ready, q_ready, v_copied, sq_done, ss_done, ss_max, ln_done, rn_done) = (
            sem(n) for n in ("xt_ready", "xs_copied", "v_ready", "k_ready", "q_ready", "v_copied", "sq_done", "ss_done",
                             "ss_max", "ln_done", "rn_done"))
        ab_done, rot_done, k_normed, t_ready, t_copied, s_ready, max_done, bias_done, exp_done, rec_done, p_normed = (
            sem(n) for n in ("ab_done", "rot_done", "k_normed", "t_ready", "t_copied", "s_ready", "max_done", "bias_done",
                             "exp_done", "rec_done", "p_normed"))
        pt_ready, pt_copied, pv_ready, o_copied, f_ready, summed = (
            sem(n) for n in ("pt_ready", "pt_copied", "pv_ready", "o_copied", "f_ready", "summed"))
        block = ph.block()
        h0, h1 = slice(0, HALF), slice(HALF, WD)
        pairs = [(wqkv[:, :], wqkv_in), (wo[:, :, :], wo_in), (ident[:, :], ident_in), (maskf[:, :], mask_in),
                 (consts[:, :], consts_in), (tables[:, :, :], tables_in)]
        for j, scale_in in ((0, q_scale_in), (2, k_scale_in)):
            pairs += [(scales[:, j, :], scale_in.partition_broadcast(S)),
                      (scales[:, j + 1, h0], scale_in[h1].partition_broadcast(S)),
                      (scales[:, j + 1, h1], scale_in[h0].partition_broadcast(S))]
        all_consts = 16 * len(pairs)
        KQ = (1, 0)

        def seq(n):
            return not isinstance(n, int) or 0 <= n < NSEQ

        def seq_steps(eng):
            for g, u in groups(eng):
                for b in range(GB):
                    yield g * GB + b, g, u, b
            for b in range(DRAIN):
                yield NSEQ + b, NG + b // GB, b // GB, b % GB

        @block.sync
        def _(sp):
            load_constants(ph, sp, pairs)
            for g, u in groups(sp):
                if there(g - 2):
                    sp.wait_ge(xt_ready, (g - 1) * GB)
                sp.dma_start(x[u][:, :, :], x_in[g, :, :, :]).then_inc(loaded[u], 16)
                if there(g - 2):
                    sp.wait_ge(summed, (g - 1) * GB)
                sp.dma_start(xr[u][:, :, :], x_in[g, :, :, :]).then_inc(r_loaded[u], 16)

        @block.gpsimd
        def _(pool):
            nc.gpsimd.memset(xs[:, :], 0.0).then_inc(set_up, 1)
            nc.gpsimd.memset(kTm[:, :, :, :], 0.0).then_inc(set_up, 1)
            pool.wait_ge(ph.consts_in, all_consts)
            nc.gpsimd.tensor_copy(identb[:, :], ident[:, :]).then_inc(set_up, 1)
            nc.gpsimd.tensor_copy(maskb[:, :], maskf[:, :]).then_inc(set_up, 1)
            for s, g, u, b in seq_steps(pool):
                if seq(s - 1):
                    i = (b - 1) % 2
                    for at, j in enumerate(KQ):
                        pool.wait_ge(ab_done, (s - 1) * 6 + 3 * (at + 1))
                        if seq(s - 3):
                            pool.wait_ge(t_ready, (s - 2) * 2)
                        nc.gpsimd.tensor_tensor(rot[j][i][:, :, :], A[j][:, :, :], Bm[j][:, :, :], ALU.add).then_inc(rot_done, 1)
                if b == 2 and there(g - 2):
                    pool.wait_ge(summed, (g - 1) * GB)
                    pool.dma_start(x_out[g - 2, :, :, :], R[u][:, :, :]).then_inc(stored[u], 16)
            for u in range(2):
                pool.wait_ge(stored[u], 16 * (NG // 2))

        @block.tensor
        def _(pe):
            pe.wait_ge(ph.consts_in, all_consts)
            pe.wait_ge(set_up, 4)
            for s, g, u, b in seq_steps(pe):
                for j in range(2):
                    if seq(s - 2):
                        n, i = s - 2, b % 2
                        if seq(n - 3):
                            pe.wait_ge(pt_copied, (n - 3) * 2 + j + 1)
                        if j == 0:
                            pe.wait_ge(rot_done, n * 2 + 2)
                        else:
                            pe.wait_ge(k_normed, n + 1)
                        for c in range(PAIRS):
                            last = nc.tensor.transpose(pT[j][:, c, :],
                                                       rot[j][i][:, 2 * c:2 * c + 2, :].rearrange("p h d -> p (h d)"), ident[:, :])
                        last.then_inc(t_ready, 1)
                    if seq(s - 1) and j == 0:
                        n = s - 1
                        pe.wait_ge(xs_copied, 2 * n + 2)
                        if seq(n - 1):
                            pe.wait_ge(ab_done, (n - 1) * 6 + 3)
                            pe.wait_ge(sq_done, (n - 1) * 2 + 1)
                        nc.tensor.matmul(pK[:, :], xs[:, :], wqkv[:, INNER:2 * INNER], start=True, stop=True).then_inc(k_ready, 1)
                        nc.tensor.matmul(pV[:, :], xs[:, :], wqkv[:, 2 * INNER:3 * INNER], start=True, stop=True).then_inc(v_ready, 1)
                if seq(s - 1):
                    n = s - 1
                    if seq(n - 5):
                        pe.wait_ge(summed, n - 4)
                    elif seq(n - 1):
                        pe.wait_ge(ab_done, n * 6)
                        pe.wait_ge(sq_done, n * 2)
                    nc.tensor.matmul(pQ[:, :], xs[:, :], wqkv[:, 0:INNER], start=True, stop=True).then_inc(q_ready, 1)
                if seq(s - 2):
                    n = s - 2
                    pe.wait_ge(t_copied, (n + 1) * 3)
                    for j in range(2):
                        if seq(n - 1):
                            pe.wait_ge(exp_done, (n - 1) * WH + 4 * j + 4)
                        nc.tensor.matmul(pS[j][:, :, :], identb[:, :], maskb[:, :].unsqueeze(1).to_broadcast([S, 4, S]),
                                         start=True, stop=False, skip_group_check=True)
                        for c in range(2):
                            last = nc.tensor.matmul(pS[j][:, 2 * c:2 * c + 2, :], qT[:, 2 * j + c, :], kTm[:, 2 * j + c, :, :],
                                                    start=False, stop=(c == 1), skip_group_check=True)
                        last.then_inc(s_ready, 1)
                if seq(s - 4):
                    n, i = s - 4, b % 2
                    for h in range(WH):
                        if h % 4 == 0 and not seq(s - 2):
                            pe.wait_ge(pt_copied, n * 2)
                        pe.wait_ge(p_normed, n * WH + h + 1)
                        last = nc.tensor.transpose(pT[h // 4][:, h % 4, :], P[i][:, h, :], ident[:, :])
                        if h % 4 == 3:
                            last.then_inc(pt_ready, 1)
                if seq(s):
                    if b == 0:
                        pe.wait_ge(loaded[u], (g - u) * 8 + 16)
                    if seq(s - 1):
                        pe.wait_ge(v_copied, s)
                    nc.tensor.transpose(pV[:, 0:S], x[u][:, b, :], ident[:, :]).then_inc(xt_ready, 1)
                if seq(s - 4):
                    n = s - 4
                    if seq(n - 1):
                        pe.wait_ge(o_copied, n)
                    for h in range(WH):
                        if h % 4 == 0:
                            pe.wait_ge(pt_copied, n * 2 + h // 4 + 1)
                        r = slice(WD * (h % 2), WD * (h % 2) + WD)
                        last = nc.tensor.matmul(pO[r, h // 2, :], V[b][:, h * WD:(h + 1) * WD], PT[:, h, :],
                                                start=True, stop=True)
                    last.then_inc(pv_ready, 1)
                if seq(s - 5):
                    n = s - 5
                    pe.wait_ge(o_copied, n + 1)
                    if seq(s - 1):
                        pe.wait_ge(ab_done, s * 6)
                        pe.wait_ge(sq_done, s * 2)
                    else:
                        pe.wait_ge(summed, n)
                    for c in range(PAIRS):
                        last = nc.tensor.matmul(pQ[:, 0:D], oT[:, c, :], wo[:, c, :], start=(c == 0), stop=(c == PAIRS - 1))
                    last.then_inc(f_ready, 1)

        @block.scalar
        def _(act):
            nc.scalar.preload_act_table_set(LN_EXP)
            act.wait_ge(ph.consts_in, all_consts)
            act.wait_ge(set_up, 4)
            for s, g, u, b in seq_steps(act):
                if seq(s - 3):
                    n, i = s - 3, (b + 1) % 2
                    if seq(n - 2):
                        act.wait_ge(pt_ready, (n - 1) * 2)
                    for h in range(WH):
                        if h % 4 == 0:
                            act.wait_ge(bias_done, n * 2 + h // 4 + 1)
                        nc.scalar.activation(P[i][:, h, :], pS[h // 4][:, h % 4, :], ACT.Exp, bias=bias[:, h:h + 1],
                                             scale=rn[i][:, h:h + 1], accum_out=total[:, h:h + 1]).then_inc(exp_done, 1)
                if seq(s - 2):
                    n = s - 2
                    if seq(n - 1):
                        act.wait_ge(s_ready, n * 2)
                    act.wait_ge(t_ready, n * 2 + 1)
                    nc.scalar.activation(qT[:, :, :], pT[0][:, :, :], ACT.Copy).then_inc(t_copied, 1)
                    act.wait_ge(t_ready, n * 2 + 2)
                    for j in range(2):
                        r = slice(64 * j, 64 * j + 64)
                        nc.scalar.activation(kTm[r, :, j, :], pT[1][r, :, :], ACT.Copy).then_inc(t_copied, 1)
                if seq(s - 5):
                    n = s - 5
                    act.wait_ge(pv_ready, n + 1)
                    if seq(n - 1):
                        act.wait_ge(f_ready, n)
                    nc.scalar.activation(oT[:, :, :], pO[:, :, :], ACT.Copy).then_inc(o_copied, 1)
                if seq(s - 1):
                    n = s - 1
                    if seq(n - 1):
                        act.wait_ge(ss_done, n * 2)
                    for j, of, ready in ((1, pK, k_ready), (0, pQ, q_ready)):
                        act.wait_ge(ready, n + 1)
                        nc.scalar.activation(sq[j][:, :, :], of[:, :].rearrange("p (h d) -> p h d", d=WD), ACT.Square).then_inc(sq_done, 1)
                    act.wait_ge(v_ready, n + 1)
                    nc.scalar.activation(V[(b - 1) % GB][:, :], pV[:, :], ACT.Copy).then_inc(v_copied, 1)
                if seq(s - 4):
                    n = s - 4
                    for j in range(2):
                        act.wait_ge(pt_ready, n * 2 + j + 1)
                        nc.scalar.activation(PT[:, 4 * j:4 * j + 4, :], pT[j][:, :, :], ACT.Copy).then_inc(pt_copied, 1)
                if seq(s):
                    act.wait_ge(xt_ready, s + 1)
                    if seq(s - 1):
                        act.wait_ge(q_ready, s)
                    nc.scalar.activation(xs[0:64, :], pV[0:64, 0:S], ACT.Copy).then_inc(xs_copied, 1)
                    nc.scalar.activation(xs[64:128, 1:S], pV[64:128, 0:S - 1], ACT.Copy).then_inc(xs_copied, 1)
                if seq(s - 1):
                    n, i = s - 1, (b - 1) % 2
                    act.wait_ge(ss_max, n + 1)
                    nc.scalar.activation(rn[i][:, :], ss[:, :], ACT.Ln, scale=2.0 ** 32).then_inc(ln_done, 1)
                    act.wait_ge(ln_done, n + 1)
                    nc.scalar.activation(rn[i][:, :], rn[i][:, :], ACT.Exp, scale=-0.5, bias=consts[:, 2:3]).then_inc(rn_done, 1)

        @block.vector
        def _(dve):
            dve.wait_ge(ph.consts_in, all_consts)
            nc.vector.tensor_tensor(tables[:, :, :], tables[:, :, :], scales[:, :, :], ALU.mult).then_inc(tabled, 1)
            dve.wait_ge(tabled, 1)
            def rotate(n, at, j, of):
                if seq(n - 1):
                    dve.wait_ge(rot_done, (n - 1) * 2 + at + 1)
                dve.wait_ge(sq_done, n * 2 + at + 1)
                of4 = of[:, :].rearrange("p (h d) -> p h d", d=WD)
                nc.vector.tensor_tensor(A[j][:, :, :], of4, tables[:, 2 * j, :].unsqueeze(1).to_broadcast([S, WH, WD]),
                                        ALU.mult).then_inc(ab_done, 1)
                for to, fr in ((h0, h1), (h1, h0)):
                    nc.vector.tensor_tensor(Bm[j][:, :, to], of4[:, :, fr],
                                            tables[:, 2 * j + 1, to].unsqueeze(1).to_broadcast([S, WH, HALF]),
                                            ALU.mult).then_inc(ab_done, 1)
                if at == 0 and seq(n - 1):
                    dve.wait_ge(ln_done, n)
                nc.vector.reduce_sum(ss[:, WH * j:WH * j + WH], sq[j][:, :, :], AX.X).then_inc(ss_done, 1)

            def normalise(n, i, j):
                dve.wait_ge(exp_done, n * WH + 4 * j + 4)
                nc.vector.reciprocal(rec[:, 4 * j:4 * j + 4], total[:, 4 * j:4 * j + 4]).then_inc(rec_done, 1)
                dve.wait_ge(rec_done, n * 2 + j + 1)
                for h in range(4 * j, 4 * j + 4):
                    nc.vector.tensor_scalar(P[i][:, h, :], P[i][:, h, :], rec[:, h:h + 1], None, ALU.mult).then_inc(p_normed, 1)

            for s, g, u, b in seq_steps(dve):
                if seq(s - 2):
                    n, i = s - 2, b % 2
                    dve.wait_ge(rot_done, n * 2 + 1)
                    dve.wait_ge(rn_done, n + 1)
                    nc.vector.tensor_tensor(rot[1][i][:, :, :], rot[1][i][:, :, :],
                                            rn[i][:, WH:2 * WH].unsqueeze(2).to_broadcast([S, WH, WD]), ALU.mult).then_inc(k_normed, 1)
                if seq(s - 6):
                    n = s - 6
                    w, at = (u, b + 2) if b < 2 else (1 - u, b - 2)
                    dve.wait_ge(f_ready, n + 1)
                    if at == 0:
                        dve.wait_ge(r_loaded[w], (g - 1 - w) * 8 + 16)
                        if there(g - 3):
                            dve.wait_ge(stored[w], (g - 1 - w) * 8)
                    nc.vector.tensor_tensor(R[w][:, at, :], pQ[:, 0:D], xr[w][:, at, :], ALU.add).then_inc(summed, 1)
                if seq(s - 3):
                    normalise(s - 3, (b + 1) % 2, 0)
                    normalise(s - 3, (b + 1) % 2, 1)
                if seq(s - 1):
                    rotate(s - 1, 0, 1, pK)
                    rotate(s - 1, 1, 0, pQ)
                    dve.wait_ge(ss_done, s * 2)
                    nc.vector.tensor_scalar(ss[:, :], ss[:, :], 1e-24, None, ALU.max).then_inc(ss_max, 1)
                if seq(s - 2):
                    n, i = s - 2, b % 2
                    for j in range(2):
                        h = slice(4 * j, 4 * j + 4)
                        dve.wait_ge(s_ready, n * 2 + j + 1)
                        nc.vector.tensor_reduce(neg_max[:, h], pS[j][:, :, :], AX.X, ALU.max, negate=True).then_inc(max_done, 1)
                        dve.wait_ge(max_done, n * 2 + j + 1)
                        nc.vector.tensor_tensor(bias[:, h], neg_max[:, h], rn[i][:, h], ALU.mult).then_inc(bias_done, 1)


HID = int(D * 4 * 2 / 3)
HCH = [(at, min(128, HID - at)) for at in range(0, HID, 128)]
NHC = len(HCH)


def phase_geglu(nc, name, x1_in, x_out, w1_in, b1_in, w2_in, b2_in, ln_g_in, ln_b_in, ident_in, shift_in, consts_in, x0_in=None):
    last_layer = x0_in is not None
    with Phase(nc, name) as ph:
        sb, ps, sem = ph.sb, ph.ps, ph.sem
        w1, w2 = sb("w1", [D, 2 * HID]), sb("w2", [128, NHC, D])
        ident, shift, consts = sb("ident", [128, 128]), sb("shift", [S, S]), sb("consts", [128, 2])
        b1, ln_g, ln_b, b2 = sb("b1", [128, 2, NHC]), sb("ln_g", [D, 1]), sb("ln_b", [D, 1]), sb("b2", [S, D])
        x1, x1b, x2 = ([sb(f"{n}{u}", [S, GB, D]) for u in range(2)] for n in ("x1", "x1b", "x2"))
        x0, xo = ([sb(f"{n}{u}", [S, GB, D]) for u in range(2)] for n in ("x0", "xo")) if last_layer else (None, None)
        n1, nT = sb("n1", [S, GB, D]), [sb(f"nT{u}", [D, GT]) for u in range(2)]
        gated, H = [sb(f"gated{c}", [128, GT]) for c in range(NHC)], [sb(f"H{c}", [128, GT]) for c in range(NHC)]
        pX, pT, pO = ps("pX", [S, GB, D]), ps("pT", [D, GT]), ps("pO", [S, GB, D])
        pA, pG = [ps(f"pA{i}", [128, GT]) for i in range(2)], [ps(f"pG{i}", [128, GT]) for i in range(2)]
        ph.consts_in = sem("consts_in")
        stored = ph.stored
        loaded, r_loaded = ([sem(f"{n}{u}") for u in range(2)] for n in ("loaded", "r_loaded"))
        x1b_done, x01_done, shifted, t_ready, t_copied, g_ready, a_ready, gelu_done, h_done, o_ready, x2_done = (
            sem(n) for n in ("x1b_done", "x01_done", "shifted", "t_ready", "t_copied", "g_ready", "a_ready", "gelu_done",
                             "h_done", "o_ready", "x2_done"))
        norm1 = Norm(ph, "norm1", consts[:, 0:1])
        norm2 = Norm(ph, "norm2", consts[:, 0:1]) if last_layer else None
        block = ph.block()
        tail = HCH[-1][1]
        body = (NHC - 1) * 128
        pairs = [(w1[:, :], w1_in), (b1[:, :, :], b1_in), (ident[:, :], ident_in), (shift[:, :], shift_in), (consts[:, :], consts_in),
                 (w2[:, 0:NHC - 1, :], w2_in[0:body, :].rearrange("(c p) d -> p c d", p=128)),
                 (w2[0:tail, NHC - 1, :], w2_in[body:HID, :]),
                 (ln_g[:, :], ln_g_in), (ln_b[:, :], ln_b_in), (b2[:, :], b2_in.partition_broadcast(S))]
        all_consts = 16 * len(pairs)

        @block.sync
        def _(sp):
            load_constants(ph, sp, pairs)
            for g, u in groups(sp):
                if there(g - 2):
                    sp.wait_ge(shifted, g - 1)
                    sp.nop(nofuse=True)
                    sp.wait_ge(x1b_done, (g - 1) * GB)
                sp.dma_start(x1[u][:, :, :], x1_in[g, :, :, :]).then_inc(loaded[u], 16)
                if last_layer:
                    if there(g - 2):
                        sp.wait_ge(x01_done, (g - 1) * GB)
                    sp.dma_start(x0[u][:, :, :], x0_in[g, :, :, :]).then_inc(r_loaded[u], 16)

        @block.gpsimd
        def _(pool):
            pool.wait_ge(ph.consts_in, all_consts)
            for g, u in steps(pool):
                if has(g):
                    pool.wait_ge(loaded[u], (g - u) * 8 + 16)
                    if there(g - 2):
                        pool.wait_ge(x2_done, g - 1)
                    for b in range(GB):
                        nc.gpsimd.tensor_tensor(x1b[u][:, b, :], x1[u][:, b, :], b2[:, :], ALU.add).then_inc(x1b_done, 1)
                    if last_layer:
                        pool.wait_ge(r_loaded[u], (g - u) * 8 + 16)
                        for b in range(GB):
                            pool.wait_ge(x1b_done, g * GB + b + 1)
                            nc.gpsimd.tensor_tensor(x1b[u][:, b, :], x1b[u][:, b, :], x0[u][:, b, :], ALU.add)\
                                .then_inc(x01_done, 1)
                if there(g - 2):
                    if last_layer:
                        pool.wait_ge(norm2.normed, (g - 1) * GB)
                        pool.dma_start(x_out[g - 2, :, :, :], xo[u][:, :, :]).then_inc(stored[u], 16)
                    else:
                        pool.wait_ge(x2_done, g - 1)
                        pool.dma_start(x_out[g - 2, :, :, :], x2[u][:, :, :]).then_inc(stored[u], 16)
            for u in range(2):
                pool.wait_ge(stored[u], 16 * (NG // 2))

        @block.tensor
        def _(pe):
            pe.wait_ge(ph.consts_in, all_consts)
            for g, u in steps(pe):
                if has(g):
                    pe.wait_ge(loaded[u], (g - u) * 8 + 16)
                    if there(g - 1):
                        pe.wait_ge(norm1.normed, g * GB)
                    nc.tensor.matmul(pX[:, :, 0:64], ident[:, :], x1[u][:, :, 0:64], start=True, stop=True)
                    nc.tensor.matmul(pX[:, :, 64:128], shift[:, :], x1[u][:, :, 64:128], start=True, stop=True).then_inc(shifted, 1)
                if there(g - 1) and has(g - 1):
                    pe.wait_ge(t_copied, g)
                    for c, (at, n) in enumerate(HCH):
                        k, i = (g - 1) * NHC + c, ((1 - u) * NHC + c) % 2
                        if there(k - 2):
                            pe.wait_ge(gelu_done, k - 1)
                        nc.tensor.matmul(pG[i][0:n, :], w1[:, HID + at:HID + at + n], nT[1 - u][:, :],
                                         start=True, stop=True).then_inc(g_ready, 1)
                        if there(k - 2):
                            pe.wait_ge(h_done, k - 1)
                        nc.tensor.matmul(pA[i][0:n, :], w1[:, at:at + n], nT[1 - u][:, :],
                                         start=True, stop=True).then_inc(a_ready, 1)
                if there(g - 1) and has(g - 1):
                    pe.wait_ge(h_done, g * NHC)
                    if there(g - 2):
                        pe.wait_ge(x2_done, g - 1)
                    for b in range(GB):
                        for c, (at, n) in enumerate(HCH):
                            last = nc.tensor.matmul(pO[:, b, :], H[c][0:n, b * S:(b + 1) * S], w2[0:n, c, :],
                                                    start=(c == 0), stop=(c == NHC - 1))
                    last.then_inc(o_ready, 1)
                if has(g):
                    if there(g - 1):
                        pe.wait_ge(t_copied, g)
                    for b in range(GB):
                        pe.wait_ge(norm1.normed, g * GB + b + 1)
                        last = nc.tensor.transpose(pT[:, b * S:(b + 1) * S], n1[:, b, :], ident[:, :])
                    last.then_inc(t_ready, 1)

        @block.scalar
        def _(act):
            act.wait_ge(ph.consts_in, all_consts)
            for g, u in steps(act):
                if there(g - 1) and has(g - 1):
                    for c, (at, n) in enumerate(HCH):
                        k, i = (g - 1) * NHC + c, ((1 - u) * NHC + c) % 2
                        act.wait_ge(g_ready, k + 1)
                        if there(g - 2):
                            act.wait_ge(h_done, (g - 2) * NHC + c + 1)
                        nc.scalar.activation(gated[c][0:n, :], pG[i][0:n, :], ACT.Gelu, bias=b1[0:n, 1, c:c + 1]).then_inc(gelu_done, 1)
                nc.scalar.preload_act_table_set(LN_EXP)
                if has(g):
                    norm1.act_rstd(nc, act, g)
                if there(g - 2) and last_layer:
                    norm2.act_rstd(nc, act, g - 2)
                if has(g):
                    act.wait_ge(t_ready, g + 1)
                    if there(g - 2):
                        act.wait_ge(a_ready, (g - 1) * NHC)
                    nc.scalar.activation(nT[u][:, :], pT[:, :], ACT.Identity, scale=ln_g[:, 0:1],
                                         bias=ln_b[:, 0:1]).then_inc(t_copied, 1)

        @block.vector
        def _(dve):
            dve.wait_ge(ph.consts_in, all_consts)
            for g, u in steps(dve):
                if has(g):
                    dve.wait_ge(shifted, g + 1)
                    norm1.dve_stats(nc, dve, g, pX)
                if there(g - 2) and last_layer:
                    norm2.dve_stats(nc, dve, g - 2, x2[u])
                if there(g - 1) and has(g - 1):
                    for c, (at, n) in enumerate(HCH):
                        k, i = (g - 1) * NHC + c, ((1 - u) * NHC + c) % 2
                        dve.wait_ge(a_ready, k + 1)
                        dve.wait_ge(gelu_done, k + 1)
                        if c == 0 and there(g - 2):
                            dve.wait_ge(o_ready, g - 1)
                        nc.vector.scalar_tensor_tensor(out=H[c][0:n, :], in0=pA[i][0:n, :], scalar=b1[0:n, 0, c:c + 1],
                                                       in1=gated[c][0:n, :], op0=ALU.add, op1=ALU.mult).then_inc(h_done, 1)
                if has(g):
                    if there(g - 1):
                        dve.wait_ge(t_ready, g)
                    norm1.dve_scale(nc, dve, g, n1, pX)
                if there(g - 2) and last_layer:
                    if there(g - 4):
                        dve.wait_ge(stored[u], (g - 2 - u) * 8)
                    norm2.dve_scale(nc, dve, g - 2, xo[u], x2[u])
                if there(g - 1) and has(g - 1):
                    w = 1 - u
                    dve.wait_ge(o_ready, g)
                    dve.wait_ge(x01_done if last_layer else x1b_done, g * GB)
                    if there(g - 3):
                        if last_layer:
                            dve.wait_ge(norm2.normed, (g - 2) * GB)
                        else:
                            dve.wait_ge(stored[w], (g - 1 - w) * 8)
                    nc.vector.tensor_tensor(x2[w][:, :, :], pO[:, :, :], x1b[w][:, :, :], ALU.add).then_inc(x2_done, 1)
                    if last_layer:
                        dve.wait_ge(x2_done, g)


LAYERS = 2



def build(nc, t, out):
    scratch = [nc.dram_tensor(f"tokens_{i}", (NG, S, GB, D), F32, kind="Internal").ap() for i in range(3)]
    a, b, c = scratch
    ident, mask, consts = t["ident"], t["head_mask"], t["consts"]
    phase_recurrence(nc, t["x"], a, t["L0_attn_W_gates"], t["L0_attn_W_out"], ident, consts[:, 0:2])
    phase_cross(nc, "cross0", a, b, t["ctx"], t["L0_xattn_Wq"], t["L0_xattn_Wk"], t["L0_xattn_Wv"], t["L0_xattn_Wout"],
                ident, mask, consts[:, 0:2], bout_in=t["L0_xattn_bout"])
    phase_experts(nc, b, a, t["gate_W"], t["w1_experts"], t["w3_experts"], t["w2_experts"], ident, t["iota"], consts[:, 0:2])
    phase_attention(nc, a, b, t["L1_attn_Wq"], t["L1_attn_Wk"], t["L1_attn_Wv"], t["L1_attn_Wout"], ident, consts[:, 0:2])
    phase_cross(nc, "cross1", b, c, t["ctx"], t["L1_xattn_Wq"], t["L1_xattn_Wk"], t["L1_xattn_Wv"], t["L1_xattn_Wo"],
                ident, mask, consts[:, 0:2], bias_in=t["bias"])
    phase_feedforward(nc, b, c, a, t["L1_xattn_W1"], t["L1_xattn_b1"], t["L1_xattn_W2"], t["L1_xattn_b2"],
                      t["L1_xattn_g1"], t["L1_xattn_be1"], t["L1_xattn_g2"], t["L1_xattn_be2"], ident, consts[:, 0:2])
    source = a
    for l in range(LAYERS):
        last = l == LAYERS - 1
        phase_window(nc, f"window{l}", source, c, t["L1_ffn_wqkv"][l], t["L1_ffn_wo"][l], t["rotary"], t["L1_ffn_q_scale"][l],
                     t["L1_ffn_k_scale"][l], ident, t["window_mask"], consts)
        phase_geglu(nc, f"geglu{l}", c, out if last else b, t["L1_ffn_w1"][l], t["L1_ffn_b1"][l], t["L1_ffn_w2"][l],
                    t["L1_ffn_b2"][l], t["L1_ffn_ln_g"][l], t["L1_ffn_ln_b"][l], ident, t["shift"], consts[:, 0:2],
                    x0_in=a if last else None)
        source = b


def to_groups(x):
    return x.reshape(NG, GB, S, D).transpose(0, 2, 1, 3)


def rotary_tables():
    half = np.arange(0, 64, 2, dtype=np.float32)
    inv = (1.0 / 10000.0 ** (half / 64)).astype(np.float32)
    pos = np.arange(S, dtype=np.float32)
    freqs = pos[:, None] * inv[None]
    freqs = np.concatenate([freqs, freqs], -1)
    base = ((half + 0.4 * 64) / (1.4 * 64)).astype(np.float32)
    power = (pos - S // 2) / np.float32(32)
    scale = (base[None] ** power[:, None]).astype(np.float32)
    scale = np.concatenate([scale, scale], -1)
    cos, sin = np.cos(freqs), np.sin(freqs)
    sign = np.where(np.arange(64) < 32, -1, 1).astype(np.float32)
    return np.stack([8 * cos * scale, 8 * sign * sin * scale, cos / scale, sign * sin / scale], 1).astype(np.float32)


def lay_out(i):
    per_head = np.arange(D)[:, None] // (D // HEADS16) == np.arange(HEADS16)[None]
    q, k = np.arange(S)[:, None], np.arange(S)[None]
    wkv, wqkv = i["L0_xattn_Wkv"], i["L1_attn_W_qkv"]

    def rows_in_chunks(w):
        return w.reshape(-1, 128, w.shape[-1]).transpose(1, 0, 2)

    def up(routed, shared):
        shared = shared.transpose(1, 0, 2).reshape(1, D, -1)
        return np.concatenate([routed, shared]).transpose(1, 0, 2)

    t = {
        "x": to_groups(i["x"]),
        "ctx": i["ctx_1024"].reshape(NG, GB * S2, D).transpose(0, 2, 1),
        "bias": i["fside_Bx16xSxS2_0"].transpose(0, 2, 1, 3).reshape(NG, GB, S, HEADS16, S2),
        "ident": np.eye(128, dtype=np.float32),
        "head_mask": per_head.astype(np.float32),
        "consts": np.tile(np.array([[EPS, 2.0, 16 * math.log(2.0), 0.0]], np.float32), (128, 1)),
        "iota": np.tile(np.arange(8, dtype=np.float32), (128, 1)),
        "shift": np.eye(S, k=1, dtype=np.float32),
        "window_mask": np.where((k <= q) & (q <= k + 64), 0, -1e30).astype(np.float32),
        "rotary": rotary_tables(),
        "L0_attn_W_gates": i["L0_attn_W_fwd"].T,
        "L0_attn_W_out": rows_in_chunks(i["L0_attn_W_out"].T),
        "L0_xattn_Wq": i["L0_xattn_Wq"].T, "L0_xattn_Wk": wkv[:D].T, "L0_xattn_Wv": wkv[D:].T,
        "L0_xattn_Wout": i["L0_xattn_Wout"].T, "L0_xattn_bout": i["L0_xattn_bout"],
        "gate_W": i["L0_ffn_gate_W"].T,
        "w1_experts": up(i["L0_ffn_w1_e"], i["L0_ffn_w1_s"]),
        "w3_experts": up(i["L0_ffn_w3_e"], i["L0_ffn_w3_s"]),
        "w2_experts": np.concatenate([i["L0_ffn_w2_e"], i["L0_ffn_w2_s"].reshape(1, -1, D)])
                        .reshape(9, -1, 128, D).transpose(2, 0, 1, 3),
        "L1_attn_Wq": wqkv[0::3].T, "L1_attn_Wk": wqkv[1::3].T, "L1_attn_Wv": wqkv[2::3].T,
        "L1_attn_Wout": i["L1_attn_W_out"].T,
        "L1_xattn_Wq": i["L1_xattn_Wq"].T, "L1_xattn_Wk": i["L1_xattn_Wk"].T,
        "L1_xattn_Wv": i["L1_xattn_Wv"].T, "L1_xattn_Wo": i["L1_xattn_Wo"].T,
        "L1_xattn_W1": i["L1_xattn_W1"].T, "L1_xattn_b1": i["L1_xattn_b1"].reshape(-1, 128).T,
        "L1_xattn_W2": rows_in_chunks(i["L1_xattn_W2"].T), "L1_xattn_b2": i["L1_xattn_b2"],
        "L1_xattn_g1": i["L1_xattn_g1"].reshape(D, 1), "L1_xattn_be1": i["L1_xattn_be1"].reshape(D, 1),
        "L1_xattn_g2": i["L1_xattn_g2"], "L1_xattn_be2": i["L1_xattn_be2"],
        "L1_ffn_wqkv": i["L1_ffn_wqkv"],
        "L1_ffn_wo": i["L1_ffn_wo"].reshape(LAYERS, -1, 128, D).transpose(0, 2, 1, 3),
        "L1_ffn_q_scale": i["L1_ffn_q_scale"], "L1_ffn_k_scale": i["L1_ffn_k_scale"],
        "L1_ffn_ln_g": i["L1_ffn_ln_g"].reshape(LAYERS, D, 1), "L1_ffn_ln_b": i["L1_ffn_ln_b"].reshape(LAYERS, D, 1),
        "L1_ffn_w1": i["L1_ffn_w1"], "L1_ffn_w2": i["L1_ffn_w2"], "L1_ffn_b2": i["L1_ffn_b2"],
        "L1_ffn_b1": np.pad(i["L1_ffn_b1"].reshape(LAYERS, 2, HID), ((0, 0), (0, 0), (0, NHC * 128 - HID)))
                       .reshape(LAYERS, 2, NHC, 128).transpose(0, 3, 1, 2),
    }
    return t


def kernel(**inputs):
    import concourse.bacc as bacc
    from concourse.bass_utils import run_bass_kernel_spmd

    nc = bacc.Bacc("TRN2", target_bir_lowering=False, num_devices=1)
    arrays, aps = {}, {}
    for name, a in lay_out({k: np.asarray(v) for k, v in inputs.items()}).items():
        arrays[f"in_{name}"] = np.ascontiguousarray(a)
        aps[name] = nc.dram_tensor(f"in_{name}", a.shape, mybir.dt.from_np(a.dtype), kind="ExternalInput").ap()
    out = nc.dram_tensor("out_x", (NG, S, GB, D), F32, kind="ExternalOutput").ap()
    build(nc, aps, out)
    r = run_bass_kernel_spmd(nc, [arrays], core_ids=[0])
    return r.results[0]["out_x"].reshape(NG, S, GB, D).transpose(0, 2, 1, 3).reshape(B, S, D)
```

```python
import math
import numpy as np
from contextlib import ExitStack

import concourse.bass as bass
from concourse import mybir

B, S, D = 64, 128, 128
GB = 4
NG = B // GB
GT = GB * S
S2 = 77
HEADS16 = 16
EPS = 1e-5
LN_EXP = "natural_log_exp_and_others"

F32 = mybir.dt.float32
BF16 = mybir.dt.bfloat16
ALU = mybir.AluOpType
ACT = mybir.ActivationFunctionType
AX = mybir.AxisListType


def groups(eng, peeled=4):
    for g in range(peeled):
        yield g, g % 2
    with eng.Fori(peeled // 2, NG // 2) as pair:
        yield pair * 2, 0
        yield pair * 2 + 1, 1


def there(n):
    return not isinstance(n, int) or n >= 0


def has(g):
    return not isinstance(g, int) or g < NG


def steps(eng, peeled=4):
    yield from groups(eng, peeled)
    yield NG, 0
    yield NG + 1, 1


def had(g, depth):
    return not isinstance(g, int) or g >= depth


class Phase:

    def __init__(self, nc, name):
        self.nc, self.name, self.stack, self.sems = nc, name, ExitStack(), []

    def __enter__(self):
        self.stack.__enter__()
        self.stored = [self.sem(f"stored{u}") for u in range(2)]
        self.pool_loaded = [self.sem(f"pool_loaded{u}") for u in range(2)]
        return self

    def __exit__(self, *e):
        self.stack.__exit__(*e)
        self.nc.clear_and_free_semaphores(self.sems)
        self.nc.all_engine_barrier()

    def sb(self, name, shape, dt=F32):
        return self.stack.enter_context(self.nc.sbuf_tensor(f"{self.name}_{name}", shape, dt))

    def ps(self, name, shape, dt=F32):
        return self.stack.enter_context(self.nc.psum_tensor(f"{self.name}_{name}", shape, dt))

    def sem(self, name):
        self.sems.append(self.nc.alloc_semaphore(f"{self.name}_{name}"))
        return self.sems[-1]

    def block(self):
        return self.stack.enter_context(self.nc.Block())


class Norm:

    def __init__(self, ph, name, eps, count=GB):
        self.count, self.eps = count, eps
        self.stats = ph.sb(f"{name}_stats", [S, count, 6])
        self.mv = ph.sb(f"{name}_mv", [S, count, 2])
        self.rstd = ph.sb(f"{name}_rstd", [S, count])
        self.summed = ph.sem(f"{name}_summed")
        self.stats_done = ph.sem(f"{name}_stats_done")
        self.mv_done = ph.sem(f"{name}_mv_done")
        self.ln_done = ph.sem(f"{name}_ln_done")
        self.rstd_done = ph.sem(f"{name}_rstd_done")
        self.normed = ph.sem(f"{name}_normed")

    def dve_stats(self, nc, dve, g, x):
        n = self.count
        for b in range(n):
            nc.vector.bn_stats(self.stats[:, b, :], x[:, b, :]).then_inc(self.stats_done, 1)
        dve.wait_ge(self.stats_done, (g + 1) * n)
        dve.nop(nofuse=True)
        for b in range(n):
            nc.vector.bn_aggr(self.mv[:, b, :], self.stats[:, b, :]).then_inc(self.mv_done, 1)

    def act_rstd(self, nc, act, g):
        act.wait_ge(self.mv_done, (g + 1) * self.count)
        nc.scalar.activation(self.rstd[:, :], self.mv[:, :, 1], ACT.Ln, bias=self.eps).then_inc(self.ln_done, 1)
        act.wait_ge(self.ln_done, g + 1)
        nc.scalar.activation(self.rstd[:, :], self.rstd[:, :], ACT.Exp, scale=-0.5).then_inc(self.rstd_done, 1)

    def dve_scale(self, nc, dve, g, out, x):
        dve.wait_ge(self.rstd_done, g + 1)
        for b in range(self.count):
            nc.vector.tensor_scalar(out[:, b, :], x[:, b, :], self.mv[:, b, 0:1], self.rstd[:, b:b + 1],
                                    ALU.subtract, ALU.mult).then_inc(self.normed, 1)


def load_constants(ph, eng, pairs):
    for to, of in pairs:
        eng.dma_start(to, of).then_inc(ph.consts_in, 16)
    return 16 * len(pairs)


def phase_recurrence(nc, x_in, x_out, w_gates, w_out, ident_in, eps_in):
    HID = 256
    NC = HID // 128
    with Phase(nc, "rec") as ph:
        sb, ps, sem = ph.sb, ph.ps, ph.sem
        w1 = sb("w1", [D, 3 * HID])
        w2 = sb("w2", [128, NC, D])
        ident = sb("ident", [128, 128])
        eps = sb("eps", [128, 2])
        x = [sb(f"x{u}", [S, GB, D]) for u in range(2)]
        xr = [sb(f"xr{u}", [S, GB, D]) for u in range(2)]
        xT = [sb(f"xT{u}", [D, GT]) for u in range(2)]
        E = [sb(f"E{c}", [128, 3, GT]) for c in range(NC)]
        LI = [sb(f"LI{c}", [128, GT]) for c in range(NC)]
        LH = [sb(f"LH{c}", [128, GT]) for c in range(NC)]
        T = [sb(f"T{c}", [128, GT]) for c in range(NC)]
        Dd = [sb(f"D{c}", [128, GT]) for c in range(NC)]
        Fg = [sb(f"F{c}", [128, GT]) for c in range(NC)]
        G = [sb(f"G{c}", [128, GT]) for c in range(NC)]
        hs = [[sb(f"hs{u}{c}", [128, GT]) for c in range(NC)] for u in range(2)]
        R = sb("R", [S, GB, D])
        xo = [sb(f"xo{u}", [S, GB, D]) for u in range(2)]
        pT = ps("pT", [128, GT])
        pg = [[ps(f"pg{c}{j}", [128, GT]) for j in range(3)] for c in range(NC)]
        pO = ps("pO", [S, GB, D])
        ph.consts_in = sem("consts_in")
        x_in_sem = [sem(f"x_loaded{u}") for u in range(2)]
        r_loaded = [sem(f"r_loaded{u}") for u in range(2)]
        xT_ready, xT_copied, gate_ready, exp_done = sem("xT_ready"), sem("xT_copied"), sem("gate_ready"), sem("exp_done")
        clamped, lnI_done, lnH_done, t_done, lnT_done, sig_done = (
            sem("clamped"), sem("lnI_done"), sem("lnH_done"), sem("t_done"), sem("lnT_done"), sem("sig_done"))
        d_done, f_done, g_done, v_done, scanned, out_ready = (
            sem("d_done"), sem("f_done"), sem("g_done"), sem("v_done"), sem("scanned"), sem("out_ready"))
        stored = ph.stored
        norm = Norm(ph, "norm", eps[:, 0:1])
        block = ph.block()
        NCONST = 4

        @block.sync
        def _(sp):
            load_constants(ph, sp, [(w1[:, :], w_gates), (w2[:, :, :], w_out), (ident[:, :], ident_in), (eps[:, :], eps_in)])
            for g, u in groups(sp):
                if had(g, 2):
                    sp.wait_ge(xT_ready, g - 1)
                sp.dma_start(x[u][:, :, :], x_in[g, :, :, :]).then_inc(x_in_sem[u], 16)
                if had(g, 2):
                    sp.wait_ge(norm.summed, g - 1)
                sp.dma_start(xr[u][:, :, :], x_in[g, :, :, :]).then_inc(r_loaded[u], 16)

        @block.gpsimd
        def _(pool):
            for g, u in groups(pool):
                pool.wait_ge(norm.normed, g * GB + GB)
                pool.dma_start(x_out[g, :, :, :], xo[u][:, :, :]).then_inc(stored[u], 16)
            for u in range(2):
                pool.wait_ge(stored[u], 16 * (NG // 2))

        @block.tensor
        def _(pe):
            pe.wait_ge(ph.consts_in, 16 * NCONST)

            def gates(g, u):
                pe.wait_ge(x_in_sem[u], (g - u) * 8 + 16)
                if had(g, 1):
                    pe.wait_ge(xT_copied, g)
                for b in range(GB):
                    last = nc.tensor.transpose(pT[:, b * S:(b + 1) * S], x[u][:, b, :], ident[:, :])
                last.then_inc(xT_ready, 1)
                pe.wait_ge(xT_copied, g + 1)
                for c in range(NC):
                    for j in range(3):
                        if had(g, 1):
                            pe.wait_ge(exp_done, (g - 1) * (3 * NC) + 3 * c + j + 1)
                            if j == 2:
                                pe.wait_ge(g_done, (g - 1) * NC + c + 1)
                        nc.tensor.matmul(pg[c][j][:, :], w1[:, j * HID + c * 128:j * HID + (c + 1) * 128],
                                         xT[u][:, :], start=True, stop=True).then_inc(gate_ready, 1)

            def project(g, u):
                if had(g, 1):
                    pe.wait_ge(norm.summed, g)
                pe.wait_ge(scanned, (g + 1) * (NC * GB))
                for b in range(GB):
                    for c in range(NC):
                        last = nc.tensor.matmul(pO[:, b, :], hs[u][c][:, b * S:(b + 1) * S], w2[:, c, :],
                                                start=(c == 0), stop=(c == NC - 1))
                last.then_inc(out_ready, 1)

            for g, u in steps(pe):
                if has(g):
                    gates(g, u)
                if there(g - 1) and has(g - 1):
                    project(g - 1, 1 - u)

        @block.scalar
        def _(act):
            nc.scalar.preload_act_table_set(LN_EXP)
            act.wait_ge(ph.consts_in, 16 * NCONST)

            def copy_xT(g, u):
                act.wait_ge(xT_ready, g + 1)
                if had(g, 2):
                    act.wait_ge(gate_ready, (g - 1) * (3 * NC))
                nc.scalar.activation(xT[u][:, :], pT[:, :], ACT.Copy).then_inc(xT_copied, 1)

            def exponentials(g):
                for c in range(NC):
                    if had(g, 1):
                        act.wait_ge(t_done, (g - 1) * NC + c + 1)
                        act.wait_ge(lnH_done, (g - 1) * NC + c + 1)
                    for j in range(3):
                        act.wait_ge(gate_ready, g * (3 * NC) + 3 * c + j + 1)
                        nc.scalar.activation(E[c][:, j, :], pg[c][j][:, :], ACT.Exp, scale=-1.0).then_inc(exp_done, 1)

            def sigmoids(g):
                for c in range(NC):
                    act.wait_ge(clamped, g * NC + c + 1)
                    if had(g, 1):
                        act.wait_ge(d_done, (g - 1) * NC + c + 1)
                        act.wait_ge(g_done, (g - 1) * NC + c + 1)
                    nc.scalar.activation(LH[c][:, :], E[c][:, 2, :], ACT.Ln, bias=1.0).then_inc(lnH_done, 1)
                    nc.scalar.activation(LI[c][:, :], E[c][:, 1, :], ACT.Ln, bias=1.0).then_inc(lnI_done, 1)
                    act.wait_ge(lnH_done, g * NC + c + 1)
                    nc.scalar.activation(LH[c][:, :], LH[c][:, :], ACT.Exp, scale=-1.0).then_inc(sig_done, 1)

            def ln_total(g):
                for c in range(NC):
                    act.wait_ge(t_done, g * NC + c + 1)
                    nc.scalar.activation(T[c][:, :], T[c][:, :], ACT.Ln, bias=eps[:, 1:2]).then_inc(lnT_done, 1)

            def forget(g):
                for c in range(NC):
                    act.wait_ge(d_done, g * NC + c + 1)
                    if had(g, 1):
                        act.wait_ge(scanned, (g - 1) * (NC * GB) + GB * (c + 1))
                    nc.scalar.activation(Fg[c][:, :], Dd[c][:, :], ACT.Exp).then_inc(f_done, 1)

            for g, u in steps(act):
                if has(g):
                    copy_xT(g, u)
                if there(g - 1) and has(g - 1):
                    ln_total(g - 1)
                    forget(g - 1)
                if has(g):
                    exponentials(g)
                if has(g):
                    sigmoids(g)
                if there(g - 2):
                    norm.act_rstd(nc, act, g - 2)

        @block.vector
        def _(dve):
            def clamp_and_total(g):
                for c in range(NC):
                    dve.wait_ge(exp_done, g * (3 * NC) + 3 * (c + 1))
                    nc.vector.tensor_scalar(E[c][:, :, :], E[c][:, :, :], 2.0 ** 62, None, ALU.min).then_inc(clamped, 1)
                for c in range(NC):
                    dve.wait_ge(clamped, g * NC + c + 1)
                    if had(g, 1):
                        dve.wait_ge(d_done, (g - 1) * NC + c + 1)
                    nc.vector.tensor_tensor(T[c][:, :], E[c][:, 0, :], E[c][:, 1, :], ALU.add).then_inc(t_done, 1)

            def g_of_hidden(g):
                for c in range(NC):
                    dve.wait_ge(sig_done, g * NC + c + 1)
                    if had(g, 1):
                        dve.wait_ge(scanned, (g - 1) * (NC * GB) + GB * (c + 1))
                    nc.vector.scalar_tensor_tensor(out=G[c][:, :], in0=pg[c][2][:, :], scalar=0.5, in1=LH[c][:, :],
                                                   op0=ALU.add, op1=ALU.max).then_inc(g_done, 1)

            def log_forget(g):
                for c in range(NC):
                    dve.wait_ge(lnT_done, g * NC + c + 1)
                    dve.wait_ge(lnI_done, g * NC + c + 1)
                    if had(g, 1):
                        dve.wait_ge(f_done, (g - 1) * NC + c + 1)
                    nc.vector.tensor_tensor(Dd[c][:, :], LI[c][:, :], T[c][:, :], ALU.subtract).then_inc(d_done, 1)

            def scan(g, u):
                for c in range(NC):
                    dve.wait_ge(f_done, g * NC + c + 1)
                    dve.wait_ge(g_done, g * NC + c + 1)
                    nc.vector.scalar_tensor_tensor(out=G[c][:, :], in0=Fg[c][:, :], scalar=1.0, in1=G[c][:, :],
                                                   op0=ALU.subtract, op1=ALU.mult).then_inc(v_done, 1)
                for c in range(NC):
                    dve.wait_ge(v_done, g * NC + c + 1)
                    if had(g, 2):
                        dve.wait_ge(out_ready, g - 1)
                    for b in range(GB):
                        t = slice(b * S, (b + 1) * S)
                        nc.vector.tensor_tensor_scan(hs[u][c][:, t], Fg[c][:, t], G[c][:, t], 0.0,
                                                     ALU.mult, ALU.subtract).then_inc(scanned, 1)

            def residual(g, u):
                dve.wait_ge(out_ready, g + 1)
                if had(g, 1):
                    dve.wait_ge(norm.normed, g * GB)
                dve.wait_ge(r_loaded[u], (g - u) * 8 + 16)
                nc.vector.tensor_tensor(R[:, :, :], pO[:, :, :], xr[u][:, :, :], ALU.add).then_inc(norm.summed, 1)
                dve.wait_ge(norm.summed, g + 1)
                norm.dve_stats(nc, dve, g, R)

            def normalise(g, u):
                if had(g, 2):
                    dve.wait_ge(stored[u], (g - u) * 8)
                norm.dve_scale(nc, dve, g, xo[u], R)

            for g, u in steps(dve):
                if there(g - 1) and has(g - 1):
                    log_forget(g - 1)
                    scan(g - 1, 1 - u)
                if has(g):
                    clamp_and_total(g)
                if has(g):
                    g_of_hidden(g)
                if there(g - 2):
                    normalise(g - 2, u)
                if there(g - 1) and has(g - 1):
                    residual(g - 1, 1 - u)


QG = 4
QH = 4
DH = 8
K4 = GB * S2
SCALE8 = DH ** -0.5
NSEQ = NG * GB
NUNIT = NSEQ * QG
F16 = mybir.dt.float16


def phase_cross(nc, name, x_in, x_out, ctx_in, w_q, w_k, w_v, w_out, ident_in, mask_in, consts_in, bout_in=None, bias_in=None):
    biased = bias_in is not None
    with Phase(nc, name) as ph:
        sb, ps, sem = ph.sb, ph.ps, ph.sem
        wq, wk, wv, wo = (sb(n, [D, D]) for n in ("wq", "wk", "wv", "wo"))
        ident = sb("ident", [128, 128])
        identh = sb("identh", [128, 128], F16)
        mask = sb("mask", [128, HEADS16])
        consts = sb("consts", [128, 4])
        x, xr, R = ([sb(f"{n}{u}", [S, GB, D]) for u in range(2)] for n in ("x", "xr", "R"))
        ctxT = [sb(f"ctxT{u}", [D, K4]) for u in range(2)]
        xT = sb("xT", [D, GT])
        qT = [sb(f"qT{u}", [D, GT]) for u in range(2)]
        kT = sb("kT", [D, K4])
        Km = [sb(f"Km{u}", [D, HEADS16, K4]) for u in range(2)]
        V = [[sb(f"V{half}{u}", [S2, GB * HEADS16, DH + 1], F16) for half in ("high", "low")] for u in range(2)]
        top = [sb(f"top{i}", [S, QH]) for i in range(2)]
        shifted = [sb(f"shifted{i}", [S, QH, S2]) for i in range(2)]
        P, halves = [sb(f"P{q}", [S, QH, S2]) for q in range(QG)], [sb(f"halves{q}", [S, 2, QH, S2], F16) for q in range(QG)]
        PT = [sb(f"PT{i}", [S2, 2, QH, S], F16) for i in range(2)]
        rec = sb("rec", [S, HEADS16])
        on = sb("on", [S, HEADS16, DH])
        oT = sb("oT", [D, S])
        if biased:
            bias = [sb(f"bias{i}", [S, HEADS16, S2]) for i in range(2)]
        else:
            bout = sb("bout", [S, D])
            xo = [sb(f"xo{u}", [S, GB, D]) for u in range(2)]
        pS = [ps(f"pS{i}", [S, QH, S2]) for i in range(2)]
        pT = [ps(f"pT{i}", [S2, 2, QH, S], F16) for i in range(2)]
        pO = [ps(f"pO{i}", [S, HEADS16, DH + 1]) for i in range(2)]
        pPrep = ps("pPrep", [128, 512])
        pF = ps("pF", [128, 2, 128])

        ph.consts_in = sem("consts_in")
        loaded, r_loaded = ([sem(f"{n}{u}") for u in range(2)] for n in ("loaded", "r_loaded"))
        bias_loaded = [sem(f"bias_loaded{i}") for i in range(2)]
        set_up, xr_done = sem("set_up"), sem("xr_done")
        prep_ready = sem("prep_ready")
        prep_copied = sem("prep_copied")
        v_low, km_done = sem("v_low"), sem("km_done")
        s_ready, added, top_done, sub_done, exp_done, high_done, low_done = (
            sem(n) for n in ("s_ready", "added", "top_done", "sub_done", "exp_done", "high_done", "low_done"))
        pt_ready, pt_copied, pv_done, rec_done, on_done, ot_ready, ot_copied, f_ready = (
            sem(n) for n in ("pt_ready", "pt_copied", "pv_done", "rec_done", "on_done", "ot_ready", "ot_copied", "f_ready"))
        stored = ph.stored
        norm = Norm(ph, "norm", consts[:, 0:1])
        block = ph.block()
        const_pairs = [(wq[:, :], w_q), (wk[:, :], w_k), (wv[:, :], w_v), (wo[:, :], w_out),
                       (ident[:, :], ident_in), (mask[:, :], mask_in), (consts[:, :], consts_in)]
        if not biased:
            const_pairs.append((bout[:, :], bout_in.partition_broadcast(S)))
        all_consts = 16 * len(const_pairs)
        scores_read = added if biased else sub_done

        def unit(n):
            return not isinstance(n, int) or 0 <= n < NUNIT

        def seq(m):
            return not isinstance(m, int) or 0 <= m < NSEQ

        def back(G, w, b, depth):
            return (G, w, b - depth) if b >= depth else (G - 1, 1 - w, b - depth + GB)

        @block.sync
        def _(sp):
            load_constants(ph, sp, const_pairs)
            for g, u in steps(sp):
                if has(g):
                    if there(g - 2):
                        sp.wait_ge(prep_ready, (g - 1) * 4)
                        sp.nop(nofuse=True)
                    sp.dma_start(x[u][:, :, :], x_in[g, :, :, :]).then_inc(loaded[u], 16)
                    sp.dma_start(ctxT[u][:, :], ctx_in[g, :, :]).then_inc(loaded[u], 16)
                if biased and there(g - 1) and has(g - 1):
                    for b in range(GB):
                        n = (g - 1) * GB + b
                        if there(n - 2):
                            sp.wait_ge(added, (n - 1) * QG)
                            sp.nop(nofuse=True)
                        sp.dma_start(bias[b % 2][:, :, :], bias_in[g - 1, b, :, :, :]).then_inc(bias_loaded[b % 2], 16)
                if has(g):
                    if there(g - 2):
                        sp.wait_ge(norm.summed, (g - 1) * GB)
                        sp.nop(nofuse=True)
                    sp.dma_start(xr[u][:, :, :], x_in[g, :, :, :]).then_inc(r_loaded[u], 16)

        @block.gpsimd
        def _(pool):
            for u in range(2):
                nc.gpsimd.memset(V[u][0][:, :, DH:DH + 1], 1.0).then_inc(set_up, 1)
                nc.gpsimd.memset(V[u][1][:, :, DH:DH + 1], 0.0).then_inc(set_up, 1)
            pool.wait_ge(ph.consts_in, all_consts)
            nc.gpsimd.tensor_copy(identh[:, :], ident[:, :]).then_inc(set_up, 1)

            for g, u in steps(pool):
                G, w = g - 1, 1 - u
                for b in range(GB):
                    for q in range(QG):
                        n = (G * GB + b) * QG + q
                        i = (q - 2) % QG
                        if there(G) and unit(n - 2):
                            pool.wait_ge(high_done, n - 1)
                            nc.gpsimd.tensor_tensor(halves[i][:, 1, :, :], P[i][:, :, :], halves[i][:, 0, :, :],
                                                    ALU.subtract).then_inc(low_done, 1)
                    if b == 0 and there(G) and has(G) and not biased:
                        pool.wait_ge(r_loaded[w], (G - w) * 8 + 16)
                        for i in range(GB):
                            nc.gpsimd.tensor_tensor(xr[w][:, i, :], xr[w][:, i, :], bout[:, :], ALU.add).then_inc(xr_done, 1)
                if there(G - 1):
                    pool.wait_ge(norm.summed if biased else norm.normed, G * GB)
                    pool.dma_start(x_out[G - 1, :, :, :], (R if biased else xo)[u][:, :, :]).then_inc(stored[u], 16)
            for u in range(2):
                pool.wait_ge(stored[u], 16 * (NG // 2))

        @block.tensor
        def _(pe):
            pe.wait_ge(ph.consts_in, all_consts)
            pe.wait_ge(set_up, 5)

            def prepare(g, u, b):
                if b == 0:
                    pe.wait_ge(loaded[u], (g - u) * 16 + 32)
                    if there(g - 1):
                        pe.wait_ge(v_low, g)
                else:
                    pe.wait_ge(prep_copied, g * 4 + b)
                if b == 0:
                    for i in range(GB):
                        last = nc.tensor.transpose(pPrep[:, i * S:(i + 1) * S], x[u][:, i, :], ident[:, :])
                elif b == 1:
                    last = nc.tensor.matmul(pPrep[:, 0:K4], wk[:, :], ctxT[u][:, :], start=True, stop=True)
                elif b == 2:
                    last = nc.tensor.matmul(pPrep[:, :], wq[:, :], xT[:, :], start=True, stop=True)
                else:
                    for i in range(GB):
                        last = nc.tensor.matmul(pPrep[0:S2, i * D:(i + 1) * D], ctxT[u][:, i * S2:(i + 1) * S2],
                                                wv[:, :], start=True, stop=True)
                last.then_inc(prep_ready, 1)

            def scores(n, G, w, b, q):
                if b == 0:
                    if q == 0:
                        pe.wait_ge(prep_copied, G * 4 + 3)
                    pe.wait_ge(km_done, G * HEADS16 + QH * (q + 1))
                if there(n - 2):
                    pe.wait_ge(scores_read, n - 1)
                nc.tensor.matmul(pS[q % 2][:, :, :], qT[w][:, b * S:(b + 1) * S],
                                 Km[w][:, QH * q:QH * q + QH, b * S2:(b + 1) * S2], start=True, stop=True).then_inc(s_ready, 1)

            def turn_probabilities(k, q):
                i = q % 2
                pe.wait_ge(low_done, k + 1)
                if there(k - 2):
                    pe.wait_ge(pt_copied, k - 1)
                for half in range(2):
                    for h in range(QH):
                        last = nc.tensor.transpose(pT[i][:, half, h, :], halves[q][:, half, h, :], identh[:, :])
                last.then_inc(pt_ready, 1)

            def values(k, G, w, b, q):
                i, m = q % 2, G * GB + b
                pe.wait_ge(pt_copied, k + 1)
                if q == 0:
                    if b == 0:
                        pe.wait_ge(v_low, G + 1)
                    if there(m - 2):
                        pe.wait_ge(on_done, m - 1)
                for h in range(QH):
                    out, at = pO[b % 2][:, QH * q + h, :], b * HEADS16 + QH * q + h
                    nc.tensor.matmul(out, PT[i][:, 0, h, :], V[w][0][:, at, :], start=True, stop=False)
                    nc.tensor.matmul(out, PT[i][:, 0, h, :], V[w][1][:, at, :], start=False, stop=False)
                    last = nc.tensor.matmul(out, PT[i][:, 1, h, :], V[w][0][:, at, :], start=False, stop=True)
                last.then_inc(pv_done, 1)

            for g, u in steps(pe):
                G, w = g - 1, 1 - u
                for b in range(GB):
                    m = G * GB + b
                    if has(g):
                        prepare(g, u, b)
                    if not there(G):
                        if b == GB - 1:
                            scores(0, g, u, 0, 0)
                        continue
                    for q in range(QG):
                        n = m * QG + q
                        if has(G) and (q < QG - 1 or b < GB - 1):
                            scores(n + 1, G, w, b + (q + 1) // QG, (q + 1) % QG)
                        elif has(G) and has(g):
                            scores(n + 1, g, u, 0, 0)
                        if unit(n - 3):
                            turn_probabilities(n - 3, (q - 3) % QG)
                        if unit(n - 4):
                            values(n - 4, *back(G, w, b, 1), q)
                        if q == 2 and seq(m - 2):
                            pe.wait_ge(on_done, m - 1)
                            if seq(m - 3):
                                pe.wait_ge(norm.summed, m - 2)
                            nc.tensor.transpose(pF[:, 0, :], on[:, :, :].rearrange("p h d -> p (h d)"), ident[:, :])\
                                .then_inc(ot_ready, 1)
                        if q == 0 and seq(m - 3):
                            pe.wait_ge(ot_copied, m - 2)
                            nc.tensor.matmul(pF[:, 1, :], oT[:, :], wo[:, :], start=True, stop=True).then_inc(f_ready, 1)

        @block.scalar
        def _(act):
            nc.scalar.preload_act_table_set(LN_EXP)
            act.wait_ge(ph.consts_in, all_consts)
            act.wait_ge(set_up, 5)

            def copy_prep(g, u, b):
                act.wait_ge(prep_ready, g * 4 + b + 1)
                if b == 0:
                    if there(g - 1):
                        act.wait_ge(prep_ready, g * 4)
                    ins = nc.scalar.activation(xT[:, :], pPrep[:, :], ACT.Copy)
                elif b == 1:
                    if there(g - 1):
                        act.wait_ge(km_done, g * HEADS16)
                    ins = nc.scalar.activation(kT[:, :], pPrep[:, 0:K4], ACT.Copy)
                elif b == 2:
                    if there(g - 2):
                        act.wait_ge(s_ready, (g - 1) * GB * QG)
                    ins = nc.scalar.activation(qT[u][:, :], pPrep[:, :], ACT.Copy, scale=SCALE8)
                else:
                    if there(g - 2):
                        act.wait_ge(pv_done, (g - 1) * GB * QG)
                    ins = nc.scalar.activation(V[u][0][:, :, 0:DH], pPrep[0:S2, :].rearrange("p (h d) -> p h d", d=DH), ACT.Copy)
                ins.then_inc(prep_copied, 1)

            for g, u in steps(act):
                G, w = g - 1, 1 - u
                for b in range(GB):
                    m = G * GB + b
                    if has(g):
                        copy_prep(g, u, b)
                    if not there(G):
                        continue
                    for q in range(QG):
                        n, i = m * QG + q, q % 2
                        if unit(n - 3):
                            act.wait_ge(pt_ready, n - 2)
                            if there(n - 5):
                                act.wait_ge(pv_done, n - 4)
                            nc.scalar.activation(PT[1 - i][:, :, :, :], pT[1 - i][:, :, :, :], ACT.Copy).then_inc(pt_copied, 1)
                        if has(G):
                            act.wait_ge(sub_done, n + 1)
                            if there(n - QG):
                                act.wait_ge(low_done, n - QG + 1)
                            nc.scalar.activation(P[q][:, :, :], shifted[i][:, :, :], ACT.Exp, bias=consts[:, 3:4]).then_inc(exp_done, 1)
                        if q == 3 and seq(m - 2):
                            act.wait_ge(ot_ready, m - 1)
                            if seq(m - 3):
                                act.wait_ge(f_ready, m - 2)
                            nc.scalar.activation(oT[:, :], pF[:, 0, :], ACT.Copy).then_inc(ot_copied, 1)
                        if b == 3 and q == 0 and there(G - 1) and not biased:
                            norm.act_rstd(nc, act, G - 1)

        @block.vector
        def _(dve):
            dve.wait_ge(ph.consts_in, all_consts)

            def masked(g, u, b, q):
                if b == 2 and q == 0:
                    dve.wait_ge(prep_copied, g * 4 + 2)
                    if there(g - 2):
                        dve.wait_ge(s_ready, (g - 1) * GB * QG)
                for h in range(HEADS16 // 2 * (b - 2) + 2 * q, HEADS16 // 2 * (b - 2) + 2 * q + 2):
                    nc.vector.tensor_scalar(Km[u][:, h, :], kT[:, :], mask[:, h:h + 1], None, ALU.mult).then_inc(km_done, 1)

            def add_bias(n, m, b, q):
                i = q % 2
                dve.wait_ge(s_ready, n + 1)
                if there(n - 2):
                    dve.wait_ge(exp_done, n - 1)
                if q == 0:
                    dve.wait_ge(bias_loaded[b % 2], (m - b % 2) * 8 + 16)
                nc.vector.tensor_tensor(shifted[i][:, :, :], pS[i][:, :, :], bias[b % 2][:, QH * q:QH * q + QH, :],
                                        ALU.add).then_inc(added, 1)

            def maximum(n, i):
                if biased:
                    dve.wait_ge(added, n + 1)
                else:
                    dve.wait_ge(s_ready, n + 1)
                nc.vector.tensor_reduce(top[i][:, :], (shifted if biased else pS)[i][:, :, :], AX.X, ALU.max).then_inc(top_done, 1)

            def subtract_maximum(n, i):
                dve.wait_ge(top_done, n + 1)
                if there(n - 2):
                    dve.wait_ge(exp_done, n - 1)
                nc.vector.tensor_tensor(shifted[i][:, :, :], (shifted if biased else pS)[i][:, :, :],
                                        top[i][:, :].unsqueeze(2).to_broadcast([S, QH, S2]), ALU.subtract).then_inc(sub_done, 1)

            def high_half(k, i):
                dve.wait_ge(exp_done, k + 1)
                if there(k - QG):
                    dve.wait_ge(pt_ready, k - QG + 1)
                nc.vector.tensor_copy(halves[i][:, 0, :, :], P[i][:, :, :]).then_inc(high_done, 1)

            def divide(m, b):
                dve.wait_ge(pv_done, (m + 1) * QG)
                nc.vector.reciprocal(rec[:, :], pO[b % 2][:, :, DH]).then_inc(rec_done, 1)
                dve.wait_ge(rec_done, m + 1)
                if there(m - 1):
                    dve.wait_ge(ot_ready, m)
                nc.vector.tensor_tensor(on[:, :, :], pO[b % 2][:, :, 0:DH], rec[:, :].unsqueeze(2).to_broadcast([S, HEADS16, DH]),
                                        ALU.mult).then_inc(on_done, 1)

            def residual(m, G, w, b):
                dve.wait_ge(f_ready, m + 1)
                if b == 0:
                    if biased:
                        dve.wait_ge(r_loaded[w], (G - w) * 8 + 16)
                    else:
                        dve.wait_ge(xr_done, (G + 1) * GB)
                    if there(G - 2):
                        dve.wait_ge(*((stored[w], (G - w) * 8) if biased else (norm.normed, (G - 1) * GB)))
                nc.vector.tensor_tensor(R[w][:, b, :], pF[:, 1, :], xr[w][:, b, :], ALU.add).then_inc(norm.summed, 1)

            for g, u in steps(dve):
                G, w = g - 1, 1 - u
                for b in range(GB):
                    m = G * GB + b
                    for q in range(QG):
                        n = m * QG + q
                        scored, halved = there(G) and has(G), there(G) and unit(n - 2)
                        if scored and biased:
                            add_bias(n, m, b, q)
                        if halved and biased:
                            high_half(n - 2, (q - 2) % QG)
                        if scored:
                            maximum(n, q % 2)
                        if halved and not biased:
                            high_half(n - 2, (q - 2) % QG)
                        if has(g) and b >= 2:
                            masked(g, u, b, q)
                        if scored:
                            subtract_maximum(n, q % 2)
                        if there(G) and q == 0 and seq(m - 2):
                            divide(m - 2, b)
                        if there(G) and q == 1 and seq(m - 3):
                            residual(m - 3, *back(G, w, b, 3))
                        if there(G - 1) and not biased:
                            if b == 2 and q == 2:
                                dve.wait_ge(norm.summed, G * GB)
                                norm.dve_stats(nc, dve, G - 1, R[u])
                            if b == 3 and q == 2:
                                if there(G - 3):
                                    dve.wait_ge(stored[u], (G - 1 - u) * 8)
                                norm.dve_scale(nc, dve, G - 1, xo[u], R[u])
                    if has(g) and b == 3:
                        dve.wait_ge(prep_copied, g * 4 + 4)
                        nc.vector.tensor_tensor(V[u][1][:, :, 0:DH], pPrep[0:S2, :].rearrange("p (h d) -> p h d", d=DH),
                                                V[u][0][:, :, 0:DH], ALU.subtract).then_inc(v_low, 1)


E_R = 8
NE = E_R + 1
FC = 4
TOP = 2
ALPHA = 0.5
W_SCALE = 64.0


def phase_experts(nc, x_in, x_out, gate_in, w1_in, w3_in, w2_in, ident_in, iota_in, consts_in):
    with Phase(nc, "moe") as ph:
        sb, ps, sem = ph.sb, ph.ps, ph.sem
        w1, w3 = sb("w1", [D, NE, FC * 128]), sb("w3", [D, NE, FC * 128])
        w2 = sb("w2", [128, NE, FC, D])
        w1s, w3s = ([sb(f"{n}{half}", [D, NE, FC * 128], F16) for half in ("high", "low")] for n in ("w1", "w3"))
        wg = sb("wg", [D, E_R])
        ident, iota, consts = sb("ident", [128, 128]), sb("iota", [S, E_R]), sb("consts", [128, 2])
        x = [sb(f"x{u}", [S, GB, D]) for u in range(2)]
        xT = [sb(f"xT{u}", [D, GT]) for u in range(2)]
        xs = [[sb(f"x{half}{u}", [D, GT], F16) for half in ("high", "low")] for u in range(2)]
        logits, top = sb("logits", [S, GB, E_R]), sb("top", [S, GB, 8])
        where = sb("where", [S, GB, 8], mybir.dt.uint32)
        wheref, shifted, probs = sb("wheref", [S, GB, TOP]), sb("shifted", [S, GB, E_R]), sb("probs", [S, GB, E_R])
        chosen = [sb(f"chosen{k}", [S, GB, E_R]) for k in range(TOP)]
        total, scale = sb("total", [S, GB]), sb("scale", [S, GB])
        gate = [sb(f"gate{u}", [S, GB, E_R]) for u in range(2)]
        act_g = [sb(f"act_g{i}", [128, GT]) for i in range(2)]
        H = [[sb(f"H{i}{c}", [128, GT]) for c in range(FC)] for i in range(2)]
        acc = [sb(f"acc{u}", [S, GB, D]) for u in range(2)]
        xo = [sb(f"xo{u}", [S, GB, D]) for u in range(2)]
        pG = [ps(f"pG{i}", [128, GT]) for i in range(2)]
        pU = [ps(f"pU{i}", [128, GT]) for i in range(2)]
        pO = [ps(f"pO{i}", [S, GB, D]) for i in range(2)]
        pX, pL = ps("pX", [128, GT]), ps("pL", [S, GB, E_R])
        ph.consts_in = sem("consts_in")
        loaded = [sem(f"loaded{u}") for u in range(2)]
        xt_ready, xt_copied, logits_ready, probs_exp = sem("xt_ready"), sem("xt_copied"), sem("logits_ready"), sem("probs_exp")
        w_high, w_low, x_high, x_low = sem("w_high"), sem("w_low"), sem("x_high"), sem("x_low")
        small = sem("small")
        w_loaded = [sem(f"w_loaded{e}") for e in range(NE)]
        g_ready, u_ready, silu_done, h_done, o_ready, acc_done = (
            sem("g_ready"), sem("u_ready"), sem("silu_done"), sem("h_done"), sem("o_ready"), sem("acc_done"))
        stored = ph.stored
        norm = Norm(ph, "norm", consts[:, 0:1])
        block = ph.block()
        pairs = [(ident[:, :], ident_in), (wg[:, :], gate_in), (iota[:, :], iota_in), (consts[:, :], consts_in)]
        all_consts = 16 * len(pairs)
        SMALL = 2 * GB + 10

        @block.sync
        def _(sp):
            load_constants(ph, sp, pairs)
            for g, u in groups(sp):
                if there(g - 2):
                    sp.wait_ge(acc_done, (g - 2) * (NE * GB) + GB)
                sp.dma_start(x[u][:, :, :], x_in[g, :, :, :]).then_inc(loaded[u], 16)
                if isinstance(g, int) and g == 1:
                    for e in range(NE):
                        for w, w_in in ((w1, w1_in), (w3, w3_in), (w2, w2_in)):
                            sp.dma_start(w[:, e], w_in[:, e]).then_inc(w_loaded[e], 16)

        @block.gpsimd
        def _(pool):
            for g, u in steps(pool):
                if has(g):
                    pool.wait_ge(xt_copied, g + 1)
                    if there(g - 2):
                        pool.wait_ge(u_ready, (g - 1) * (NE * FC))
                    nc.gpsimd.tensor_tensor(xs[u][1][:, :], xT[u][:, :], xs[u][0][:, :], ALU.subtract).then_inc(x_low, 1)
                if there(g - 2):
                    pool.wait_ge(norm.normed, (g - 1) * GB)
                    pool.dma_start(x_out[g - 2, :, :, :], xo[u][:, :, :]).then_inc(stored[u], 16)
            for u in range(2):
                pool.wait_ge(stored[u], 16 * (NG // 2))

        @block.tensor
        def _(pe):
            pe.wait_ge(ph.consts_in, all_consts)

            def turn_x(g, u):
                pe.wait_ge(loaded[u], (g - u) * 8 + 16)
                if there(g - 1):
                    pe.wait_ge(xt_copied, g)
                for b in range(GB):
                    last = nc.tensor.transpose(pX[:, b * S:(b + 1) * S], x[u][:, b, :], ident[:, :])
                last.then_inc(xt_ready, 1)

            def gate_logits(g, u):
                pe.wait_ge(xt_copied, g + 1)
                if there(g - 1):
                    pe.wait_ge(small, (g - 1) * SMALL + 1)
                for b in range(GB):
                    last = nc.tensor.matmul(pL[:, b, :], xT[u][:, b * S:(b + 1) * S], wg[:, :], start=True, stop=True)
                last.then_inc(logits_ready, 1)

            def three_products(out, halves, e, w, c):
                (high, low), (x_h, x_l), cols = halves, xs[w], slice(c * 128, (c + 1) * 128)
                nc.tensor.matmul(out[:, :], high[:, e, cols], x_h[:, :], start=True, stop=False)
                nc.tensor.matmul(out[:, :], high[:, e, cols], x_l[:, :], start=False, stop=False)
                return nc.tensor.matmul(out[:, :], low[:, e, cols], x_h[:, :], start=False, stop=True)

            def up(m, e, w, c):
                k = m * FC + c
                if c == 0 and isinstance(m, int) and m < NE:
                    pe.wait_ge(w_loaded[e], 16 * 3)
                    pe.wait_ge(w_low, 2 * (e + 1))
                if c == 0 and e == 0:
                    pe.wait_ge(x_low, m // NE + 1)
                if there(k - 2):
                    pe.wait_ge(silu_done, k - 1)
                three_products(pG[c % 2], w1s, e, w, c).then_inc(g_ready, 1)
                if there(k - 2):
                    pe.wait_ge(h_done, k - 1)
                three_products(pU[c % 2], w3s, e, w, c).then_inc(u_ready, 1)

            def down(m, e, i):
                pe.wait_ge(h_done, m * FC + FC)
                if there(m - 2):
                    pe.wait_ge(acc_done, (m - 1) * GB)
                for b in range(GB):
                    for c in range(FC):
                        last = nc.tensor.matmul(pO[i][:, b, :], H[i][c][:, b * S:(b + 1) * S], w2[:, e, c, :],
                                                start=(c == 0), stop=(c == FC - 1))
                last.then_inc(o_ready, 1)

            for g, u in steps(pe):
                G, w = g - 1, 1 - u
                if has(g):
                    turn_x(g, u)
                if there(G) and has(G):
                    for e in range(NE):
                        m, i = G * NE + e, (w * NE + e) % 2
                        for c in range(FC):
                            up(m, e, w, c)
                            if c == 0 and there(m - 1):
                                down(m - 1, (e - 1) % NE, 1 - i)
                        if e == 0 and has(g):
                            gate_logits(g, u)
                elif has(g):
                    gate_logits(g, u)
                else:
                    down(NG * NE - 1, NE - 1, (NG * NE - 1) % 2)

        @block.scalar
        def _(act):
            act.wait_ge(ph.consts_in, all_consts)

            def high_weights(e):
                act.wait_ge(w_loaded[e], 16 * 3)
                for w_of, halves in ((w1, w1s), (w3, w3s)):
                    nc.scalar.activation(halves[0][:, e, :], w_of[:, e, :], ACT.Copy, scale=W_SCALE).then_inc(w_high, 1)

            def copy_xt(g, u):
                act.wait_ge(xt_ready, g + 1)
                if there(g - 2):
                    act.wait_ge(u_ready, (g - 1) * (NE * FC))
                nc.scalar.activation(xs[u][0][:, :], pX[:, :], ACT.Copy).then_inc(x_high, 1)
                nc.scalar.activation(xT[u][:, :], pX[:, :], ACT.Copy).then_inc(xt_copied, 1)

            def exp_logits(g):
                act.wait_ge(small, g * SMALL + 2 * GB + 2)
                nc.scalar.activation(probs[:, :, :], shifted[:, :, :], ACT.Exp).then_inc(probs_exp, 1)

            for g, u in steps(act):
                G, w = g - 1, 1 - u
                if has(g):
                    copy_xt(g, u)
                if isinstance(g, int) and g == 0:
                    high_weights(0)
                if there(G) and has(G):
                    for e in range(NE):
                        m, i = G * NE + e, (w * NE + e) % 2
                        for c in range(FC):
                            k = m * FC + c
                            act.wait_ge(g_ready, k + 1)
                            if there(k - 2):
                                act.wait_ge(h_done, k - 1)
                            nc.scalar.activation(act_g[c % 2][:, :], pG[c % 2][:, :], ACT.Silu,
                                                 scale=1.0 / W_SCALE).then_inc(silu_done, 1)
                            if c == 1 and isinstance(G, int) and G == 0 and e < NE - 1:
                                high_weights(e + 1)
                        if e == 1:
                            nc.scalar.preload_act_table_set(LN_EXP)
                            if there(G - 1):
                                norm.act_rstd(nc, act, G - 1)
                            if has(g):
                                exp_logits(g)
                else:
                    nc.scalar.preload_act_table_set(LN_EXP)
                    if has(g):
                        exp_logits(g)
                    else:
                        norm.act_rstd(nc, act, NG - 1)

        @block.vector
        def _(dve):
            dve.wait_ge(ph.consts_in, all_consts)
            def low_weights(e):
                dve.wait_ge(w_loaded[e], 16 * 3)
                for j, (w_of, halves) in enumerate(((w1, w1s), (w3, w3s))):
                    dve.wait_ge(w_high, 2 * e + j + 1)
                    nc.vector.scalar_tensor_tensor(out=halves[1][:, e, :], in0=w_of[:, e, :], scalar=W_SCALE,
                                                   in1=halves[0][:, e, :], op0=ALU.mult, op1=ALU.subtract).then_inc(w_low, 1)

            def bc(a):
                return a.unsqueeze(2).to_broadcast([S, GB, E_R])

            def gates_before_exp(g):
                at = g * SMALL
                dve.wait_ge(logits_ready, g + 1)
                nc.vector.tensor_copy(logits[:, :, :], pL[:, :, :]).then_inc(small, 1)
                dve.wait_ge(small, at + 1)
                dve.nop(nofuse=True)
                for b in range(GB):
                    nc.vector.max(top[:, b, :], logits[:, b, :]).then_inc(small, 1)
                dve.wait_ge(small, at + 1 + GB)
                dve.nop(nofuse=True)
                for b in range(GB):
                    nc.vector.max_index(where[:, b, :], top[:, b, :], logits[:, b, :]).then_inc(small, 1)
                if there(g - 1):
                    dve.wait_ge(probs_exp, g)
                nc.vector.tensor_tensor(shifted[:, :, :], logits[:, :, :], bc(top[:, :, 0]), ALU.subtract).then_inc(small, 1)

            def gates_after_exp(g, u):
                at = g * SMALL + 2 * GB + 2
                dve.wait_ge(small, at - 1)
                nc.vector.tensor_copy(wheref[:, :, :], where[:, :, 0:TOP]).then_inc(small, 1)
                dve.wait_ge(probs_exp, g + 1)
                nc.vector.reduce_sum(total[:, :], probs[:, :, :], AX.X).then_inc(small, 1)
                dve.wait_ge(small, at + 1)
                iota_b = iota[:, :].unsqueeze(1).to_broadcast([S, GB, E_R])
                for k in range(TOP):
                    nc.vector.tensor_tensor(chosen[k][:, :, :], iota_b, bc(wheref[:, :, k]), ALU.is_equal).then_inc(small, 1)
                dve.wait_ge(small, at + 2)
                nc.vector.reciprocal(scale[:, :], total[:, :]).then_inc(small, 1)
                dve.wait_ge(small, at + 4)
                nc.vector.tensor_tensor(chosen[0][:, :, :], chosen[0][:, :, :], chosen[1][:, :, :], ALU.add).then_inc(small, 1)
                dve.wait_ge(small, at + 5)
                nc.vector.scalar_tensor_tensor(out=shifted[:, :, :], in0=probs[:, :, :], scalar=1.0 - ALPHA,
                                               in1=bc(scale[:, :]), op0=ALU.mult, op1=ALU.mult).then_inc(small, 1)
                dve.wait_ge(small, at + 7)
                if there(g - 2):
                    dve.wait_ge(acc_done, (g - 1) * (NE * GB) - GB)
                nc.vector.tensor_tensor(gate[u][:, :, :], shifted[:, :, :], chosen[0][:, :, :], ALU.mult).then_inc(small, 1)

            def add_expert(G, w, m, e, i):
                dve.wait_ge(o_ready, m + 1)
                for b in range(GB):
                    if e == 0:
                        if b == 0:
                            dve.wait_ge(small, (G + 1) * SMALL)
                            if there(G - 2):
                                dve.wait_ge(norm.normed, (G - 1) * GB)
                    else:
                        dve.wait_ge(acc_done, m * GB - GB + b + 1)
                    by = ALPHA / E_R if e == NE - 1 else gate[w][:, b, e:e + 1]
                    nc.vector.scalar_tensor_tensor(out=acc[w][:, b, :], in0=pO[i][:, b, :], scalar=by,
                                                   in1=(x if e == 0 else acc)[w][:, b, :],
                                                   op0=ALU.mult, op1=ALU.add).then_inc(acc_done, 1)

            for g, u in steps(dve):
                G, w = g - 1, 1 - u
                if there(G) and has(G):
                    for e in range(NE):
                        m, i = G * NE + e, (w * NE + e) % 2
                        for c in range(FC):
                            k = m * FC + c
                            dve.wait_ge(u_ready, k + 1)
                            dve.wait_ge(silu_done, k + 1)
                            if c == 0 and there(m - 2):
                                dve.wait_ge(o_ready, m - 1)
                            nc.vector.scalar_tensor_tensor(out=H[i][c][:, :], in0=pU[c % 2][:, :], scalar=1.0 / W_SCALE,
                                                           in1=act_g[c % 2][:, :], op0=ALU.mult, op1=ALU.mult).then_inc(h_done, 1)
                            if c == 1 and isinstance(G, int) and G == 0 and e < NE - 1:
                                low_weights(e + 1)
                            if c == 0 and there(m - 1):
                                if e:
                                    add_expert(G, w, m - 1, e - 1, 1 - i)
                                else:
                                    add_expert(G - 1, u, m - 1, NE - 1, 1 - i)
                        if e == 0 and there(G - 1):
                            dve.wait_ge(acc_done, m * GB)
                            norm.dve_stats(nc, dve, G - 1, acc[u])
                        if e == 1 and has(g):
                            gates_before_exp(g)
                        if e == 2 and there(G - 1):
                            if there(G - 3):
                                dve.wait_ge(stored[u], (G - 1 - u) * 8)
                            norm.dve_scale(nc, dve, G - 1, xo[u], acc[u])
                        if e == 2 and has(g):
                            gates_after_exp(g, u)
                elif has(g):
                    low_weights(0)
                    gates_before_exp(g)
                    gates_after_exp(g, u)
                else:
                    m = NG * NE - 1
                    add_expert(NG - 1, u, m, NE - 1, m % 2)
                    dve.wait_ge(acc_done, NG * NE * GB)
                    norm.dve_stats(nc, dve, NG - 1, acc[u])
                    dve.wait_ge(stored[u], (NG - 1 - u) * 8)
                    norm.dve_scale(nc, dve, NG - 1, xo[u], acc[u])


def phase_attention(nc, x_in, x_out, w_q, w_k, w_v, w_out, ident_in, consts_in):
    with Phase(nc, "att") as ph:
        sb, ps, sem = ph.sb, ph.ps, ph.sem
        wq, wk, wv, wo = (sb(n, [D, D]) for n in ("wq", "wk", "wv", "wo"))
        ident, consts = sb("ident", [128, 128]), sb("consts", [128, 2])
        x = [sb(f"x{u}", [S, GB, D]) for u in range(2)]
        xr = [sb(f"xr{u}", [S, GB, D]) for u in range(2)]
        xT = sb("xT", [D, GT])
        qT = [sb(f"qT{u}", [D, GT]) for u in range(2)]
        kT = [sb(f"kT{u}", [D, GT]) for u in range(2)]
        V = [sb(f"V{u}", [S, GB, D]) for u in range(2)]
        neg_max, P, PT, cT = sb("neg_max", [S, GB]), sb("P", [S, GB, S]), sb("PT", [S, GT]), sb("cT", [D, GT])
        total, rec = [sb(f"total{u}", [S, GB]) for u in range(2)], sb("rec", [S, GB])
        R, xo = sb("R", [S, GB, D]), [sb(f"xo{u}", [S, GB, D]) for u in range(2)]
        pX, pQ, pK, pP, pC = (ps(n, [128, GT]) for n in ("pX", "pQ", "pK", "pP", "pC"))
        pV, pS, pO = (ps(n, [S, GB, D]) for n in ("pV", "pS", "pO"))
        ph.consts_in = sem("consts_in")
        loaded, r_loaded = [sem(f"loaded{u}") for u in range(2)], ph.pool_loaded
        stored = ph.stored
        x_ready, x_copied, q_ready, q_copied, k_ready, k_copied, v_ready, v_copied = (
            sem(n) for n in ("x_ready", "x_copied", "q_ready", "q_copied", "k_ready", "k_copied", "v_ready", "v_copied"))
        s_ready, max_done, exp_done, p_ready, p_copied, c_ready, c_copied, o_ready, rec_done = (
            sem(n) for n in ("s_ready", "max_done", "exp_done", "p_ready", "p_copied", "c_ready", "c_copied", "o_ready",
                             "rec_done"))
        norm = Norm(ph, "norm", consts[:, 0:1])
        block = ph.block()
        pairs = [(wq[:, :], w_q), (wk[:, :], w_k), (wv[:, :], w_v), (wo[:, :], w_out), (ident[:, :], ident_in),
                 (consts[:, :], consts_in)]
        all_consts = 16 * len(pairs)

        @block.sync
        def _(sp):
            load_constants(ph, sp, pairs)
            for g, u in groups(sp):
                if there(g - 2):
                    sp.wait_ge(x_ready, g - 1)
                sp.dma_start(x[u][:, :, :], x_in[g, :, :, :]).then_inc(loaded[u], 16)

        @block.gpsimd
        def _(pool):
            for g, u in steps(pool):
                if there(g - 2):
                    pool.wait_ge(norm.normed, (g - 1) * GB)
                    pool.dma_start(x_out[g - 2, :, :, :], xo[u][:, :, :]).then_inc(stored[u], 16)
                if has(g):
                    pool.dma_start(xr[u][:, :, :], x_in[g, :, :, :]).then_inc(r_loaded[u], 16)
            for u in range(2):
                pool.wait_ge(stored[u], 16 * (NG // 2))

        @block.tensor
        def _(pe):
            pe.wait_ge(ph.consts_in, all_consts)
            for g, u in steps(pe):
                w = 1 - u
                if has(g):
                    pe.wait_ge(loaded[u], (g - u) * 8 + 16)
                    if there(g - 1):
                        pe.wait_ge(x_copied, g)
                    for b in range(GB):
                        last = nc.tensor.transpose(pX[:, b * S:(b + 1) * S], x[u][:, b, :], ident[:, :])
                    last.then_inc(x_ready, 1)
                if there(g - 1) and has(g - 1):
                    pe.wait_ge(q_copied, g)
                    pe.wait_ge(k_copied, g)
                    if there(g - 2):
                        pe.wait_ge(exp_done, (g - 1) * GB)
                    for b in range(GB):
                        t = slice(b * S, (b + 1) * S)
                        last = nc.tensor.matmul(pS[:, b, :], qT[w][:, t], kT[w][:, t], start=True, stop=True)
                    last.then_inc(s_ready, 1)
                if has(g):
                    pe.wait_ge(x_copied, g + 1)
                    if there(g - 1):
                        pe.wait_ge(q_copied, g)
                    nc.tensor.matmul(pQ[:, :], wq[:, :], xT[:, :], start=True, stop=True).then_inc(q_ready, 1)
                    if there(g - 1):
                        pe.wait_ge(k_copied, g)
                    nc.tensor.matmul(pK[:, :], wk[:, :], xT[:, :], start=True, stop=True).then_inc(k_ready, 1)
                    if there(g - 1):
                        pe.wait_ge(v_copied, g)
                    for b in range(GB):
                        last = nc.tensor.matmul(pV[:, b, :], xT[:, b * S:(b + 1) * S], wv[:, :], start=True, stop=True)
                    last.then_inc(v_ready, 1)
                if there(g - 1) and has(g - 1):
                    if there(g - 2):
                        pe.wait_ge(p_copied, g - 1)
                    for b in range(GB):
                        pe.wait_ge(exp_done, (g - 1) * GB + b + 1)
                        last = nc.tensor.transpose(pP[:, b * S:(b + 1) * S], P[:, b, :], ident[:, :])
                    last.then_inc(p_ready, 1)
                if there(g - 2):
                    pe.wait_ge(c_copied, g - 1)
                    if there(g - 3):
                        pe.wait_ge(norm.summed, (g - 2) * GB)
                    for b in range(GB):
                        last = nc.tensor.matmul(pO[:, b, :], cT[:, b * S:(b + 1) * S], wo[:, :], start=True, stop=True)
                    last.then_inc(o_ready, 1)
                if there(g - 1) and has(g - 1):
                    pe.wait_ge(p_copied, g)
                    pe.wait_ge(v_copied, g)
                    if there(g - 2):
                        pe.wait_ge(c_copied, g - 1)
                    for b in range(GB):
                        t = slice(b * S, (b + 1) * S)
                        last = nc.tensor.matmul(pC[:, t], V[w][:, b, :], PT[:, t], start=True, stop=True)
                    last.then_inc(c_ready, 1)

        @block.scalar
        def _(act):
            nc.scalar.preload_act_table_set(LN_EXP)
            act.wait_ge(ph.consts_in, all_consts)
            for g, u in steps(act):
                if has(g):
                    act.wait_ge(x_ready, g + 1)
                    if there(g - 1):
                        act.wait_ge(v_ready, g)
                    nc.scalar.activation(xT[:, :], pX[:, :], ACT.Copy).then_inc(x_copied, 1)
                if there(g - 1) and has(g - 1):
                    if there(g - 2):
                        act.wait_ge(p_ready, g - 1)
                    if there(g - 3):
                        act.wait_ge(rec_done, g - 2)
                    act.wait_ge(max_done, g)
                    for b in range(GB):
                        nc.scalar.activation(P[:, b, :], pS[:, b, :], ACT.Exp, bias=neg_max[:, b:b + 1],
                                             accum_out=total[1 - u][:, b:b + 1]).then_inc(exp_done, 1)
                if has(g):
                    act.wait_ge(q_ready, g + 1)
                    if there(g - 2):
                        act.wait_ge(s_ready, g - 1)
                    nc.scalar.activation(qT[u][:, :], pQ[:, :], ACT.Copy, scale=float(D) ** -0.5).then_inc(q_copied, 1)
                    act.wait_ge(k_ready, g + 1)
                    nc.scalar.activation(kT[u][:, :], pK[:, :], ACT.Copy).then_inc(k_copied, 1)
                if there(g - 1) and has(g - 1):
                    act.wait_ge(p_ready, g)
                    if there(g - 2):
                        act.wait_ge(c_ready, g - 1)
                    nc.scalar.activation(PT[:, :], pP[:, :], ACT.Copy).then_inc(p_copied, 1)
                if there(g - 2):
                    norm.act_rstd(nc, act, g - 2)

        @block.vector
        def _(dve):
            dve.wait_ge(ph.consts_in, all_consts)
            for g, u in steps(dve):
                if there(g - 1) and has(g - 1):
                    dve.wait_ge(s_ready, g)
                    if there(g - 2):
                        dve.wait_ge(exp_done, (g - 1) * GB)
                    nc.vector.tensor_reduce(neg_max[:, :], pS[:, :, :], AX.X, ALU.max, negate=True).then_inc(max_done, 1)
                if there(g - 2):
                    nc.vector.reciprocal(rec[:, :], total[u][:, :]).then_inc(rec_done, 1)
                if has(g):
                    dve.wait_ge(v_ready, g + 1)
                    if there(g - 2):
                        dve.wait_ge(c_ready, g - 1)
                    nc.vector.tensor_copy(V[u][:, :, :], pV[:, :, :]).then_inc(v_copied, 1)
                if there(g - 2):
                    dve.wait_ge(o_ready, g - 1)
                    dve.wait_ge(rec_done, g - 1)
                    dve.wait_ge(r_loaded[u], (g - 2 - u) * 8 + 16)
                    for b in range(GB):
                        nc.vector.scalar_tensor_tensor(out=R[:, b, :], in0=pO[:, b, :], scalar=rec[:, b:b + 1],
                                                       in1=xr[u][:, b, :], op0=ALU.mult, op1=ALU.add).then_inc(norm.summed, 1)
                    dve.wait_ge(norm.summed, (g - 1) * GB)
                    norm.dve_stats(nc, dve, g - 2, R)
                if there(g - 1) and has(g - 1):
                    dve.wait_ge(c_ready, g)
                    if there(g - 2):
                        dve.wait_ge(o_ready, g - 1)
                    nc.vector.tensor_copy(cT[:, :], pC[:, :]).then_inc(c_copied, 1)
                if there(g - 2):
                    if there(g - 4):
                        dve.wait_ge(stored[u], (g - 2 - u) * 8)
                    norm.dve_scale(nc, dve, g - 2, xo[u], R)


def phase_feedforward(nc, x_in, x1_in, x_out, w1_in, b1_in, w2_in, b2_in, g1_in, be1_in, g2_in, be2_in, ident_in, consts_in):
    FC1 = 4
    with Phase(nc, "ffn") as ph:
        sb, ps, sem = ph.sb, ph.ps, ph.sem
        w1, w2 = sb("w1", [D, FC1 * 128]), sb("w2", [128, FC1, D])
        ident, consts = sb("ident", [128, 128]), sb("consts", [128, 2])
        b1, g1, be1 = sb("b1", [128, FC1]), sb("g1", [D, 1]), sb("be1", [D, 1])
        b2, g2, be2 = sb("b2", [S, D]), sb("g2", [S, D]), sb("be2", [S, D])
        x1 = [sb(f"x1{u}", [S, GB, D]) for u in range(2)]
        x1b = [sb(f"x1b{u}", [S, GB, D]) for u in range(2)]
        x0 = [sb(f"x0{u}", [S, GB, D]) for u in range(2)]
        x2, y, xo = ([sb(f"{n}{u}", [S, GB, D]) for u in range(2)] for n in ("x2", "y", "xo"))
        n1, nT = sb("n1", [S, GB, D]), [sb(f"nT{u}", [D, GT]) for u in range(2)]
        H = [sb(f"H{c}", [128, GT]) for c in range(FC1)]
        pX, pH, pO = ps("pX", [D, GT]), [ps(f"pH{c}", [128, GT]) for c in range(FC1)], ps("pO", [S, GB, D])
        ph.consts_in = sem("consts_in")
        loaded, r_loaded = [sem(f"loaded{u}") for u in range(2)], [sem(f"r_loaded{u}") for u in range(2)]
        stored = ph.stored
        x1b_done, x0b_done, t_ready, t_copied, h_ready, gelu_done, o_ready, x2_done, scaled, y_done = (
            sem(n) for n in ("x1b_done", "x0b_done", "t_ready", "t_copied", "h_ready", "gelu_done", "o_ready", "x2_done",
                             "scaled", "y_done"))
        norm1, norm2, norm3 = (Norm(ph, f"norm{i}", consts[:, 0:1]) for i in (1, 2, 3))
        block = ph.block()
        pairs = [(w1[:, :], w1_in), (w2[:, :, :], w2_in), (ident[:, :], ident_in), (consts[:, :], consts_in),
                 (b1[:, :], b1_in), (g1[:, :], g1_in), (be1[:, :], be1_in), (b2[:, :], b2_in.partition_broadcast(S)),
                 (g2[:, :], g2_in.partition_broadcast(S)), (be2[:, :], be2_in.partition_broadcast(S))]
        all_consts = 16 * len(pairs)

        def steps3(eng):
            yield from steps(eng, 6)
            yield NG + 2, 0

        @block.sync
        def _(sp):
            load_constants(ph, sp, pairs)
            for g, u in steps(sp):
                if has(g):
                    if there(g - 2):
                        sp.wait_ge(norm1.normed, (g - 1) * GB)
                        sp.wait_ge(x1b_done, (g - 1) * GB)
                        sp.nop(nofuse=True)
                    sp.dma_start(x1[u][:, :, :], x1_in[g, :, :, :]).then_inc(loaded[u], 16)
                if there(g - 1) and has(g - 1):
                    if there(g - 3):
                        sp.wait_ge(y_done, g - 2)
                        sp.nop(nofuse=True)
                    sp.dma_start(x0[1 - u][:, :, :], x_in[g - 1, :, :, :]).then_inc(r_loaded[1 - u], 16)

        @block.gpsimd
        def _(pool):
            pool.wait_ge(ph.consts_in, all_consts)
            for g, u in steps3(pool):
                if has(g):
                    pool.wait_ge(loaded[u], (g - u) * 8 + 16)
                    if there(g - 2):
                        pool.wait_ge(x2_done, g - 1)
                    for b in range(GB):
                        nc.gpsimd.tensor_tensor(x1b[u][:, b, :], x1[u][:, b, :], b2[:, :], ALU.add).then_inc(x1b_done, 1)
                    pool.wait_ge(r_loaded[u], (g - u) * 8 + 16)
                    for b in range(GB):
                        nc.gpsimd.tensor_tensor(x0[u][:, b, :], x0[u][:, b, :], be2[:, :], ALU.add).then_inc(x0b_done, 1)
                if there(g - 3):
                    pool.wait_ge(norm3.normed, (g - 2) * GB)
                    pool.dma_start(x_out[g - 3, :, :, :], xo[1 - u][:, :, :]).then_inc(stored[1 - u], 16)
            for u in range(2):
                pool.wait_ge(stored[u], 16 * (NG // 2))

        @block.tensor
        def _(pe):
            pe.wait_ge(ph.consts_in, all_consts)
            for g, u in steps(pe):
                if there(g - 1) and has(g - 1):
                    pe.wait_ge(t_copied, g)
                    for c in range(FC1):
                        if there(g - 2):
                            pe.wait_ge(gelu_done, (g - 2) * FC1 + c + 1)
                        nc.tensor.matmul(pH[c][:, :], w1[:, c * 128:(c + 1) * 128], nT[1 - u][:, :],
                                         start=True, stop=True).then_inc(h_ready, 1)
                if there(g - 1) and has(g - 1):
                    pe.wait_ge(gelu_done, g * FC1)
                    if there(g - 2):
                        pe.wait_ge(x2_done, g - 1)
                    for b in range(GB):
                        for c in range(FC1):
                            last = nc.tensor.matmul(pO[:, b, :], H[c][:, b * S:(b + 1) * S], w2[:, c, :],
                                                    start=(c == 0), stop=(c == FC1 - 1))
                    last.then_inc(o_ready, 1)
                if has(g):
                    if there(g - 1):
                        pe.wait_ge(t_copied, g)
                    for b in range(GB):
                        pe.wait_ge(norm1.normed, g * GB + b + 1)
                        last = nc.tensor.transpose(pX[:, b * S:(b + 1) * S], n1[:, b, :], ident[:, :])
                    last.then_inc(t_ready, 1)

        @block.scalar
        def _(act):
            act.wait_ge(ph.consts_in, all_consts)
            for g, u in steps3(act):
                if there(g - 1) and has(g - 1):
                    for c in range(FC1):
                        act.wait_ge(h_ready, (g - 1) * FC1 + c + 1)
                        if c == 0 and there(g - 2):
                            act.wait_ge(o_ready, g - 1)
                        nc.scalar.activation(H[c][:, :], pH[c][:, :], ACT.Gelu, bias=b1[:, c:c + 1]).then_inc(gelu_done, 1)
                nc.scalar.preload_act_table_set(LN_EXP)
                if has(g):
                    norm1.act_rstd(nc, act, g)
                if there(g - 2) and has(g - 2):
                    norm2.act_rstd(nc, act, g - 2)
                if has(g):
                    act.wait_ge(t_ready, g + 1)
                    if there(g - 2):
                        act.wait_ge(h_ready, (g - 1) * FC1)
                    nc.scalar.activation(nT[u][:, :], pX[:, :], ACT.Identity, scale=g1[:, 0:1],
                                         bias=be1[:, 0:1]).then_inc(t_copied, 1)
                if there(g - 3):
                    norm3.act_rstd(nc, act, g - 3)

        @block.vector
        def _(dve):
            dve.wait_ge(ph.consts_in, all_consts)
            for g, u in steps3(dve):
                if has(g):
                    dve.wait_ge(loaded[u], (g - u) * 8 + 16)
                    norm1.dve_stats(nc, dve, g, x1[u])
                if there(g - 2) and has(g - 2):
                    norm2.dve_stats(nc, dve, g - 2, x2[u])
                if has(g):
                    if there(g - 1):
                        dve.wait_ge(t_ready, g)
                    norm1.dve_scale(nc, dve, g, n1, x1[u])
                if there(g - 3):
                    norm3.dve_stats(nc, dve, g - 3, y[1 - u])
                if there(g - 2) and has(g - 2):
                    norm2.dve_scale(nc, dve, g - 2, x2[u], x2[u])
                if there(g - 3):
                    if there(g - 5):
                        dve.wait_ge(stored[1 - u], (g - 4 + u) * 8)
                    norm3.dve_scale(nc, dve, g - 3, xo[1 - u], y[1 - u])
                if there(g - 2) and has(g - 2):
                    dve.wait_ge(norm2.normed, (g - 1) * GB)
                    nc.vector.tensor_tensor(x2[u][:, :, :], x2[u][:, :, :], g2[:, :].unsqueeze(1).to_broadcast([S, GB, D]),
                                            ALU.mult).then_inc(scaled, 1)
                if there(g - 1) and has(g - 1):
                    dve.wait_ge(o_ready, g)
                    dve.wait_ge(x1b_done, g * GB)
                    if there(g - 3):
                        dve.wait_ge(y_done, g - 2)
                    nc.vector.tensor_tensor(x2[1 - u][:, :, :], pO[:, :, :], x1b[1 - u][:, :, :], ALU.add).then_inc(x2_done, 1)
                if there(g - 2) and has(g - 2):
                    dve.wait_ge(scaled, g - 1)
                    dve.wait_ge(x0b_done, (g - 1) * GB)
                    if there(g - 4):
                        dve.wait_ge(norm3.normed, (g - 3) * GB)
                    nc.vector.tensor_tensor(y[u][:, :, :], x2[u][:, :, :], x0[u][:, :, :], ALU.add).then_inc(y_done, 1)
                if there(g - 1) and has(g - 1):
                    dve.wait_ge(x2_done, g)
                if there(g - 2) and has(g - 2):
                    dve.wait_ge(y_done, g - 1)


WH, WD = 8, 64
INNER = WH * WD
HALF = WD // 2
PAIRS = WH // 2
DRAIN = 7


def phase_window(nc, name, x_in, x_out, wqkv_in, wo_in, tables_in, q_scale_in, k_scale_in, ident_in, mask_in, consts_in):
    with Phase(nc, name) as ph:
        sb, ps, sem = ph.sb, ph.ps, ph.sem
        wqkv, wo = sb("wqkv", [D, 3 * INNER]), sb("wo", [128, PAIRS, D])
        ident, identb, maskb = sb("ident", [128, 128]), sb("identb", [128, 128], BF16), sb("maskb", [S, S], BF16)
        maskf, consts = sb("maskf", [S, S]), sb("consts", [128, 4])
        tables = sb("tables", [S, 4, WD])
        scales = sb("scales", [S, 4, WD])
        x, xr, R = ([sb(f"{n}{u}", [S, GB, D]) for u in range(2)] for n in ("x", "xr", "R"))
        xs = sb("xs", [D, S])
        sq = [sb(f"sq{i}", [S, WH, WD]) for i in range(2)]
        ss = sb("ss", [S, 2 * WH])
        rn = [sb(f"rn{i}", [S, 2 * WH]) for i in range(2)]
        A = [sb(f"A{i}", [S, WH, WD]) for i in range(2)]
        Bm = [sb(f"B{i}", [S, WH, WD]) for i in range(2)]
        rot = [[sb(f"rot{j}{i}", [S, WH, WD]) for i in range(2)] for j in range(2)]
        V = [sb(f"V{b}", [S, INNER]) for b in range(GB)]
        qT, kTm = sb("qT", [128, PAIRS, S]), sb("kTm", [128, PAIRS, 2, S])
        neg_max, bias = sb("neg_max", [S, WH]), sb("bias", [S, WH])
        P, PT = [sb(f"P{i}", [S, WH, S]) for i in range(2)], sb("PT", [S, WH, S])
        total, rec, oT = sb("total", [S, WH]), sb("rec", [S, WH]), sb("oT", [128, PAIRS, S])
        pQ, pK, pV = (ps(n, [S, 512]) for n in ("pQ", "pK", "pV"))
        pT = [ps(f"pT{i}", [128, 4, S]) for i in range(2)]
        pS = [ps(f"pS{i}", [S, 4, S]) for i in range(2)]
        pO = ps("pO", [128, PAIRS, S])
        ph.consts_in = sem("consts_in")
        stored = ph.stored
        loaded, r_loaded = ([sem(f"{n}{u}") for u in range(2)] for n in ("loaded", "r_loaded"))
        set_up, tabled, total_done = sem("set_up"), sem("tabled"), sem("total_done")
        (xt_ready, xs_copied, v_ready, k_ready, q_ready, v_copied, sq_done, ss_done, ss_max, ln_done, rn_done) = (
            sem(n) for n in ("xt_ready", "xs_copied", "v_ready", "k_ready", "q_ready", "v_copied", "sq_done", "ss_done",
                             "ss_max", "ln_done", "rn_done"))
        ab_done, rot_done, k_normed, t_ready, t_copied, s_ready, max_done, bias_done, exp_done, rec_done, p_normed = (
            sem(n) for n in ("ab_done", "rot_done", "k_normed", "t_ready", "t_copied", "s_ready", "max_done", "bias_done",
                             "exp_done", "rec_done", "p_normed"))
        pt_ready, pt_copied, pv_ready, o_copied, f_ready, summed = (
            sem(n) for n in ("pt_ready", "pt_copied", "pv_ready", "o_copied", "f_ready", "summed"))
        block = ph.block()
        h0, h1 = slice(0, HALF), slice(HALF, WD)
        pairs = [(wqkv[:, :], wqkv_in), (wo[:, :, :], wo_in), (ident[:, :], ident_in), (maskf[:, :], mask_in),
                 (consts[:, :], consts_in), (tables[:, :, :], tables_in)]
        for j, scale_in in ((0, q_scale_in), (2, k_scale_in)):
            pairs += [(scales[:, j, :], scale_in.partition_broadcast(S)),
                      (scales[:, j + 1, h0], scale_in[h1].partition_broadcast(S)),
                      (scales[:, j + 1, h1], scale_in[h0].partition_broadcast(S))]
        all_consts = 16 * len(pairs)
        KQ = (1, 0)

        def seq(n):
            return not isinstance(n, int) or 0 <= n < NSEQ

        def seq_steps(eng):
            for g, u in groups(eng):
                for b in range(GB):
                    yield g * GB + b, g, u, b
            for b in range(DRAIN):
                yield NSEQ + b, NG + b // GB, b // GB, b % GB

        @block.sync
        def _(sp):
            load_constants(ph, sp, pairs)
            for g, u in groups(sp):
                if there(g - 2):
                    sp.wait_ge(xt_ready, (g - 1) * GB)
                sp.dma_start(x[u][:, :, :], x_in[g, :, :, :]).then_inc(loaded[u], 16)
                if there(g - 2):
                    sp.wait_ge(summed, (g - 1) * GB)
                sp.dma_start(xr[u][:, :, :], x_in[g, :, :, :]).then_inc(r_loaded[u], 16)

        @block.gpsimd
        def _(pool):
            nc.gpsimd.memset(xs[:, :], 0.0).then_inc(set_up, 1)
            nc.gpsimd.memset(kTm[:, :, :, :], 0.0).then_inc(set_up, 1)
            pool.wait_ge(ph.consts_in, all_consts)
            nc.gpsimd.tensor_copy(identb[:, :], ident[:, :]).then_inc(set_up, 1)
            nc.gpsimd.tensor_copy(maskb[:, :], maskf[:, :]).then_inc(set_up, 1)
            for s, g, u, b in seq_steps(pool):
                if seq(s - 3):
                    n, i = s - 3, (b + 1) % 2
                    for j in range(2):
                        h = slice(4 * j, 4 * j + 4)
                        pool.wait_ge(rec_done, n * 2 + j + 1)
                        nc.gpsimd.tensor_tensor(P[i][:, h, :], P[i][:, h, :], rec[:, h].unsqueeze(2).to_broadcast([S, 4, S]),
                                                ALU.mult).then_inc(p_normed, 1)
                if seq(s - 1):
                    i = (b - 1) % 2
                    for at, j in enumerate(KQ):
                        pool.wait_ge(ab_done, (s - 1) * 6 + 3 * (at + 1))
                        if seq(s - 3):
                            pool.wait_ge(t_ready, (s - 2) * 2)
                        nc.gpsimd.tensor_tensor(rot[j][i][:, :, :], A[j][:, :, :], Bm[j][:, :, :], ALU.add).then_inc(rot_done, 1)
                if b == 2 and there(g - 2):
                    pool.wait_ge(summed, (g - 1) * GB)
                    pool.dma_start(x_out[g - 2, :, :, :], R[u][:, :, :]).then_inc(stored[u], 16)
            for u in range(2):
                pool.wait_ge(stored[u], 16 * (NG // 2))

        @block.tensor
        def _(pe):
            pe.wait_ge(ph.consts_in, all_consts)
            pe.wait_ge(set_up, 4)
            for s, g, u, b in seq_steps(pe):
                for j in range(2):
                    if seq(s - 2):
                        n, i = s - 2, b % 2
                        if seq(n - 3):
                            pe.wait_ge(pt_copied, (n - 3) * 2 + j + 1)
                        if j == 0:
                            pe.wait_ge(rot_done, n * 2 + 2)
                        else:
                            pe.wait_ge(k_normed, n + 1)
                        for c in range(PAIRS):
                            last = nc.tensor.transpose(pT[j][:, c, :],
                                                       rot[j][i][:, 2 * c:2 * c + 2, :].rearrange("p h d -> p (h d)"), ident[:, :])
                        last.then_inc(t_ready, 1)
                    if seq(s - 1) and j == 0:
                        n = s - 1
                        pe.wait_ge(xs_copied, 2 * n + 2)
                        if seq(n - 1):
                            pe.wait_ge(ab_done, (n - 1) * 6 + 3)
                            pe.wait_ge(sq_done, (n - 1) * 2 + 1)
                        nc.tensor.matmul(pK[:, :], xs[:, :], wqkv[:, INNER:2 * INNER], start=True, stop=True).then_inc(k_ready, 1)
                        nc.tensor.matmul(pV[:, :], xs[:, :], wqkv[:, 2 * INNER:3 * INNER], start=True, stop=True).then_inc(v_ready, 1)
                if seq(s - 1):
                    n = s - 1
                    if seq(n - 5):
                        pe.wait_ge(summed, n - 4)
                    elif seq(n - 1):
                        pe.wait_ge(ab_done, n * 6)
                        pe.wait_ge(sq_done, n * 2)
                    nc.tensor.matmul(pQ[:, :], xs[:, :], wqkv[:, 0:INNER], start=True, stop=True).then_inc(q_ready, 1)
                if seq(s - 2):
                    n = s - 2
                    pe.wait_ge(t_copied, (n + 1) * 3)
                    for j in range(2):
                        if seq(n - 1):
                            pe.wait_ge(exp_done, (n - 1) * WH + 4 * j + 4)
                        nc.tensor.matmul(pS[j][:, :, :], identb[:, :], maskb[:, :].unsqueeze(1).to_broadcast([S, 4, S]),
                                         start=True, stop=False, skip_group_check=True)
                        for c in range(2):
                            last = nc.tensor.matmul(pS[j][:, 2 * c:2 * c + 2, :], qT[:, 2 * j + c, :], kTm[:, 2 * j + c, :, :],
                                                    start=False, stop=(c == 1), skip_group_check=True)
                        last.then_inc(s_ready, 1)
                if seq(s - 4):
                    n, i = s - 4, b % 2
                    for h in range(WH):
                        if h % 4 == 0 and not seq(s - 2):
                            pe.wait_ge(pt_copied, n * 2)
                        if h % 4 == 0:
                            pe.wait_ge(p_normed, n * 2 + h // 4 + 1)
                        last = nc.tensor.transpose(pT[h // 4][:, h % 4, :], P[i][:, h, :], ident[:, :])
                        if h % 4 == 3:
                            last.then_inc(pt_ready, 1)
                if seq(s):
                    if b == 0:
                        pe.wait_ge(loaded[u], (g - u) * 8 + 16)
                    if seq(s - 1):
                        pe.wait_ge(v_copied, s)
                    nc.tensor.transpose(pV[:, 0:S], x[u][:, b, :], ident[:, :]).then_inc(xt_ready, 1)
                if seq(s - 4):
                    n = s - 4
                    if seq(n - 1):
                        pe.wait_ge(o_copied, n)
                    for h in range(WH):
                        if h % 4 == 0:
                            pe.wait_ge(pt_copied, n * 2 + h // 4 + 1)
                        r = slice(WD * (h % 2), WD * (h % 2) + WD)
                        last = nc.tensor.matmul(pO[r, h // 2, :], V[b][:, h * WD:(h + 1) * WD], PT[:, h, :],
                                                start=True, stop=True)
                    last.then_inc(pv_ready, 1)
                if seq(s - 5):
                    n = s - 5
                    pe.wait_ge(o_copied, n + 1)
                    if seq(s - 1):
                        pe.wait_ge(ab_done, s * 6)
                        pe.wait_ge(sq_done, s * 2)
                    else:
                        pe.wait_ge(summed, n)
                    for c in range(PAIRS):
                        last = nc.tensor.matmul(pQ[:, 0:D], oT[:, c, :], wo[:, c, :], start=(c == 0), stop=(c == PAIRS - 1))
                    last.then_inc(f_ready, 1)

        @block.scalar
        def _(act):
            nc.scalar.preload_act_table_set(LN_EXP)
            act.wait_ge(ph.consts_in, all_consts)
            act.wait_ge(set_up, 4)
            def square(n, j, of, ready):
                if j == 1 and seq(n - 1):
                    act.wait_ge(ss_done, n * 2)
                act.wait_ge(ready, n + 1)
                nc.scalar.activation(sq[j][:, :, :], of[:, :].rearrange("p (h d) -> p h d", d=WD), ACT.Square).then_inc(sq_done, 1)

            for s, g, u, b in seq_steps(act):
                if seq(s - 3):
                    n, i = s - 3, (b + 1) % 2
                    if seq(n - 2):
                        act.wait_ge(pt_ready, (n - 1) * 2)
                    for h in range(WH):
                        if h % 4 == 0:
                            act.wait_ge(bias_done, n * 2 + h // 4 + 1)
                        nc.scalar.activation(P[i][:, h, :], pS[h // 4][:, h % 4, :], ACT.Exp, bias=bias[:, h:h + 1],
                                             scale=rn[i][:, h:h + 1]).then_inc(exp_done, 1)
                if seq(s - 1):
                    square(s - 1, 1, pK, k_ready)
                if seq(s - 2):
                    n = s - 2
                    if seq(n - 1):
                        act.wait_ge(s_ready, n * 2)
                    act.wait_ge(t_ready, n * 2 + 1)
                    nc.scalar.activation(qT[:, :, :], pT[0][:, :, :], ACT.Copy).then_inc(t_copied, 1)
                    act.wait_ge(t_ready, n * 2 + 2)
                    for j in range(2):
                        r = slice(64 * j, 64 * j + 64)
                        nc.scalar.activation(kTm[r, :, j, :], pT[1][r, :, :], ACT.Copy).then_inc(t_copied, 1)
                if seq(s - 1):
                    square(s - 1, 0, pQ, q_ready)
                if seq(s - 5):
                    n = s - 5
                    act.wait_ge(pv_ready, n + 1)
                    if seq(n - 1):
                        act.wait_ge(f_ready, n)
                    nc.scalar.activation(oT[:, :, :], pO[:, :, :], ACT.Copy).then_inc(o_copied, 1)
                if seq(s - 1):
                    n = s - 1
                    act.wait_ge(v_ready, n + 1)
                    nc.scalar.activation(V[(b - 1) % GB][:, :], pV[:, :], ACT.Copy).then_inc(v_copied, 1)
                if seq(s - 4):
                    n = s - 4
                    for j in range(2):
                        act.wait_ge(pt_ready, n * 2 + j + 1)
                        nc.scalar.activation(PT[:, 4 * j:4 * j + 4, :], pT[j][:, :, :], ACT.Copy).then_inc(pt_copied, 1)
                if seq(s):
                    act.wait_ge(xt_ready, s + 1)
                    if seq(s - 1):
                        act.wait_ge(q_ready, s)
                    nc.scalar.activation(xs[0:64, :], pV[0:64, 0:S], ACT.Copy).then_inc(xs_copied, 1)
                    nc.scalar.activation(xs[64:128, 1:S], pV[64:128, 0:S - 1], ACT.Copy).then_inc(xs_copied, 1)
                if seq(s - 1):
                    n, i = s - 1, (b - 1) % 2
                    act.wait_ge(ss_max, n + 1)
                    nc.scalar.activation(rn[i][:, :], ss[:, :], ACT.Ln, scale=2.0 ** 32).then_inc(ln_done, 1)
                    act.wait_ge(ln_done, n + 1)
                    nc.scalar.activation(rn[i][:, :], rn[i][:, :], ACT.Exp, scale=-0.5, bias=consts[:, 2:3]).then_inc(rn_done, 1)

        @block.vector
        def _(dve):
            dve.wait_ge(ph.consts_in, all_consts)
            nc.vector.tensor_tensor(tables[:, :, :], tables[:, :, :], scales[:, :, :], ALU.mult).then_inc(tabled, 1)
            dve.wait_ge(tabled, 1)
            def rotate(n, at, j, of):
                if seq(n - 1):
                    dve.wait_ge(rot_done, (n - 1) * 2 + at + 1)
                dve.wait_ge(sq_done, n * 2 + at + 1)
                of4 = of[:, :].rearrange("p (h d) -> p h d", d=WD)
                nc.vector.tensor_tensor(A[j][:, :, :], of4, tables[:, 2 * j, :].unsqueeze(1).to_broadcast([S, WH, WD]),
                                        ALU.mult).then_inc(ab_done, 1)
                for to, fr in ((h0, h1), (h1, h0)):
                    nc.vector.tensor_tensor(Bm[j][:, :, to], of4[:, :, fr],
                                            tables[:, 2 * j + 1, to].unsqueeze(1).to_broadcast([S, WH, HALF]),
                                            ALU.mult).then_inc(ab_done, 1)
                if at == 0 and seq(n - 1):
                    dve.wait_ge(ln_done, n)
                nc.vector.reduce_sum(ss[:, WH * j:WH * j + WH], sq[j][:, :, :], AX.X).then_inc(ss_done, 1)

            def inverse_total(n, i, j):
                dve.wait_ge(exp_done, n * WH + 4 * j + 4)
                nc.vector.reduce_sum(total[:, 4 * j:4 * j + 4], P[i][:, 4 * j:4 * j + 4, :], AX.X).then_inc(total_done, 1)
                dve.wait_ge(total_done, n * 2 + j + 1)
                if seq(n - 1):
                    dve.wait_ge(p_normed, (n - 1) * 2 + j + 1)
                nc.vector.reciprocal(rec[:, 4 * j:4 * j + 4], total[:, 4 * j:4 * j + 4]).then_inc(rec_done, 1)

            for s, g, u, b in seq_steps(dve):
                if seq(s - 2):
                    n, i = s - 2, b % 2
                    dve.wait_ge(rot_done, n * 2 + 1)
                    dve.wait_ge(rn_done, n + 1)
                    nc.vector.tensor_tensor(rot[1][i][:, :, :], rot[1][i][:, :, :],
                                            rn[i][:, WH:2 * WH].unsqueeze(2).to_broadcast([S, WH, WD]), ALU.mult).then_inc(k_normed, 1)
                if seq(s - 6):
                    n = s - 6
                    w, at = (u, b + 2) if b < 2 else (1 - u, b - 2)
                    dve.wait_ge(f_ready, n + 1)
                    if at == 0:
                        dve.wait_ge(r_loaded[w], (g - 1 - w) * 8 + 16)
                        if there(g - 3):
                            dve.wait_ge(stored[w], (g - 1 - w) * 8)
                    nc.vector.tensor_tensor(R[w][:, at, :], pQ[:, 0:D], xr[w][:, at, :], ALU.add).then_inc(summed, 1)
                if seq(s - 3):
                    inverse_total(s - 3, (b + 1) % 2, 0)
                    inverse_total(s - 3, (b + 1) % 2, 1)
                if seq(s - 1):
                    rotate(s - 1, 0, 1, pK)
                    rotate(s - 1, 1, 0, pQ)
                    dve.wait_ge(ss_done, s * 2)
                    nc.vector.tensor_scalar(ss[:, :], ss[:, :], 1e-24, None, ALU.max).then_inc(ss_max, 1)
                if seq(s - 2):
                    n, i = s - 2, b % 2
                    for j in range(2):
                        h = slice(4 * j, 4 * j + 4)
                        dve.wait_ge(s_ready, n * 2 + j + 1)
                        nc.vector.tensor_reduce(neg_max[:, h], pS[j][:, :, :], AX.X, ALU.max, negate=True).then_inc(max_done, 1)
                        dve.wait_ge(max_done, n * 2 + j + 1)
                        nc.vector.tensor_tensor(bias[:, h], neg_max[:, h], rn[i][:, h], ALU.mult).then_inc(bias_done, 1)


HID = int(D * 4 * 2 / 3)
HCH = [(at, min(128, HID - at)) for at in range(0, HID, 128)]
NHC = len(HCH)


def phase_geglu(nc, name, x1_in, x_out, w1_in, b1_in, w2_in, b2_in, ln_g_in, ln_b_in, ident_in, shift_in, consts_in, x0_in=None):
    last_layer = x0_in is not None
    with Phase(nc, name) as ph:
        sb, ps, sem = ph.sb, ph.ps, ph.sem
        w1, w2 = sb("w1", [D, 2 * HID]), sb("w2", [128, NHC, D])
        ident, shift, consts = sb("ident", [128, 128]), sb("shift", [S, S]), sb("consts", [128, 2])
        b1, ln_g, ln_b, b2 = sb("b1", [128, 2, NHC]), sb("ln_g", [D, 1]), sb("ln_b", [D, 1]), sb("b2", [S, D])
        x1, x1b, x2 = ([sb(f"{n}{u}", [S, GB, D]) for u in range(2)] for n in ("x1", "x1b", "x2"))
        x0, xo = ([sb(f"{n}{u}", [S, GB, D]) for u in range(2)] for n in ("x0", "xo")) if last_layer else (None, None)
        n1, nT = sb("n1", [S, GB, D]), [sb(f"nT{u}", [D, GT]) for u in range(2)]
        gated, H = [sb(f"gated{c}", [128, GT]) for c in range(NHC)], [sb(f"H{c}", [128, GT]) for c in range(NHC)]
        pX, pT, pO = ps("pX", [S, GB, D]), ps("pT", [D, GT]), ps("pO", [S, GB, D])
        pA, pG = [ps(f"pA{i}", [128, GT]) for i in range(2)], [ps(f"pG{i}", [128, GT]) for i in range(2)]
        ph.consts_in = sem("consts_in")
        stored = ph.stored
        loaded, r_loaded = ([sem(f"{n}{u}") for u in range(2)] for n in ("loaded", "r_loaded"))
        x1b_done, x01_done, shifted, t_ready, t_copied, g_ready, a_ready, gelu_done, h_done, o_ready, x2_done = (
            sem(n) for n in ("x1b_done", "x01_done", "shifted", "t_ready", "t_copied", "g_ready", "a_ready", "gelu_done",
                             "h_done", "o_ready", "x2_done"))
        norm1 = Norm(ph, "norm1", consts[:, 0:1])
        norm2 = Norm(ph, "norm2", consts[:, 0:1]) if last_layer else None
        block = ph.block()
        tail = HCH[-1][1]
        body = (NHC - 1) * 128
        pairs = [(w1[:, :], w1_in), (b1[:, :, :], b1_in), (ident[:, :], ident_in), (shift[:, :], shift_in), (consts[:, :], consts_in),
                 (w2[:, 0:NHC - 1, :], w2_in[0:body, :].rearrange("(c p) d -> p c d", p=128)),
                 (w2[0:tail, NHC - 1, :], w2_in[body:HID, :]),
                 (ln_g[:, :], ln_g_in), (ln_b[:, :], ln_b_in), (b2[:, :], b2_in.partition_broadcast(S))]
        all_consts = 16 * len(pairs)

        @block.sync
        def _(sp):
            load_constants(ph, sp, pairs)
            for g, u in groups(sp):
                if there(g - 2):
                    sp.wait_ge(shifted, g - 1)
                    sp.nop(nofuse=True)
                    sp.wait_ge(x1b_done, (g - 1) * GB)
                sp.dma_start(x1[u][:, :, :], x1_in[g, :, :, :]).then_inc(loaded[u], 16)
                if last_layer:
                    if there(g - 2):
                        sp.wait_ge(x01_done, (g - 1) * GB)
                    sp.dma_start(x0[u][:, :, :], x0_in[g, :, :, :]).then_inc(r_loaded[u], 16)

        @block.gpsimd
        def _(pool):
            pool.wait_ge(ph.consts_in, all_consts)
            for g, u in steps(pool):
                if has(g):
                    pool.wait_ge(loaded[u], (g - u) * 8 + 16)
                    if there(g - 2):
                        pool.wait_ge(x2_done, g - 1)
                    for b in range(GB):
                        nc.gpsimd.tensor_tensor(x1b[u][:, b, :], x1[u][:, b, :], b2[:, :], ALU.add).then_inc(x1b_done, 1)
                    if last_layer:
                        pool.wait_ge(r_loaded[u], (g - u) * 8 + 16)
                        for b in range(GB):
                            pool.wait_ge(x1b_done, g * GB + b + 1)
                            nc.gpsimd.tensor_tensor(x1b[u][:, b, :], x1b[u][:, b, :], x0[u][:, b, :], ALU.add)\
                                .then_inc(x01_done, 1)
                if there(g - 2):
                    if last_layer:
                        pool.wait_ge(norm2.normed, (g - 1) * GB)
                        pool.dma_start(x_out[g - 2, :, :, :], xo[u][:, :, :]).then_inc(stored[u], 16)
                    else:
                        pool.wait_ge(x2_done, g - 1)
                        pool.dma_start(x_out[g - 2, :, :, :], x2[u][:, :, :]).then_inc(stored[u], 16)
            for u in range(2):
                pool.wait_ge(stored[u], 16 * (NG // 2))

        @block.tensor
        def _(pe):
            pe.wait_ge(ph.consts_in, all_consts)
            for g, u in steps(pe):
                if has(g):
                    pe.wait_ge(loaded[u], (g - u) * 8 + 16)
                    if there(g - 1):
                        pe.wait_ge(norm1.normed, g * GB)
                    nc.tensor.matmul(pX[:, :, 0:64], ident[:, :], x1[u][:, :, 0:64], start=True, stop=True)
                    nc.tensor.matmul(pX[:, :, 64:128], shift[:, :], x1[u][:, :, 64:128], start=True, stop=True).then_inc(shifted, 1)
                if there(g - 1) and has(g - 1):
                    pe.wait_ge(t_copied, g)
                    for c, (at, n) in enumerate(HCH):
                        k, i = (g - 1) * NHC + c, ((1 - u) * NHC + c) % 2
                        if there(k - 2):
                            pe.wait_ge(gelu_done, k - 1)
                        nc.tensor.matmul(pG[i][0:n, :], w1[:, HID + at:HID + at + n], nT[1 - u][:, :],
                                         start=True, stop=True).then_inc(g_ready, 1)
                        if there(k - 2):
                            pe.wait_ge(h_done, k - 1)
                        nc.tensor.matmul(pA[i][0:n, :], w1[:, at:at + n], nT[1 - u][:, :],
                                         start=True, stop=True).then_inc(a_ready, 1)
                if there(g - 1) and has(g - 1):
                    pe.wait_ge(h_done, g * NHC)
                    if there(g - 2):
                        pe.wait_ge(x2_done, g - 1)
                    for b in range(GB):
                        for c, (at, n) in enumerate(HCH):
                            last = nc.tensor.matmul(pO[:, b, :], H[c][0:n, b * S:(b + 1) * S], w2[0:n, c, :],
                                                    start=(c == 0), stop=(c == NHC - 1))
                    last.then_inc(o_ready, 1)
                if has(g):
                    if there(g - 1):
                        pe.wait_ge(t_copied, g)
                    for b in range(GB):
                        pe.wait_ge(norm1.normed, g * GB + b + 1)
                        last = nc.tensor.transpose(pT[:, b * S:(b + 1) * S], n1[:, b, :], ident[:, :])
                    last.then_inc(t_ready, 1)

        @block.scalar
        def _(act):
            act.wait_ge(ph.consts_in, all_consts)
            for g, u in steps(act):
                if there(g - 1) and has(g - 1):
                    for c, (at, n) in enumerate(HCH):
                        k, i = (g - 1) * NHC + c, ((1 - u) * NHC + c) % 2
                        act.wait_ge(g_ready, k + 1)
                        if there(g - 2):
                            act.wait_ge(h_done, (g - 2) * NHC + c + 1)
                        nc.scalar.activation(gated[c][0:n, :], pG[i][0:n, :], ACT.Gelu, bias=b1[0:n, 1, c:c + 1]).then_inc(gelu_done, 1)
                nc.scalar.preload_act_table_set(LN_EXP)
                if has(g):
                    norm1.act_rstd(nc, act, g)
                if there(g - 2) and last_layer:
                    norm2.act_rstd(nc, act, g - 2)
                if has(g):
                    act.wait_ge(t_ready, g + 1)
                    if there(g - 2):
                        act.wait_ge(a_ready, (g - 1) * NHC)
                    nc.scalar.activation(nT[u][:, :], pT[:, :], ACT.Identity, scale=ln_g[:, 0:1],
                                         bias=ln_b[:, 0:1]).then_inc(t_copied, 1)

        @block.vector
        def _(dve):
            dve.wait_ge(ph.consts_in, all_consts)
            for g, u in steps(dve):
                if has(g):
                    dve.wait_ge(shifted, g + 1)
                    norm1.dve_stats(nc, dve, g, pX)
                if there(g - 2) and last_layer:
                    norm2.dve_stats(nc, dve, g - 2, x2[u])
                if there(g - 1) and has(g - 1):
                    for c, (at, n) in enumerate(HCH):
                        k, i = (g - 1) * NHC + c, ((1 - u) * NHC + c) % 2
                        dve.wait_ge(a_ready, k + 1)
                        dve.wait_ge(gelu_done, k + 1)
                        if c == 0 and there(g - 2):
                            dve.wait_ge(o_ready, g - 1)
                        nc.vector.scalar_tensor_tensor(out=H[c][0:n, :], in0=pA[i][0:n, :], scalar=b1[0:n, 0, c:c + 1],
                                                       in1=gated[c][0:n, :], op0=ALU.add, op1=ALU.mult).then_inc(h_done, 1)
                if has(g):
                    if there(g - 1):
                        dve.wait_ge(t_ready, g)
                    norm1.dve_scale(nc, dve, g, n1, pX)
                if there(g - 2) and last_layer:
                    if there(g - 4):
                        dve.wait_ge(stored[u], (g - 2 - u) * 8)
                    norm2.dve_scale(nc, dve, g - 2, xo[u], x2[u])
                if there(g - 1) and has(g - 1):
                    w = 1 - u
                    dve.wait_ge(o_ready, g)
                    dve.wait_ge(x01_done if last_layer else x1b_done, g * GB)
                    if there(g - 3):
                        if last_layer:
                            dve.wait_ge(norm2.normed, (g - 2) * GB)
                        else:
                            dve.wait_ge(stored[w], (g - 1 - w) * 8)
                    nc.vector.tensor_tensor(x2[w][:, :, :], pO[:, :, :], x1b[w][:, :, :], ALU.add).then_inc(x2_done, 1)
                    if last_layer:
                        dve.wait_ge(x2_done, g)


LAYERS = 2



def build(nc, t, out):
    scratch = [nc.dram_tensor(f"tokens_{i}", (NG, S, GB, D), F32, kind="Internal").ap() for i in range(3)]
    a, b, c = scratch
    ident, mask, consts = t["ident"], t["head_mask"], t["consts"]
    phase_recurrence(nc, t["x"], a, t["L0_attn_W_gates"], t["L0_attn_W_out"], ident, consts[:, 0:2])
    phase_cross(nc, "cross0", a, b, t["ctx"], t["L0_xattn_Wq"], t["L0_xattn_Wk"], t["L0_xattn_Wv"], t["L0_xattn_Wout"],
                ident, mask, consts, bout_in=t["L0_xattn_bout"])
    phase_experts(nc, b, a, t["gate_W"], t["w1_experts"], t["w3_experts"], t["w2_experts"], ident, t["iota"], consts[:, 0:2])
    phase_attention(nc, a, b, t["L1_attn_Wq"], t["L1_attn_Wk"], t["L1_attn_Wv"], t["L1_attn_Wout"], ident, consts[:, 0:2])
    phase_cross(nc, "cross1", b, c, t["ctx"], t["L1_xattn_Wq"], t["L1_xattn_Wk"], t["L1_xattn_Wv"], t["L1_xattn_Wo"],
                ident, mask, consts, bias_in=t["bias"])
    phase_feedforward(nc, b, c, a, t["L1_xattn_W1"], t["L1_xattn_b1"], t["L1_xattn_W2"], t["L1_xattn_b2"],
                      t["L1_xattn_g1"], t["L1_xattn_be1"], t["L1_xattn_g2"], t["L1_xattn_be2"], ident, consts[:, 0:2])
    source = a
    for l in range(LAYERS):
        last = l == LAYERS - 1
        phase_window(nc, f"window{l}", source, c, t["L1_ffn_wqkv"][l], t["L1_ffn_wo"][l], t["rotary"], t["L1_ffn_q_scale"][l],
                     t["L1_ffn_k_scale"][l], ident, t["window_mask"], consts)
        phase_geglu(nc, f"geglu{l}", c, out if last else b, t["L1_ffn_w1"][l], t["L1_ffn_b1"][l], t["L1_ffn_w2"][l],
                    t["L1_ffn_b2"][l], t["L1_ffn_ln_g"][l], t["L1_ffn_ln_b"][l], ident, t["shift"], consts[:, 0:2],
                    x0_in=a if last else None)
        source = b


def to_groups(x):
    return x.reshape(NG, GB, S, D).transpose(0, 2, 1, 3)


def rotary_tables():
    half = np.arange(0, 64, 2, dtype=np.float32)
    inv = (1.0 / 10000.0 ** (half / 64)).astype(np.float32)
    pos = np.arange(S, dtype=np.float32)
    freqs = pos[:, None] * inv[None]
    freqs = np.concatenate([freqs, freqs], -1)
    base = ((half + 0.4 * 64) / (1.4 * 64)).astype(np.float32)
    power = (pos - S // 2) / np.float32(32)
    scale = (base[None] ** power[:, None]).astype(np.float32)
    scale = np.concatenate([scale, scale], -1)
    cos, sin = np.cos(freqs), np.sin(freqs)
    sign = np.where(np.arange(64) < 32, -1, 1).astype(np.float32)
    return np.stack([8 * cos * scale, 8 * sign * sin * scale, cos / scale, sign * sin / scale], 1).astype(np.float32)


def lay_out(i):
    per_head = np.arange(D)[:, None] // (D // HEADS16) == np.arange(HEADS16)[None]
    q, k = np.arange(S)[:, None], np.arange(S)[None]
    wkv, wqkv = i["L0_xattn_Wkv"], i["L1_attn_W_qkv"]

    def rows_in_chunks(w):
        return w.reshape(-1, 128, w.shape[-1]).transpose(1, 0, 2)

    def up(routed, shared):
        shared = shared.transpose(1, 0, 2).reshape(1, D, -1)
        return np.concatenate([routed, shared]).transpose(1, 0, 2)

    t = {
        "x": to_groups(i["x"]),
        "ctx": i["ctx_1024"].reshape(NG, GB * S2, D).transpose(0, 2, 1),
        "bias": i["fside_Bx16xSxS2_0"].transpose(0, 2, 1, 3).reshape(NG, GB, S, HEADS16, S2),
        "ident": np.eye(128, dtype=np.float32),
        "head_mask": per_head.astype(np.float32),
        "consts": np.tile(np.array([[EPS, 2.0, 16 * math.log(2.0), 10 * math.log(2.0)]], np.float32), (128, 1)),
        "iota": np.tile(np.arange(8, dtype=np.float32), (128, 1)),
        "shift": np.eye(S, k=1, dtype=np.float32),
        "window_mask": np.where((k <= q) & (q <= k + 64), 0, -1e30).astype(np.float32),
        "rotary": rotary_tables(),
        "L0_attn_W_gates": i["L0_attn_W_fwd"].T,
        "L0_attn_W_out": rows_in_chunks(i["L0_attn_W_out"].T),
        "L0_xattn_Wq": i["L0_xattn_Wq"].T, "L0_xattn_Wk": wkv[:D].T, "L0_xattn_Wv": wkv[D:].T,
        "L0_xattn_Wout": i["L0_xattn_Wout"].T, "L0_xattn_bout": i["L0_xattn_bout"],
        "gate_W": i["L0_ffn_gate_W"].T,
        "w1_experts": up(i["L0_ffn_w1_e"], i["L0_ffn_w1_s"]),
        "w3_experts": up(i["L0_ffn_w3_e"], i["L0_ffn_w3_s"]),
        "w2_experts": np.concatenate([i["L0_ffn_w2_e"], i["L0_ffn_w2_s"].reshape(1, -1, D)])
                        .reshape(9, -1, 128, D).transpose(2, 0, 1, 3),
        "L1_attn_Wq": wqkv[0::3].T, "L1_attn_Wk": wqkv[1::3].T, "L1_attn_Wv": wqkv[2::3].T,
        "L1_attn_Wout": i["L1_attn_W_out"].T,
        "L1_xattn_Wq": i["L1_xattn_Wq"].T, "L1_xattn_Wk": i["L1_xattn_Wk"].T,
        "L1_xattn_Wv": i["L1_xattn_Wv"].T, "L1_xattn_Wo": i["L1_xattn_Wo"].T,
        "L1_xattn_W1": i["L1_xattn_W1"].T, "L1_xattn_b1": i["L1_xattn_b1"].reshape(-1, 128).T,
        "L1_xattn_W2": rows_in_chunks(i["L1_xattn_W2"].T), "L1_xattn_b2": i["L1_xattn_b2"],
        "L1_xattn_g1": i["L1_xattn_g1"].reshape(D, 1), "L1_xattn_be1": i["L1_xattn_be1"].reshape(D, 1),
        "L1_xattn_g2": i["L1_xattn_g2"], "L1_xattn_be2": i["L1_xattn_be2"],
        "L1_ffn_wqkv": i["L1_ffn_wqkv"],
        "L1_ffn_wo": i["L1_ffn_wo"].reshape(LAYERS, -1, 128, D).transpose(0, 2, 1, 3),
        "L1_ffn_q_scale": i["L1_ffn_q_scale"], "L1_ffn_k_scale": i["L1_ffn_k_scale"],
        "L1_ffn_ln_g": i["L1_ffn_ln_g"].reshape(LAYERS, D, 1), "L1_ffn_ln_b": i["L1_ffn_ln_b"].reshape(LAYERS, D, 1),
        "L1_ffn_w1": i["L1_ffn_w1"], "L1_ffn_w2": i["L1_ffn_w2"], "L1_ffn_b2": i["L1_ffn_b2"],
        "L1_ffn_b1": np.pad(i["L1_ffn_b1"].reshape(LAYERS, 2, HID), ((0, 0), (0, 0), (0, NHC * 128 - HID)))
                       .reshape(LAYERS, 2, NHC, 128).transpose(0, 3, 1, 2),
    }
    return t


def kernel(**inputs):
    import concourse.bacc as bacc
    from concourse.bass_utils import run_bass_kernel_spmd

    nc = bacc.Bacc("TRN2", target_bir_lowering=False, num_devices=1)
    arrays, aps = {}, {}
    for name, a in lay_out({k: np.asarray(v) for k, v in inputs.items()}).items():
        arrays[f"in_{name}"] = np.ascontiguousarray(a)
        aps[name] = nc.dram_tensor(f"in_{name}", a.shape, mybir.dt.from_np(a.dtype), kind="ExternalInput").ap()
    out = nc.dram_tensor("out_x", (NG, S, GB, D), F32, kind="ExternalOutput").ap()
    build(nc, aps, out)
    r = run_bass_kernel_spmd(nc, [arrays], core_ids=[0])
    return r.results[0]["out_x"].reshape(NG, S, GB, D).transpose(0, 2, 1, 3).reshape(B, S, D)
```
